# Optimizing a Trainium2 kernel written in Bass

```python
import numpy as np
import jax
import jax.numpy as jnp

def _softmax(x, axis=-1):
    return jax.nn.softmax(x, axis=axis)

def _gelu(x):
    return jax.nn.gelu(x, approximate=True)

def _silu(x):
    return jax.nn.silu(x)

def _sigmoid(x):
    return jax.nn.sigmoid(x)

def _layernorm(x, axis=-1, eps=1e-05):
    m = jnp.mean(x, axis=axis, keepdims=True)
    v = jnp.var(x, axis=axis, keepdims=True)
    return (x - m) / jnp.sqrt(v + eps)

def _scatter_add(tgt, idx, src, axis=0):
    return tgt.at[idx].add(src)

def _segment_sum(src, seg, n):
    return jax.ops.segment_sum(src, seg, n)
kernel_name = 'mk_seq_postln_d2_jaxref_r8_7c21d0'

def setup_inputs(seed: int=0):
    np.random.seed(seed)
    _w = jnp.asarray

    def _L0_attn_setup():
        import jax, jax.numpy as jnp
        import numpy as np
        B, T, D = (2, 256, 128)
        H = 16
        HD = D // H
        WINDOW = 128
        N_GLOBAL = 1
        SCALE = 1.0 / np.sqrt(HD)

        def _attend_mask(T):
            idx = jnp.arange(T)
            dist = jnp.abs(idx[:, None] - idx[None, :])
            attend = dist <= WINDOW
            glb = idx < N_GLOBAL
            attend = attend | glb[:, None] | glb[None, :]
            return attend
        key = jax.random.key(seed)
        ks = jax.random.split(key, 5)
        scale_w = 1.0 / np.sqrt(D)
        return {'x': jax.random.normal(ks[0], (B, T, D), dtype=jnp.float32), 'Wq': jax.random.normal(ks[1], (D, D), dtype=jnp.float32) * scale_w, 'Wk': jax.random.normal(ks[2], (D, D), dtype=jnp.float32) * scale_w, 'Wv': jax.random.normal(ks[3], (D, D), dtype=jnp.float32) * scale_w, 'Wo': jax.random.normal(ks[4], (D, D), dtype=jnp.float32) * scale_w}
    _L0_attn_in = _L0_attn_setup()

    def _L0_ffn_setup():
        import jax, jax.numpy as jnp
        import numpy as np
        B, S, H, E, K = (2, 256, 128, 8, 2)
        FF = 4 * H
        EPS = 1e-05
        key = jax.random.key(seed)
        ks = jax.random.split(key, 5)
        rn = lambda k, shape, scale: jax.random.normal(k, shape, dtype=jnp.float32) * scale
        return {'x': rn(ks[0], (B, S, H), 1.0), 'router_W': rn(ks[1], (H, E), H ** (-0.5)), 'router_b': jnp.zeros((E,), jnp.float32), 'ln_g': jnp.ones((E, H), jnp.float32), 'ln_b': jnp.zeros((E, H), jnp.float32), 'W1': rn(ks[2], (E, H, FF), H ** (-0.5)), 'b1': jnp.zeros((E, FF), jnp.float32), 'W2': rn(ks[3], (E, FF, H), FF ** (-0.5)), 'b2': jnp.zeros((E, H), jnp.float32)}
    _L0_ffn_in = _L0_ffn_setup()

    def _L1_attn_setup():
        import jax, jax.numpy as jnp
        import numpy as np
        B, S, HID, NH = (4, 512, 128, 16)
        D = HID // NH
        EPS = 1e-05

        def _delta_scan(q, k, v, beta):
            vsum = v.sum(-1)
            qs = jnp.moveaxis(q, 1, 0)
            ks_ = jnp.moveaxis(k, 1, 0)
            vs = jnp.moveaxis(vsum, 1, 0)
            bs = jnp.moveaxis(beta, 1, 0)

            def step(h, inp):
                q_t, k_t, vsum_t, beta_t = inp
                h = h * beta_t[..., None, None]
                h = h + (k_t * vsum_t[..., None])[:, :, None, :]
                o_t = jnp.einsum('bhj,bhjk->bhk', q_t, h)
                return (h, o_t)
            h0 = jnp.zeros((q.shape[0], q.shape[2], D, D), dtype=q.dtype)
            _, o = jax.lax.scan(step, h0, (qs, ks_, vs, bs))
            return jnp.moveaxis(o, 0, 1)
        key = jax.random.key(seed)
        ks = jax.random.split(key, 8)
        x = jax.random.normal(ks[0], (B, S, HID), dtype=jnp.float32)
        sc = 0.03
        Wq = jax.random.normal(ks[1], (HID, HID), dtype=jnp.float32) * sc
        Wk = jax.random.normal(ks[2], (HID, HID), dtype=jnp.float32) * sc
        Wv = jax.random.normal(ks[3], (HID, HID), dtype=jnp.float32) * sc
        Wbeta = jax.random.normal(ks[4], (HID, NH), dtype=jnp.float32) * sc
        b_beta = jnp.full((NH,), 0.9, dtype=jnp.float32)
        Wo = jax.random.normal(ks[5], (HID, HID), dtype=jnp.float32) * sc
        b_o = jnp.zeros((HID,), dtype=jnp.float32)
        ln_g = jnp.ones((HID,), dtype=jnp.float32)
        ln_b = jnp.zeros((HID,), dtype=jnp.float32)
        return {'x': x, 'Wq': Wq, 'Wk': Wk, 'Wv': Wv, 'Wbeta': Wbeta, 'b_beta': b_beta, 'Wo': Wo, 'b_o': b_o, 'ln_g': ln_g, 'ln_b': ln_b}
    _L1_attn_in = _L1_attn_setup()

    def _L1_ffn_setup():
        import jax, jax.numpy as jnp
        import numpy as np
        D_MODEL = 128
        N_HEADS = 16
        D_HEAD = D_MODEL // N_HEADS
        N_EXPERTS = 8
        TOP_K = 2
        D_FF = 256
        EPS = 1e-06

        def rmsnorm(x, w):
            return x * jax.lax.rsqrt(jnp.mean(x * x, axis=-1, keepdims=True) + EPS) * w

        def swiglu(x, w_gate, w_up, w_down):
            return jax.nn.silu(x @ w_gate) * (x @ w_up) @ w_down
        key = jax.random.key(seed)
        ks = jax.random.split(key, 16)
        s = 0.02
        B, S = (2, 256)
        return {'X': jax.random.normal(ks[0], (B, S, D_MODEL), dtype=jnp.float32), 'norm1_w': jnp.ones((D_MODEL,), jnp.float32), 'norm2_w': jnp.ones((D_MODEL,), jnp.float32), 'wq': jax.random.normal(ks[1], (D_MODEL, D_MODEL), jnp.float32) * s, 'wk': jax.random.normal(ks[2], (D_MODEL, D_MODEL), jnp.float32) * s, 'wv': jax.random.normal(ks[3], (D_MODEL, D_MODEL), jnp.float32) * s, 'wo': jax.random.normal(ks[4], (D_MODEL, D_MODEL), jnp.float32) * s, 'router_w': jax.random.normal(ks[5], (D_MODEL, N_EXPERTS), jnp.float32) * s, 'sh_gate': jax.random.normal(ks[6], (D_MODEL, D_FF), jnp.float32) * s, 'sh_up': jax.random.normal(ks[7], (D_MODEL, D_FF), jnp.float32) * s, 'sh_down': jax.random.normal(ks[8], (D_FF, D_MODEL), jnp.float32) * s, 'e_gate': jax.random.normal(ks[9], (N_EXPERTS, D_MODEL, D_FF), jnp.float32) * s, 'e_up': jax.random.normal(ks[10], (N_EXPERTS, D_MODEL, D_FF), jnp.float32) * s, 'e_down': jax.random.normal(ks[11], (N_EXPERTS, D_FF, D_MODEL), jnp.float32) * s}
    _L1_ffn_in = _L1_ffn_setup()
    _d = {'L0_attn_x': _L0_attn_in['x'], 'L0_attn_Wq': _L0_attn_in['Wq'], 'L0_attn_Wk': _L0_attn_in['Wk'], 'L0_attn_Wv': _L0_attn_in['Wv'], 'L0_attn_Wo': _L0_attn_in['Wo'], 'L0_ffn_router_W': _L0_ffn_in['router_W'], 'L0_ffn_router_b': _L0_ffn_in['router_b'], 'L0_ffn_ln_g': _L0_ffn_in['ln_g'], 'L0_ffn_ln_b': _L0_ffn_in['ln_b'], 'L0_ffn_W1': _L0_ffn_in['W1'], 'L0_ffn_b1': _L0_ffn_in['b1'], 'L0_ffn_W2': _L0_ffn_in['W2'], 'L0_ffn_b2': _L0_ffn_in['b2'], 'L1_attn_Wq': _L1_attn_in['Wq'], 'L1_attn_Wk': _L1_attn_in['Wk'], 'L1_attn_Wv': _L1_attn_in['Wv'], 'L1_attn_Wbeta': _L1_attn_in['Wbeta'], 'L1_attn_b_beta': _L1_attn_in['b_beta'], 'L1_attn_Wo': _L1_attn_in['Wo'], 'L1_attn_b_o': _L1_attn_in['b_o'], 'L1_attn_ln_g': _L1_attn_in['ln_g'], 'L1_attn_ln_b': _L1_attn_in['ln_b'], 'L1_ffn_norm1_w': _L1_ffn_in['norm1_w'], 'L1_ffn_norm2_w': _L1_ffn_in['norm2_w'], 'L1_ffn_wq': _L1_ffn_in['wq'], 'L1_ffn_wk': _L1_ffn_in['wk'], 'L1_ffn_wv': _L1_ffn_in['wv'], 'L1_ffn_wo': _L1_ffn_in['wo'], 'L1_ffn_router_w': _L1_ffn_in['router_w'], 'L1_ffn_sh_gate': _L1_ffn_in['sh_gate'], 'L1_ffn_sh_up': _L1_ffn_in['sh_up'], 'L1_ffn_sh_down': _L1_ffn_in['sh_down'], 'L1_ffn_e_gate': _L1_ffn_in['e_gate'], 'L1_ffn_e_up': _L1_ffn_in['e_up'], 'L1_ffn_e_down': _L1_ffn_in['e_down']}
    _x0 = _d['L0_attn_x']
    _d['L0_attn_x'] = jax.random.normal(jax.random.fold_in(jax.random.key(seed), 1), (4, 1024, 128), dtype=_x0.dtype)
    del _x0
    return _d

def reference(L0_attn_x, L0_attn_Wq, L0_attn_Wk, L0_attn_Wv, L0_attn_Wo, L0_ffn_router_W, L0_ffn_router_b, L0_ffn_ln_g, L0_ffn_ln_b, L0_ffn_W1, L0_ffn_b1, L0_ffn_W2, L0_ffn_b2, L1_attn_Wq, L1_attn_Wk, L1_attn_Wv, L1_attn_Wbeta, L1_attn_b_beta, L1_attn_Wo, L1_attn_b_o, L1_attn_ln_g, L1_attn_ln_b, L1_ffn_norm1_w, L1_ffn_norm2_w, L1_ffn_wq, L1_ffn_wk, L1_ffn_wv, L1_ffn_wo, L1_ffn_router_w, L1_ffn_sh_gate, L1_ffn_sh_up, L1_ffn_sh_down, L1_ffn_e_gate, L1_ffn_e_up, L1_ffn_e_down):

    def _L0_attn_ref(x, Wq, Wk, Wv, Wo):
        import jax, jax.numpy as jnp
        import numpy as np
        B, T, D = (2, 256, 128)
        H = 16
        HD = D // H
        WINDOW = 128
        N_GLOBAL = 1
        SCALE = 1.0 / np.sqrt(HD)

        def _attend_mask(T):
            idx = jnp.arange(T)
            dist = jnp.abs(idx[:, None] - idx[None, :])
            attend = dist <= WINDOW
            glb = idx < N_GLOBAL
            attend = attend | glb[:, None] | glb[None, :]
            return attend
        Bb, Tt, Dd = x.shape
        q = (x @ Wq.T).reshape(Bb, Tt, H, HD).transpose(0, 2, 1, 3)
        k = (x @ Wk.T).reshape(Bb, Tt, H, HD).transpose(0, 2, 1, 3)
        v = (x @ Wv.T).reshape(Bb, Tt, H, HD).transpose(0, 2, 1, 3)
        attend = _attend_mask(Tt)
        logits = jnp.einsum('bhqd,bhkd->bhqk', q, k) * SCALE
        logits = jnp.where(attend[None, None, :, :], logits, -jnp.inf)
        weights = jax.nn.softmax(logits, axis=-1)
        weights = jnp.nan_to_num(weights)
        out = jnp.einsum('bhqk,bhkd->bhqd', weights, v)
        out = out.transpose(0, 2, 1, 3).reshape(Bb, Tt, Dd)
        return out @ Wo.T

    def _L0_ffn_ref(x, router_W, router_b, ln_g, ln_b, W1, b1, W2, b2):
        import jax, jax.numpy as jnp
        import numpy as np
        B, S, H, E, K = (2, 256, 128, 8, 2)
        FF = 4 * H
        EPS = 1e-05
        logits = x @ router_W + router_b
        w, idx = jax.lax.top_k(logits, K)
        w = jax.nn.softmax(w, axis=-1)
        gates = jnp.einsum('bske,bsk->bse', jax.nn.one_hot(idx, E, dtype=x.dtype), w)
        mu = jnp.mean(x, axis=-1, keepdims=True)
        var = jnp.mean(jnp.square(x - mu), axis=-1, keepdims=True)
        xhat = (x - mu) * jax.lax.rsqrt(var + EPS)
        h = xhat[:, :, None, :] * ln_g + ln_b
        a = jax.nn.gelu(jnp.einsum('bseh,ehf->bsef', h, W1) + b1, approximate=False)
        y = jnp.einsum('bsef,efh->bseh', a, W2) + b2
        y = y + x[:, :, None, :]
        out = jnp.einsum('bseh,bse->bsh', y, gates)
        return out

    def _L1_attn_ref(x, Wq, Wk, Wv, Wbeta, b_beta, Wo, b_o, ln_g, ln_b):
        import jax, jax.numpy as jnp
        import numpy as np
        B, S, HID, NH = (4, 512, 128, 16)
        D = HID // NH
        EPS = 1e-05

        def _delta_scan(q, k, v, beta):
            vsum = v.sum(-1)
            qs = jnp.moveaxis(q, 1, 0)
            ks_ = jnp.moveaxis(k, 1, 0)
            vs = jnp.moveaxis(vsum, 1, 0)
            bs = jnp.moveaxis(beta, 1, 0)

            def step(h, inp):
                q_t, k_t, vsum_t, beta_t = inp
                h = h * beta_t[..., None, None]
                h = h + (k_t * vsum_t[..., None])[:, :, None, :]
                o_t = jnp.einsum('bhj,bhjk->bhk', q_t, h)
                return (h, o_t)
            h0 = jnp.zeros((q.shape[0], q.shape[2], D, D), dtype=q.dtype)
            _, o = jax.lax.scan(step, h0, (qs, ks_, vs, bs))
            return jnp.moveaxis(o, 0, 1)
        b, s, hid = x.shape
        residual = x
        q = (x @ Wq).reshape(b, s, NH, D)
        k = (x @ Wk).reshape(b, s, NH, D)
        v = (x @ Wv).reshape(b, s, NH, D)
        beta = jax.nn.sigmoid(x @ Wbeta + b_beta)
        o = _delta_scan(q, k, v, beta).reshape(b, s, hid)
        out = o @ Wo + b_o
        y = residual + out
        mu = y.mean(-1, keepdims=True)
        var = ((y - mu) ** 2).mean(-1, keepdims=True)
        return ln_g * (y - mu) * jax.lax.rsqrt(var + EPS) + ln_b

    def _L1_ffn_ref(X, norm1_w, norm2_w, wq, wk, wv, wo, router_w, sh_gate, sh_up, sh_down, e_gate, e_up, e_down):
        import jax, jax.numpy as jnp
        import numpy as np
        D_MODEL = 128
        N_HEADS = 16
        D_HEAD = D_MODEL // N_HEADS
        N_EXPERTS = 8
        TOP_K = 2
        D_FF = 256
        EPS = 1e-06

        def rmsnorm(x, w):
            return x * jax.lax.rsqrt(jnp.mean(x * x, axis=-1, keepdims=True) + EPS) * w

        def swiglu(x, w_gate, w_up, w_down):
            return jax.nn.silu(x @ w_gate) * (x @ w_up) @ w_down
        B, S, d = X.shape
        scale = 1.0 / jnp.sqrt(jnp.asarray(D_HEAD, X.dtype))
        h = rmsnorm(X, norm1_w)
        q = (h @ wq).reshape(B, S, N_HEADS, D_HEAD)
        k = (h @ wk).reshape(B, S, N_HEADS, D_HEAD)
        v = (h @ wv).reshape(B, S, N_HEADS, D_HEAD)
        scores = jnp.einsum('bshd,bthd->bhst', q, k) * scale
        attn = jax.nn.softmax(scores, axis=-1)
        ctx = jnp.einsum('bhst,bthd->bshd', attn, v).reshape(B, S, d)
        X = X + ctx @ wo
        h2 = rmsnorm(X, norm2_w).reshape(B * S, d)
        logits = h2 @ router_w
        probs = jax.nn.softmax(logits, axis=-1)
        topw, topi = jax.lax.top_k(probs, TOP_K)
        topw = jax.nn.softmax(topw, axis=-1)
        combine = jnp.sum(jax.nn.one_hot(topi, N_EXPERTS, dtype=h2.dtype) * topw[..., None], axis=1)
        shared = swiglu(h2, sh_gate, sh_up, sh_down)
        gate = jnp.einsum('td,edf->etf', h2, e_gate)
        up = jnp.einsum('td,edf->etf', h2, e_up)
        eout = jnp.einsum('etf,efd->etd', jax.nn.silu(gate) * up, e_down)
        spec = jnp.einsum('etd,te->td', eout, combine)
        moe_out = (shared + spec).reshape(B, S, d)
        return X + moe_out
    x = L0_attn_x
    x = _layernorm(x + _L0_attn_ref(x, L0_attn_Wq, L0_attn_Wk, L0_attn_Wv, L0_attn_Wo), axis=-1)
    x = _layernorm(x + _L0_ffn_ref(x, L0_ffn_router_W, L0_ffn_router_b, L0_ffn_ln_g, L0_ffn_ln_b, L0_ffn_W1, L0_ffn_b1, L0_ffn_W2, L0_ffn_b2), axis=-1)
    x = _layernorm(x + _L1_attn_ref(x, L1_attn_Wq, L1_attn_Wk, L1_attn_Wv, L1_attn_Wbeta, L1_attn_b_beta, L1_attn_Wo, L1_attn_b_o, L1_attn_ln_g, L1_attn_ln_b), axis=-1)
    x = _layernorm(x + _L1_ffn_ref(x, L1_ffn_norm1_w, L1_ffn_norm2_w, L1_ffn_wq, L1_ffn_wk, L1_ffn_wv, L1_ffn_wo, L1_ffn_router_w, L1_ffn_sh_gate, L1_ffn_sh_up, L1_ffn_sh_down, L1_ffn_e_gate, L1_ffn_e_up, L1_ffn_e_down), axis=-1)
    return x

_drawn_inputs = setup_inputs


def setup_inputs(seed=0):
    import zlib

    import numpy as np

    out = dict(_drawn_inputs(seed))
    spreads = {'L0_ffn_router_b': (0.0, 0.1),
     'L0_ffn_ln_g': (1.0, 0.2),
     'L0_ffn_ln_b': (0.0, 0.328),
     'L0_ffn_b1': (0.0, 0.33),
     'L0_ffn_b2': (0.0, 0.1),
     'L1_attn_b_beta': (0.8999999761581421, 0.6),
     'L1_attn_b_o': (0.0, 0.1),
     'L1_attn_ln_g': (1.0, 0.2),
     'L1_attn_ln_b': (0.0, 0.1),
     'L1_ffn_norm1_w': (1.0, 0.6),
     'L1_ffn_norm2_w': (1.0, 0.6)}
    factors = {'L1_attn_Wbeta': 7.651,
     'L1_ffn_wq': 8.0,
     'L1_ffn_wk': 8.0,
     'L1_ffn_wv': 8.0,
     'L1_ffn_wo': 8.0,
     'L1_ffn_router_w': 8.0,
     'L1_ffn_sh_gate': 8.0,
     'L1_ffn_sh_up': 8.0,
     'L1_ffn_sh_down': 8.0,
     'L1_ffn_e_gate': 8.0,
     'L1_ffn_e_up': 8.0,
     'L1_ffn_e_down': 8.0}
    for name, (base, spread) in spreads.items():
        noise = np.random.default_rng([zlib.crc32(name.encode()), seed]).standard_normal(out[name].shape)
        drawn = base * np.exp(spread * noise) if base else spread * noise
        out[name] = jnp.asarray(drawn.astype(out[name].dtype))
    for name, factor in factors.items():
        out[name] = (out[name] * factor).astype(out[name].dtype)
    return out
```

```python
from contextlib import ExitStack

import concourse.bass as bass
from concourse import mybir

F32 = mybir.dt.float32
BF16 = mybir.dt.bfloat16
ALU = mybir.AluOpType
ACT = mybir.ActivationFunctionType
AX = mybir.AxisListType

P = 128
B, T = 4, 1024
NT = T // P
H, HD = 16, 8
G = 4
UPB = H // G
NU = B * UPB
HALF = 512
CH = B * T // HALF
CT = HALF // P
E = 8
BANKS = 4
PARTS = 3
KROWS = PARTS * PARTS * HD
KMAX = 96
SCALE = float(HD) ** -0.5
MASKED = -1.0e30
LN_EPS = 1e-05
RMS_EPS = 1e-06

FULL = [[(0, 0, HALF, None), (HALF, HALF, HALF, None)] for _ in range(NT)]


def banded_segments():
    out = [[(0, 0, HALF, ("row0", 0)), (HALF, HALF, HALF, ("row0", HALF))],
           [(0, 0, 3 * P, ("first", 0))]]
    for r in range(2, NT):
        n = (min(r + 2, NT) - (r - 1)) * P
        out.append([(0, (r - 1) * P, n, ("band", 0)), (n, 0, 1, None)])
    return out


BANDED = banded_segments()


class Chain:

    def __init__(self, engine, semaphore, base=0):
        self.engine, self.semaphore, self.base, self.k = engine, semaphore, base, 0

    def mark(self, instruction):
        self.k += 1
        instruction.then_inc(self.semaphore, 1)

    def settle(self):
        self.engine.wait_ge(self.semaphore, self.base + self.k)

    def do(self, instruction):
        self.mark(instruction)
        self.settle()


def apart(engine, passed):
    engine.sem_inc(passed, 1)


def new_semaphore(nc, M, name):
    handle = nc.alloc_semaphore(name)
    M["semaphores"].append(handle)
    return handle


def clear_semaphores(nc, M):
    nc.clear_and_free_semaphores(M["semaphores"])
    nc.all_engine_barrier()
    M["semaphores"] = []


def bc_free(ap, n):
    return ap.unsqueeze(len(ap.shape)).broadcast_to(list(ap.shape) + [n])


def normalise(dve, chain, dst, src, stats, mv, rstd, tiles, stats_ready, rstd_ready, occasion, passed):
    for t in range(tiles):
        last = dve.bn_stats(stats[:, t, :], src[:, t, :])
    chain.do(last)
    apart(dve, passed)
    for t in range(tiles):
        last = dve.bn_aggr(mv[:, t, :], stats[:, t, :])
    last.then_inc(stats_ready, 1)
    dve.wait_ge(rstd_ready, occasion + 1)
    for t in range(tiles):
        last = dve.tensor_scalar(dst[:, t, :], src[:, t, :], mv[:, t, 0:1], rstd[:, t:t + 1],
                                 ALU.subtract, ALU.mult)
    return last


def rms_normalise(dve, chain, dst, src, square, ms, rstd, tiles, stats_ready, rstd_ready, occasion):
    chain.do(dve.tensor_tensor(square, src[:], src[:], ALU.mult))
    dve.tensor_reduce(ms, square, AX.X, ALU.add).then_inc(stats_ready, 1)
    dve.wait_ge(rstd_ready, occasion + 1)
    for t in range(tiles):
        last = dve.tensor_scalar(dst[:, t, :], src[:, t, :], rstd[:, t:t + 1], None, ALU.mult)
    return last


def make_rstd(pool, chain, rstd, src, tmp, minus_half, scale, eps, stats_ready, rstd_ready, occasion, passed):
    pool.wait_ge(stats_ready, occasion + 1)
    apart(pool, passed)
    chain.do(pool.tensor_scalar(tmp, src, scale, eps, ALU.mult, ALU.add))
    pool.tensor_tensor(rstd, tmp, minus_half, ALU.pow).then_inc(rstd_ready, 1)


def setup(nc, A, M):
    with ExitStack() as ctx:
        sem = lambda name: new_semaphore(nc, M, "su_" + name)
        sb = lambda name, shape, dt=F32: ctx.enter_context(nc.sbuf_tensor("su_" + name, shape, dt))
        pt = ctx.enter_context(nc.psum_tensor("su_pt", [P, 8, HALF], F32))
        flip = sb("flip", [P, 5, P])
        wo_nat = sb("wo_nat", [P, P])
        wo_sp = sb("wo_sp", [P, UPB, G, 32])
        qvT = sb("qvT", [P, 2, P])
        group = sb("group", [P, P])
        wbeta = sb("wbeta", [P, H])
        rows = sb("rows", [P, P])
        weights_in, consts, masks, placed = sem("weights_in"), sem("consts"), sem("masks"), sem("placed")
        spread, flipped, kept, folded = sem("spread"), sem("flipped"), sem("kept"), sem("folded")
        pool_chain = sem("pool_chain")
        block = ctx.enter_context(nc.Block())
        NB1 = E * (A["L0_ffn_b1"].shape[1] // P)
        loads = [(flip[:, n, :], A[k][:, :]) for n, k in enumerate(
            ["L0_attn_Wq", "L0_attn_Wk", "L0_attn_Wv", "L1_attn_Wq", "L1_attn_Wv"])]
        loads += [(wo_nat[:], A["L0_attn_Wo"]), (wbeta[:], A["L1_attn_Wbeta"])]
        loads += [(M["w1d"][:, 1, :], A["L1_attn_Wk"]), (M["w1d"][:, 4, :], A["L1_attn_Wo"])]
        loads += [(M["w1a"][:, n, :], A[k]) for n, k in enumerate(["L1_ffn_wq", "L1_ffn_wk", "L1_ffn_wv"])]
        row = lambda k: A[k].unsqueeze(0).broadcast_to([P, P])
        loads += [(M["bo"][:], row("L1_attn_b_o")), (M["lng"][:], row("L1_attn_ln_g")),
                  (M["lnb"][:], row("L1_attn_ln_b"))]
        loads += [(M["norm"][:, 0:1], A["L1_ffn_norm1_w"].unsqueeze(1)),
                  (M["norm"][:, 1:2], A["L1_ffn_norm2_w"].unsqueeze(1))]
        loads += [(M["rw"][:, 0, :], A["L0_ffn_router_W"]), (M["rw"][:, 1, :], A["L1_ffn_router_w"]),
                  (M["rb"][:], A["L0_ffn_router_b"].unsqueeze(0).broadcast_to([P, E]))]
        bb = A["L1_attn_b_beta"].unsqueeze(1).broadcast_to([H, HD])
        NLOAD = len(loads) + 1

        @block.sync
        def _(sp):
            for dst, src in loads:
                sp.dma_start(dst, src).then_inc(weights_in, 16)
            sp.dma_start(M["bbeta"][:], bb).then_inc(weights_in, 16)
            sp.wait_ge(consts, 3)
            sp.dma_start(rows[0:E, :], A["L0_ffn_ln_g"]).then_inc(placed, 16)
            sp.dma_start(rows[E:2 * E, :], A["L0_ffn_ln_b"]).then_inc(placed, 16)
            sp.dma_start(rows[2 * E:2 * E + NB1, :],
                         A["L0_ffn_b1"].rearrange("e (f p) -> (e f) p", p=P)).then_inc(placed, 16)
            wo = A["L1_ffn_wo"].rearrange("(g j d) n -> j d g n", j=G, d=HD)
            for j in range(G):
                sp.dma_start(M["wop1"][32 * j:32 * j + HD, :, :], wo[j]).then_inc(placed, 16)
            sp.wait_ge(placed, 16 * (G + 3))

        @block.gpsimd
        def _(pool):
            ch = Chain(pool, pool_chain)
            pool.memset(M["wop1"][:], 0.0).then_inc(consts, 1)
            pool.memset(wo_sp[:], 0.0).then_inc(consts, 1)
            pool.memset(rows[:], 0.0).then_inc(consts, 1)
            pool.memset(M["minus_half"][:], -0.5).then_inc(consts, 1)
            for t in (M["identF"], M["identB"], M["pick_sum"], M["row0"], M["first"], M["band"], M["before"]):
                ch.mark(pool.memset(t[:], 0.0))
            ch.mark(pool.memset(group[:], 1.0))
            ch.settle()
            for t in (M["identF"], M["identB"]):
                ch.mark(pool.affine_select(out=t[:], in_=t[:], compare_op=ALU.not_equal, fill=1.0, base=0,
                                           pattern=[[-1, P]], channel_multiplier=1))
            ps = M["pick_sum"][:].rearrange("p (j c) -> p j c", c=32)
            ch.mark(pool.affine_select(out=ps, in_=ps, compare_op=ALU.not_equal, fill=1.0, base=-HD,
                                       pattern=[[-32, G], [0, 32]], channel_multiplier=1))
            bf = M["before"][:]
            ch.mark(pool.affine_select(out=bf, in_=bf, compare_op=ALU.is_ge, fill=1.0, base=0,
                                       pattern=[[-1, E], [1, E]], channel_multiplier=0))
            g3 = group[:].rearrange("p (h d) -> p h d", d=HD)
            ch.do(pool.affine_select(out=g3, in_=g3, compare_op=ALU.is_ge, fill=0.0, base=0,
                                     pattern=[[-HD, H], [0, HD]], channel_multiplier=1))
            ch.do(pool.affine_select(out=g3, in_=g3, compare_op=ALU.is_ge, fill=0.0, base=HD - 1,
                                     pattern=[[HD, H], [0, HD]], channel_multiplier=-1))
            low = lambda ap: pool.affine_select(out=ap, in_=ap, compare_op=ALU.is_ge, fill=MASKED, base=0,
                                                pattern=[[1, P]], channel_multiplier=-1)
            high = lambda ap: pool.affine_select(out=ap, in_=ap, compare_op=ALU.is_ge, fill=MASKED, base=0,
                                                 pattern=[[-1, P]], channel_multiplier=1)
            ch.mark(low(M["band"][:, 0:P]))
            ch.mark(high(M["band"][:, 2 * P:3 * P]))
            ch.mark(low(M["first"][:, 0:P]))
            ch.mark(high(M["first"][:, 2 * P:3 * P]))
            ch.mark(high(M["row0"][:, P:2 * P]))
            ch.mark(pool.memset(M["row0"][:, 2 * P:], MASKED))
            ch.settle()
            pool.memset(M["first"][:, 0:1], 0.0).then_inc(masks, 1)
            pool.memset(M["row0"][0:1, :], 0.0).then_inc(masks, 1)

        @block.vector
        def _(dve):
            dve.wait_ge(weights_in, 16 * NLOAD)
            dve.wait_ge(consts, 3)
            dve.tensor_copy(wo_sp[:, :, :, 0:HD],
                            wo_nat[:].rearrange("p (g j d) -> p g j d", g=UPB, j=G)).then_inc(spread, 1)
            dve.tensor_copy(M["w1d"][:, 3, :].rearrange("p (h d) -> p h d", d=HD),
                            bc_free(wbeta[:], HD)).then_inc(spread, 1)
            dve.wait_ge(flipped, 1)
            dve.tensor_copy(M["w0a"][:], pt[:, 0, 0:3 * P].rearrange("p (n c) -> p n c", c=P)).then_inc(kept, 1)
            dve.tensor_copy(qvT[:], pt[:, 1, 0:2 * P].rearrange("p (n c) -> p n c", c=P)).then_inc(kept, 1)
            dve.tensor_copy(M["wop0"][:], pt[:, 2, :].rearrange("p (n c) -> p n c", c=P)).then_inc(kept, 1)
            dve.wait_ge(folded, 1)
            dve.tensor_copy(M["w1d"][:, 0, :], pt[:, 3, 0:P]).then_inc(kept, 1)
            dve.tensor_copy(M["w1d"][:, 2, :], pt[:, 3, P:2 * P]).then_inc(kept, 1)
            dve.tensor_copy(M["cols"][:], pt[:, 3, 2 * P:2 * P + 2 * E + NB1]).then_inc(kept, 1)

        @block.tensor
        def _(pe):
            pe.wait_ge(weights_in, 16 * NLOAD)
            pe.wait_ge(pool_chain, 14)
            pe.wait_ge(spread, 2)
            for n in range(3):
                pe.transpose(pt[:, 0, n * P:(n + 1) * P], flip[:, n, :], M["identF"][:])
            for n in range(2):
                pe.transpose(pt[:, 1, n * P:(n + 1) * P], flip[:, 3 + n, :], M["identF"][:])
            for g in range(UPB):
                last = pe.transpose(pt[:, 2, g * P:(g + 1) * P], wo_sp[:, g].rearrange("p j c -> p (j c)"),
                                    M["identF"][:])
            last.then_inc(flipped, 1)
            pe.wait_ge(kept, 3)
            pe.wait_ge(placed, 16 * (G + 3))
            pe.transpose(pt[:, 3, 2 * P:3 * P], rows[:], M["identF"][:])
            for n in range(2):
                last = pe.matmul(pt[:, 3, n * P:(n + 1) * P], qvT[:, n, :], group[:], start=True, stop=True)
            last.then_inc(folded, 1)


def read_x(nc, A, M):
    with ExitStack() as ctx:
        sem = lambda name: new_semaphore(nc, M, "rx_" + name)
        xb = ctx.enter_context(nc.sbuf_tensor("rx_xb", [P, NT, P], F32))
        pt = ctx.enter_context(nc.psum_tensor("rx_pt", [P, NT, P], F32))
        x_in, taken, flipped, freed = sem("x_in"), sem("taken"), sem("flipped"), sem("freed")
        block = ctx.enter_context(nc.Block())
        x = A["L0_attn_x"].rearrange("b (t p) d -> b p t d", p=P)

        @block.sync
        def _(sp):
            sp.dma_start(xb[:], x[0]).then_inc(x_in, 16)
            with sp.Fori(1, B) as b:
                sp.wait_ge(taken, b)
                sp.wait_ge(flipped, b)
                apart(sp, M["passed"])
                sp.dma_start(xb[:], x[b]).then_inc(x_in, 16)

        @block.vector
        def _(dve):
            with dve.Fori(0, B) as b:
                dve.wait_ge(x_in, 16 * b + 16)
                dve.tensor_copy(M["X"][:, b], xb[:]).then_inc(taken, 1)

        @block.tensor
        def _(pe):
            with pe.Fori(0, B) as b:
                pe.wait_ge(x_in, 16 * b + 16)
                pe.wait_ge(freed, b + 1)
                for t in range(NT):
                    last = pe.transpose(pt[:, t, :], xb[:, t, :], M["identF"][:])
                last.then_inc(flipped, 1)

        @block.scalar
        def _(act):
            act.sem_inc(freed, 1)
            with act.Fori(0, B) as b:
                act.wait_ge(flipped, b + 1)
                act.activation(M["XT"][:, b, :], pt[:].rearrange("p t c -> p (t c)"), ACT.Copy).then_inc(freed, 1)


def project_qkv(nc, M, name, src, w):
    with ExitStack() as ctx:
        sem = lambda n: new_semaphore(nc, M, f"{name}_{n}")
        sb = lambda n, shape, dt=F32: ctx.enter_context(nc.sbuf_tensor(f"{name}_{n}", shape, dt))
        ps = lambda n: ctx.enter_context(nc.psum_tensor(f"{name}_{n}", [P, T], F32))
        prod = [ps("pq"), ps("pk")]
        pv, pvt = ps("pv"), ps("pvt")
        parts = [sb("qparts", [P, PARTS, T], BF16), sb("kparts", [P, PARTS, T], BF16)]
        rest = [sb("qrest", [P, T]), sb("krest", [P, T])]
        vT = sb("vT", [P, T])
        v9 = sb("v9", [P, UPB, NT, G, HD + 1])
        projected, first, second, third = sem("projected"), sem("first"), sem("second"), sem("third")
        rest1, rest_done = sem("rest1"), sem("rest_done")
        v_ready, v_kept, v_flipped, v_stored, parts_out = (sem("v_ready"), sem("v_kept"), sem("v_flipped"),
                                                           sem("v_stored"), sem("parts_out"))
        v_out = sem("v_out")
        block = ctx.enter_context(nc.Block())

        @block.gpsimd
        def _(pool):
            pool.memset(v9[:], 1.0).then_inc(v_out, 16)

        @block.tensor
        def _(pe):
            with pe.Fori(0, B) as b:
                for n in range(2):
                    pe.wait_ge(rest1, 2 * b + n + 1)
                    for half in range(2):
                        c = slice(half * HALF, (half + 1) * HALF)
                        last = pe.matmul(prod[n][:, c], w[:, n, :], src[:, b, c], start=True, stop=True)
                    last.then_inc(projected, 1)
                pe.wait_ge(v_kept, b + 1)
                for half in range(2):
                    c = slice(half * HALF, (half + 1) * HALF)
                    last = pe.matmul(pv[:, c], w[:, 2, :], src[:, b, c], start=True, stop=True)
                last.then_inc(v_ready, 1)
                pe.wait_ge(v_kept, b + 2)
                pe.wait_ge(v_stored, b + 1)
                for t in range(NT):
                    c = slice(t * P, (t + 1) * P)
                    last = pe.transpose(pvt[:, c], vT[:, c], M["identF"][:])
                last.then_inc(v_flipped, 1)

        @block.scalar
        def _(act):
            act.sem_inc(v_kept, 1)
            with act.Fori(0, B) as b:
                for n in range(2):
                    act.wait_ge(projected, 2 * b + n + 1)
                    act.wait_ge(parts_out, 32 * UPB * b + 1)
                    act.activation(parts[n][:, 0, :], prod[n][:], ACT.Copy).then_inc(first, 1)
                act.wait_ge(v_ready, b + 1)
                act.wait_ge(v_flipped, b + 1)
                act.activation(vT[:], pv[:], ACT.Copy).then_inc(v_kept, 1)
                for n in range(2):
                    act.wait_ge(rest1, 2 * b + n + 3)
                    act.activation(parts[n][:, 1, :], rest[n][:], ACT.Copy).then_inc(second, 1)

        @block.vector
        def _(dve):
            dve.sem_inc(rest1, 2)
            dve.sem_inc(v_stored, 1)
            dve.sem_inc(third, 1)
            with dve.Fori(0, B) as b:
                for n in range(2):
                    dve.wait_ge(first, 2 * b + n + 1)
                    if n == 0:
                        dve.wait_ge(third, 2 * b + 1)
                    dve.tensor_tensor(rest[n][:], prod[n][:], parts[n][:, 0, :], ALU.subtract).then_inc(rest1, 1)
                for n in range(2):
                    dve.wait_ge(second, 2 * b + n + 1)
                    dve.tensor_tensor(parts[n][:, 2, :], rest[n][:], parts[n][:, 1, :],
                                      ALU.subtract).then_inc(third, 1)
                dve.wait_ge(v_flipped, b + 2)
                dve.wait_ge(v_out, b * 16 + 16)
                v = pvt[:].rearrange("p (t g j d) -> p g t j d", t=NT, g=UPB, j=G)
                for g in range(UPB):
                    last = dve.tensor_copy(v9[:, g, :, :, 0:HD], v[:, g])
                last.then_inc(v_stored, 1)

        @block.sync
        def _(sp):
            sp.sem_inc(parts_out, 1)
            sp.sem_inc(v_flipped, 1)
            with sp.Fori(0, B) as b:
                for n in range(2):
                    sp.wait_ge(third, 2 * b + n + 2)
                    apart(sp, M["passed"])
                    for g in range(UPB):
                        rows = slice(32 * g, 32 * g + 32)
                        sp.dma_start(M["parts"][n, b, g].rearrange("i r t -> r i t"),
                                     parts[n][rows, :, :]).then_inc(parts_out, 16)
                sp.wait_ge(v_stored, b + 2)
                apart(sp, M["passed"])
                sp.dma_start(M["v9"].rearrange("(b g) p t j d -> b p g (t j d)", g=UPB)[b],
                             v9[:].rearrange("p g t j d -> p g (t j d)")).then_inc(v_out, 16)
            sp.wait_ge(parts_out, 32 * UPB * B + 1)
            sp.wait_ge(v_out, 16 * B + 16)


def attend(nc, M, name, segments):
    with ExitStack() as ctx:
        sem = lambda n: new_semaphore(nc, M, f"{name}_{n}")
        sb = lambda n, shape, dt=F32: ctx.enter_context(nc.sbuf_tensor(f"{name}_{n}", shape, dt))
        NBUF = 3
        Q = [sb(f"q{i}", [KMAX, G, T], BF16) for i in range(NBUF)]
        K = [sb(f"k{i}", [KMAX, G, T], BF16) for i in range(NBUF)]
        vu = [sb(f"vu{i}", [P, NT, G, HD + 1]) for i in range(NBUF)]
        negmax = [sb(f"negmax{i}", [P, P]) for i in range(NBUF)]
        mparts = sb("mparts", [32, PARTS, P], BF16)
        mrest = sb("mrest", [32, P])
        zero3 = sb("zero3", [PARTS, T], BF16)
        prob = sb("prob", [P, 2, G, T])
        osum = sb("osum", [P, T])
        one = [ctx.enter_context(nc.psum_tensor(f"{name}_one{i}", [P, T], F32)) for i in range(2)]
        st = ctx.enter_context(nc.psum_tensor(f"{name}_st", [P, 2, HALF], F32))
        o = ctx.enter_context(nc.psum_tensor(f"{name}_o", [P, T], F32))
        qk_in = [sem(f"qk_in{i}") for i in range(NBUF)]
        clean, clean_pool = sem("clean"), sem("clean_pool")
        one_ready, one_free = sem("one_ready"), sem("one_free")
        max_split, max_in, split_chain = sem("max_split"), sem("max_in"), sem("split_chain")
        st_ready, prob_ready, prob_free = sem("st_ready"), sem("prob_ready"), sem("prob_free")
        v_in = [sem(f"v_in{i}") for i in range(NBUF)]
        o_kept, o_done = sem("o_kept"), sem("o_done")
        block = ctx.enter_context(nc.Block())

        qparts = M["parts"][0].rearrange("b g i (h d) t -> (b g) i d h t", d=HD)
        kparts = M["parts"][1].rearrange("b g i (h d) t -> (b g) i d h t", d=HD)
        QK_LOADS = 16 * (2 * PARTS * PARTS + 1)
        ITEMS = G * NT
        ONE = ITEMS + 2
        wide = [len([s for s in row if s[2] > 1]) for row in segments]
        STEPS = G * sum(wide)

        def width(r):
            return sum(s[2] for s in segments[r])

        def pieces(r):
            if wide[r] == 2:
                return [(s[0], s[2], [s]) for s in segments[r]]
            return [(0, width(r), segments[r])]

        def scores(pe, dst, left, right, j, r, segs, at):
            for c0, t0, n, mask in segs:
                out = dst[:, c0 - at:c0 - at + n]
                if mask is not None:
                    pe.matmul(out, M["identB"][:], M[mask[0]][:, mask[1]:mask[1] + n], start=True, stop=False)
                last = pe.matmul(out, left[:, j, r * P:(r + 1) * P], right[:, j, t0:t0 + n],
                                 start=mask is None, stop=True)
            return last

        def stage1(pe, buf, k, n, parity):
            j, r = divmod(k, NT)
            pe.wait_ge(one_free, n + 1)
            scores(pe, one[parity], Q[buf], K[buf], j, r, segments[r], 0).then_inc(one_ready, 1)

        def flip_max(pe, buf, n, parity):
            pe.wait_ge(one_free, n + 2)
            pe.transpose(one[parity][:, 0:P], negmax[buf][:], M["identF"][:]).then_inc(one_ready, 1)

        def values(pe, buf, r):
            runs = []
            for c0, t0, n, _ in segments[r]:
                cut = min(max(HALF - t0, 0), n)
                if cut:
                    runs.append((c0, t0, cut))
                if n - cut:
                    runs.append((c0 + cut, t0 + cut, n - cut))
            for c0, t0, n in runs:
                for j in range(G):
                    last = pe.matmul(o[32 * j:32 * j + HD + 1, t0:t0 + n], vu[buf][:, r, j, :],
                                     prob[:, r % 2, j, c0:c0 + n], start=r == 0, stop=r == NT - 1,
                                     skip_group_check=True)
            last.then_inc(prob_free, 1)

        def pe_unit(pe, u, buf, v_loaded, next_loaded):
            after = (buf + 1) % NBUF
            base = ONE * u + ITEMS + 1
            issued = 0
            pe.wait_ge(max_in, 16 * PARTS * u + 16 * PARTS)
            pe.wait_ge(v_in[buf], v_loaded)
            if next_loaded is not None:
                pe.wait_ge(qk_in[after], next_loaded)
            step = 0
            for i in range(ITEMS):
                r, j = divmod(i, G)
                if next_loaded is not None:
                    while issued < ITEMS and issued * (ITEMS - 5) <= i * ITEMS:
                        stage1(pe, after, issued, base + issued, (ITEMS + 1 + issued) % 2)
                        issued += 1
                    if i == ITEMS - 3:
                        flip_max(pe, after, base + ITEMS, 1)
                for c0, n, segs in pieces(r):
                    pe.wait_ge(prob_ready, STEPS * u + step + 1)
                    last = scores(pe, st[:, step % 2, :], K[buf], Q[buf], j, r, segs, c0)
                    last.then_inc(st_ready, 1)
                    step += 1
                if j == G - 1 and r >= 1:
                    if r == 1:
                        pe.wait_ge(o_kept, u + 1)
                    pe.wait_ge(prob_ready, STEPS * u + G * sum(wide[:r]) + 2)
                    values(pe, buf, r - 1)
            pe.wait_ge(prob_ready, STEPS * u + STEPS + 2)
            values(pe, buf, NT - 1)
            pe.wait_ge(o_kept, u + 2)
            n, parity = (base + ITEMS + 1, 0) if next_loaded is not None else (base, 1)
            pe.wait_ge(one_free, n + 1)
            for half in range(2):
                c = slice(half * HALF, (half + 1) * HALF)
                last = pe.matmul(one[parity][:, c], M["pick_sum"][:], osum[:, c], start=True, stop=True)
            last.then_inc(one_ready, 1)

        @block.tensor
        def _(pe):
            pe.wait_ge(qk_in[0], QK_LOADS)
            pe.wait_ge(clean, 1 + NBUF)
            for k in range(ITEMS):
                stage1(pe, 0, k, k, k % 2)
            flip_max(pe, 0, ITEMS, 0)
            with pe.Fori(0, NU // NBUF) as i:
                for s in range(NBUF):
                    pe_unit(pe, i * NBUF + s, s, i * 16 + 16, i * QK_LOADS + QK_LOADS * (1 if s < NBUF - 1 else 2))
            pe_unit(pe, NU - 1, (NU - 1) % NBUF, 16 * (NU // NBUF) + 16, None)

        @block.scalar
        def _(act):
            act.sem_inc(prob_ready, 2)
            act.sem_inc(o_kept, 1)

            with act.Fori(0, NU) as u:
                step = 0
                for r in range(NT):
                    act.wait_ge(prob_free, u * NT + r + 1)
                    for j in range(G):
                        for c0, n, _ in pieces(r):
                            act.wait_ge(st_ready, u * STEPS + step + 1)
                            act.activation(prob[:, r % 2, j, c0:c0 + n], st[:, step % 2, 0:n], ACT.Exp,
                                           scale=SCALE).then_inc(prob_ready, 1)
                            step += 1
                act.wait_ge(prob_free, u * NT + NT + 2)
                act.wait_ge(o_done, u + 1)
                act.activation(osum[:], o[:], ACT.Copy).then_inc(o_kept, 1)

        @block.vector
        def _(dve):
            dve.memset(o[:], 0.0).then_inc(clean, 1)
            for t in negmax:
                dve.memset(t[:], 0.0).then_inc(clean, 1)
            dve.sem_inc(one_free, 2)
            dve.sem_inc(o_done, 1)
            dve.wait_ge(clean, 1 + NBUF)

            def maxima(buf, n0, parity):
                for k in range(ITEMS):
                    j, r = divmod(k, NT)
                    dve.wait_ge(one_ready, n0 + k + 1)
                    dve.tensor_reduce(negmax[buf][:, k:k + 1], one[(parity + k) % 2][:, 0:width(r)], AX.X,
                                      ALU.max, negate=True).then_inc(one_free, 1)

            def split_max(v, n, parity):
                chain = Chain(dve, split_chain, v * 3)
                dve.wait_ge(one_ready, n + 1)
                m = one[parity][0:32, 0:P]
                chain.do(dve.tensor_copy(mparts[:, 0, :], m))
                chain.mark(dve.tensor_tensor(mrest[:], m, mparts[:, 0, :], ALU.subtract))
                chain.settle()
                chain.do(dve.tensor_copy(mparts[:, 1, :], mrest[:]))
                dve.tensor_tensor(mparts[:, 2, :], mrest[:], mparts[:, 1, :], ALU.subtract).then_inc(max_split, 1)
                dve.wait_ge(max_split, v + 1)
                dve.sem_inc(one_free, 1)

            def scale_o(u, n, parity):
                dve.wait_ge(one_ready, n + 1)
                dve.reciprocal(M["OT"][:, u, :], one[parity][:]).then_inc(one_free, 1)
                dve.wait_ge(one_free, n + 3)
                dve.tensor_tensor(M["OT"][:, u, :], osum[:], M["OT"][:, u, :], ALU.mult).then_inc(o_done, 1)

            maxima(0, 0, 0)
            split_max(0, ITEMS, 0)
            with dve.Fori(0, NU // NBUF) as i:
                for s in range(NBUF):
                    u = i * NBUF + s
                    base = u * ONE + ITEMS + 1
                    maxima((s + 1) % NBUF, base, 1)
                    dve.wait_ge(max_in, u * 16 * PARTS + 16 * PARTS)
                    split_max(u + 1, base + ITEMS, 1)
                    scale_o(u, base + ITEMS + 1, 0)
            scale_o(NU - 1, (NU - 1) * ONE + ITEMS + 1, 1)

        @block.gpsimd
        def _(pool):
            for t in Q:
                pool.memset(t[64:96], 0.0).then_inc(clean_pool, 1)
            for t in K:
                pool.memset(t[64:96], 1.0).then_inc(clean_pool, 1)
            pool.memset(zero3[:], 0.0).then_inc(clean_pool, 1)
            pool.sem_inc(prob_free, 2)

        @block.sync
        def _(sp):
            sp.wait_ge(clean_pool, 2 * NBUF + 1)

            def load(v, s):
                for i in range(PARTS):
                    for j in range(PARTS):
                        rows = slice((PARTS * i + j) * HD, (PARTS * i + j + 1) * HD)
                        sp.dma_start(Q[s][rows], qparts[v, i]).then_inc(qk_in[s], 16)
                        sp.dma_start(K[s][rows], kparts[v, j]).then_inc(qk_in[s], 16)
                sp.dma_start(Q[s][KROWS:KROWS + PARTS],
                             zero3[:].unsqueeze(1).broadcast_to([PARTS, G, T])).then_inc(qk_in[s], 16)
                sp.dma_start(vu[s][:], M["v9"][v]).then_inc(v_in[s], 16)

            def send_max(v, s):
                sp.wait_ge(max_split, v + 1)
                for i in range(PARTS):
                    row = Q[s][KROWS + i:KROWS + i + 1].rearrange("o h (r a) -> o (h r) a", a=P)
                    sp.dma_start(row, mparts[:, i, :]).then_inc(max_in, 16)

            for v in range(NBUF):
                load(v, v)
            send_max(0, 0)
            with sp.Fori(0, NU // NBUF - 1) as i:
                for s in range(NBUF):
                    send_max(i * NBUF + s + 1, (s + 1) % NBUF)
                    sp.wait_ge(prob_free, i * (NBUF * NT) + (s + 1) * NT + 2)
                    apart(sp, M["passed"])
                    load(i * NBUF + NBUF + s, s)
            u = NU - 1 - NBUF
            send_max(u + 1, (u + 1) % NBUF)
            sp.wait_ge(prob_free, (u + 1) * NT + 2)
            load(NU - 1, (NU - 1) % NBUF)
            for v in range(u + 2, NU):
                send_max(v, v % NBUF)


def project_out(nc, M, name, wop, last_layer):
    with ExitStack() as ctx:
        sem = lambda n: new_semaphore(nc, M, f"{name}_{n}")
        sb = lambda n, shape, dt=F32: ctx.enter_context(nc.sbuf_tensor(f"{name}_{n}", shape, dt))
        ps = lambda n: ctx.enter_context(nc.psum_tensor(f"{name}_{n}", [P, T], F32))
        pp, pt, px, ph = ps("pp"), ps("pt"), ps("px"), ps("ph")
        aT = sb("aT", [P, T])
        y, xn, hn = (sb(n, [P, NT, P]) for n in ("y", "xn", "hn"))
        stats, mv = sb("stats", [P, NT, 6]), sb("mv", [P, NT, 2])
        ms, tmp, rstd = sb("ms", [P, NT]), sb("tmp", [P, NT]), sb("rstd", [P, NT])
        projected, a_kept, flipped, y_made = sem("projected"), sem("a_kept"), sem("flipped"), sem("y_made")
        stats_ready, rstd_ready, chain_d, chain_p = sem("stats_ready"), sem("rstd_ready"), sem("cd"), sem("cp")
        x_ready, h_ready, x_flipped, h_flipped = sem("x_ready"), sem("h_ready"), sem("x_flipped"), sem("h_flipped")
        xt_kept, ht_kept, x_stored = sem("xt_kept"), sem("ht_kept"), sem("x_stored")
        block = ctx.enter_context(nc.Block())
        halves = [slice(0, HALF), slice(HALF, T)]

        @block.tensor
        def _(pe):
            with pe.Fori(0, B) as b:
                pe.wait_ge(a_kept, b + 1)
                for c in halves:
                    for g in range(UPB):
                        last = pe.matmul(pp[:, c], wop[:, g, :], M["OT"][:, b * UPB + g, c],
                                         start=g == 0, stop=g == UPB - 1)
                last.then_inc(projected, 1)
                pe.wait_ge(a_kept, b + 2)
                pe.wait_ge(y_made, b + 1)
                for t in range(NT):
                    last = pe.transpose(pt[:, t * P:(t + 1) * P], aT[:, t * P:(t + 1) * P], M["identF"][:])
                last.then_inc(flipped, 1)
                if not last_layer:
                    pe.wait_ge(x_ready, b + 1)
                    pe.wait_ge(xt_kept, b + 1)
                    for t in range(NT):
                        last = pe.transpose(px[:, t * P:(t + 1) * P], xn[:, t, :], M["identF"][:])
                    last.then_inc(x_flipped, 1)
                pe.wait_ge(h_ready, b + 1)
                pe.wait_ge(ht_kept, b + 1)
                for t in range(NT):
                    last = pe.transpose(ph[:, t * P:(t + 1) * P], hn[:, t, :], M["identF"][:])
                last.then_inc(h_flipped, 1)

        @block.scalar
        def _(act):
            act.sem_inc(a_kept, 1)
            act.sem_inc(xt_kept, 1)
            act.sem_inc(ht_kept, 1)
            act.sem_inc(flipped, 1)
            with act.Fori(0, B) as b:
                act.wait_ge(projected, b + 1)
                act.wait_ge(flipped, b + 1)
                act.activation(aT[:], pp[:], ACT.Copy).then_inc(a_kept, 1)
                if not last_layer:
                    act.wait_ge(x_flipped, b + 1)
                    act.activation(M["XT"][:, b, :], px[:], ACT.Copy).then_inc(xt_kept, 1)
                act.wait_ge(h_flipped, b + 1)
                if last_layer:
                    act.activation(M["HT"][:, b, :], ph[:], ACT.Copy, scale=M["norm"][:, 1:2]).then_inc(ht_kept, 1)
                else:
                    act.activation(M["HT"][:, b, :], ph[:], ACT.Copy).then_inc(ht_kept, 1)

        @block.vector
        def _(dve):
            dve.sem_inc(y_made, 1)
            PER = 3 if last_layer else 4
            with dve.Fori(0, B) as b:
                ch = Chain(dve, chain_d, b * PER)
                dve.wait_ge(flipped, b + 2)
                ptt = pt[:].rearrange("p (t c) -> p t c", c=P)
                dve.tensor_tensor(y[:], ptt, M["X"][:, b], ALU.add).then_inc(y_made, 1)
                dve.wait_ge(y_made, b + 2)
                if last_layer:
                    dve.wait_ge(ht_kept, b + 1)
                    ch.do(rms_normalise(dve, ch, hn, y, xn[:], ms[:], rstd, NT, stats_ready, rstd_ready, b))
                    dve.sem_inc(h_ready, 1)
                    ch.do(dve.tensor_tensor(M["X"][:, b], M["X"][:, b], y[:], ALU.add))
                else:
                    dve.wait_ge(xt_kept, b + 1)
                    dve.wait_ge(x_stored, b + 1)
                    ch.do(normalise(dve, ch, xn, y, stats, mv, rstd, NT, stats_ready, rstd_ready, b * 2, M["passed"]))
                    dve.sem_inc(x_ready, 1)
                    dve.wait_ge(ht_kept, b + 1)
                    ch.do(normalise(dve, ch, hn, xn, stats, mv, rstd, NT, stats_ready, rstd_ready, b * 2 + 1, M["passed"]))
                    dve.sem_inc(h_ready, 1)
                assert ch.k == PER

        @block.gpsimd
        def _(pool):
            pool.sem_inc(x_stored, 1)
            with pool.Fori(0, B) as b:
                if last_layer:
                    make_rstd(pool, Chain(pool, chain_p, b), rstd[:], ms[:], tmp[:], M["minus_half"][:, 0:NT],
                              1.0 / P, RMS_EPS, stats_ready, rstd_ready, b, M["passed"])
                else:
                    for n in range(2):
                        make_rstd(pool, Chain(pool, chain_p, b * 2 + n), rstd[:], mv[:, :, 1], tmp[:],
                                  M["minus_half"][:, 0:NT], 1.0, LN_EPS, stats_ready, rstd_ready, b * 2 + n, M["passed"])
                        if n == 0:
                            pool.wait_ge(x_ready, b + 1)
                            apart(pool, M["passed"])
                            pool.tensor_copy(M["X"][:, b], xn[:]).then_inc(x_stored, 1)


def route(nc, M, name, src, layer):
    TT = B * NT
    with ExitStack() as ctx:
        sem = lambda n: new_semaphore(nc, M, f"{name}_{n}")
        sb = lambda n, shape, dt=F32: ctx.enter_context(nc.sbuf_tensor(f"{name}_{n}", shape, dt))
        xs = sb("xs", [P, T])
        logits, expd, prob = sb("logits", [P, TT, E]), sb("expd", [P, TT, E]), sb("prob", [P, TT, E])
        cmp1, cmp2 = sb("cmp1", [P, TT, E, E]), sb("cmp2", [P, TT, E, E])
        top, total, inv = sb("top", [P, TT]), sb("total", [P, TT]), sb("inv", [P, TT])
        rank = sb("rank", [P, TT, E])
        pl = ctx.enter_context(nc.psum_tensor(f"{name}_pl", [P, HALF], F32))
        staged, judged, kept, chain_d, shifted, exped = (sem("staged"), sem("judged"), sem("kept"),
                                                         sem("cd"), sem("shifted"), sem("exped"))
        block = ctx.enter_context(nc.Block())

        @block.scalar
        def _(act):
            act.sem_inc(judged, 1)
            with act.Fori(0, B) as b:
                act.wait_ge(judged, b + 1)
                act.activation(xs[:], src[:, b, :], ACT.Copy).then_inc(staged, 1)
            for n in range(1 + layer):
                act.wait_ge(shifted, n + 1)
                act.activation(expd[:], expd[:], ACT.Exp).then_inc(exped, 1)

        @block.tensor
        def _(pe):
            with pe.Fori(0, B) as b:
                pe.wait_ge(staged, b + 1)
                pe.wait_ge(kept, b + 1)
                for t in range(NT):
                    last = pe.matmul(pl[:, t * E:(t + 1) * E], xs[:, t * P:(t + 1) * P], M["rw"][:, layer, :],
                                     start=True, stop=True)
                last.then_inc(judged, 1)

        @block.vector
        def _(dve):
            dve.sem_inc(kept, 1)
            lb = logits[:].rearrange("p (b t) e -> p b t e", b=B)
            with dve.Fori(0, B) as b:
                dve.wait_ge(judged, b + 2)
                dve.tensor_copy(lb[:, b], pl[:, 0:NT * E].rearrange("p (t e) -> p t e", e=E)).then_inc(kept, 1)
            dve.wait_ge(kept, B + 1)
            ch = Chain(dve, chain_d)
            if layer == 0:
                ch.do(dve.tensor_tensor(logits[:], logits[:], M["rb"][:].unsqueeze(1).broadcast_to([P, TT, E]),
                                        ALU.add))

            def shift(src):
                ch.do(dve.tensor_reduce(top[:], src[:], AX.X, ALU.max))
                dve.tensor_tensor(expd[:], src[:], bc_free(top[:], E), ALU.subtract).then_inc(shifted, 1)

            def divide(dst):
                ch.do(dve.tensor_reduce(total[:], expd[:], AX.X, ALU.add))
                ch.do(dve.reciprocal(inv[:], total[:]))
                ch.do(dve.tensor_tensor(dst, expd[:], bc_free(inv[:], E), ALU.mult))

            shift(logits)
            judge = logits
            if layer == 1:
                dve.wait_ge(exped, 1)
                divide(prob[:])
                shift(prob)
                judge = prob
            other = judge[:].unsqueeze(2).broadcast_to([P, TT, E, E])
            own = bc_free(judge[:], E)
            ch.mark(dve.tensor_tensor(cmp1[:], other, own, ALU.is_gt))
            ch.do(dve.tensor_tensor(cmp2[:], other, own, ALU.is_equal))
            ch.do(dve.tensor_tensor(cmp2[:], cmp2[:], M["before"][:].unsqueeze(1).broadcast_to([P, TT, E, E]),
                                    ALU.mult))
            ch.do(dve.tensor_tensor(cmp1[:], cmp1[:], cmp2[:], ALU.add))
            ch.do(dve.tensor_reduce(rank[:], cmp1[:], AX.X, ALU.add))
            ch.do(dve.tensor_scalar(rank[:], rank[:], 2.0, None, ALU.is_lt))
            dve.wait_ge(exped, 1 + layer)
            ch.do(dve.tensor_tensor(expd[:], expd[:], rank[:], ALU.mult))
            divide(M["gates"][:])
            ch.do(dve.tensor_reduce(M["gate_sum"][:], M["gates"][:], AX.X, ALU.add))


def experts(nc, A, M, name, layer, out):
    F = A["L0_ffn_W1"].shape[2] if layer == 0 else A["L1_ffn_e_gate"].shape[2]
    NE = E if layer == 0 else E + 1
    FB = F // P
    with ExitStack() as ctx:
        sem = lambda n: new_semaphore(nc, M, f"{name}_{n}")
        sb = lambda n, shape, dt=F32: ctx.enter_context(nc.sbuf_tensor(f"{name}_{n}", shape, dt))
        up = sb("up", [P, NE, BANKS, P])
        down = sb("down", [P, NE, FB, P])
        h = sb("h", [P, 2, HALF])
        hidden = sb("hidden", [P, 2, FB, HALF])
        silu = sb("silu", [P, FB, HALF])
        gch = sb("gch", [P, P])
        gsc = sb("gsc", [P, CT])
        gT = sb("gT", [CT * E, P])
        acc, y, xn = sb("acc", [P, CT, P]), sb("y", [P, CT, P]), sb("xn", [P, CT, P])
        stats, mv = sb("stats", [P, CT, 6]), sb("mv", [P, CT, 2])
        tmp, rstd = sb("tmp", [P, CT]), sb("rstd", [P, CT])
        lng, lnb = M["cols"][:, 0:E], M["cols"][:, E:2 * E]
        b1 = M["cols"][:, 2 * E:].rearrange("p (e f) -> p e f", f=BANKS)
        b2p = sb("b2p", [CT * E, CT, P])
        pa = ctx.enter_context(nc.psum_tensor(f"{name}_pa", [P, BANKS, HALF], F32))
        py = [ctx.enter_context(nc.psum_tensor(f"{name}_py{i}", [P, CT, P], F32)) for i in range(2)]
        pg = ctx.enter_context(nc.psum_tensor(f"{name}_pg", [P, CT, P], F32))
        px = ctx.enter_context(nc.psum_tensor(f"{name}_px", [P, CT, P], F32))
        w_in, clean, g_staged, g_flipped, g_kept, bias_ready = (sem("w_in"), sem("clean"), sem("g_staged"),
                                                                sem("g_flipped"), sem("g_kept"), sem("bias_ready"))
        h_ready, a_ready, a_free, u_free, y_ready, y_free = (sem("h_ready"), sem("a_ready"), sem("a_free"),
                                                             sem("u_free"), sem("y_ready"), sem("y_free"))
        stats_ready, rstd_ready, chain_d, chain_p = sem("stats_ready"), sem("rstd_ready"), sem("cd"), sem("cp")
        x_ready, x_flipped, xt_kept, x_stored = sem("x_ready"), sem("x_flipped"), sem("xt_kept"), sem("x_stored")
        block = ctx.enter_context(nc.Block())

        X = M["X"][:].rearrange("p b (k t) d -> p (b k) t d", t=CT)
        XT = M["XT"].rearrange("p b (k c) -> p (b k) c", c=HALF)
        HT = M["HT"][:].rearrange("p b (k c) -> p (b k) c", c=HALF)
        gates = M["gates"][:].rearrange("p (k t) e -> p k t e", t=CT)
        gate_sum = M["gate_sum"][:].rearrange("p (k t) -> p k t", t=CT)
        out_v = out.rearrange("b (k t p) d -> (b k) p t d", t=CT, p=P)
        loads = []
        if layer == 0:
            loads += [(up[:].rearrange("p e f c -> p e (f c)"), A["L0_ffn_W1"].rearrange("e p f -> p e f")),
                      (down[:], A["L0_ffn_W2"].rearrange("e (f p) n -> p e f n", p=P))]
        else:
            two = lambda n: up[:, 0:E, FB * n:FB * n + FB, :].rearrange("p e f c -> p e (f c)")
            one = lambda n: up[:, E, FB * n:FB * n + FB, :].rearrange("p f c -> p (f c)")
            loads += [(two(0), A["L1_ffn_e_gate"].rearrange("e p f -> p e f")),
                      (two(1), A["L1_ffn_e_up"].rearrange("e p f -> p e f")),
                      (one(0), A["L1_ffn_sh_gate"]), (one(1), A["L1_ffn_sh_up"]),
                      (down[:, 0:E], A["L1_ffn_e_down"].rearrange("e (f p) n -> p e f n", p=P)),
                      (down[:, E], A["L1_ffn_sh_down"].rearrange("(f p) n -> p f n", p=P))]
        NLOAD = len(loads) + (CT if layer == 0 else 0)

        @block.sync
        def _(sp):
            for dst, src in loads:
                sp.dma_start(dst, src).then_inc(w_in, 16)
            if layer == 0:
                sp.wait_ge(clean, 2)
                for t in range(CT):
                    sp.dma_start(b2p[E * t:E * t + E, t, :], A["L0_ffn_b2"]).then_inc(w_in, 16)
            else:
                with sp.Fori(0, CH) as c:
                    sp.wait_ge(x_ready, c + 1)
                    apart(sp, M["passed"])
                    sp.dma_start(out_v[c], xn[:]).then_inc(x_stored, 16)
                sp.wait_ge(x_stored, 16 * CH + 16)

        @block.gpsimd
        def _(pool):
            pool.memset(gch[:], 0.0).then_inc(clean, 1)
            pool.memset(b2p[:], 0.0).then_inc(clean, 1)
            pool.sem_inc(x_stored, 16)
            with pool.Fori(0, CH) as c:
                make_rstd(pool, Chain(pool, chain_p, c), rstd[:], mv[:, :, 1], tmp[:], M["minus_half"][:, 0:CT],
                          1.0, LN_EPS, stats_ready, rstd_ready, c, M["passed"])
                if layer == 0:
                    pool.wait_ge(x_ready, c + 1)
                    apart(pool, M["passed"])
                    pool.tensor_copy(X[:, c], xn[:]).then_inc(x_stored, 16)

        FREED = FB if layer == 1 else BANKS

        def reusable(eng, semaphore, c, e):
            eng.wait_ge(semaphore, c * NE + (2 if e < 2 else e + 1))

        @block.tensor
        def _(pe):
            pe.sem_inc(a_ready, 1)
            pe.sem_inc(y_ready, 2)
            pe.wait_ge(w_in, 16 * NLOAD)
            pe.wait_ge(clean, 2)

            def rise(c, e):
                if layer == 0:
                    pe.wait_ge(h_ready, c * NE + e + 1)
                for f in range(BANKS):
                    if layer == 0:
                        pe.wait_ge(a_free, c * (NE * BANKS) + e * BANKS + f + 1)
                    elif f < FB:
                        pe.wait_ge(a_free, c * (NE * FB) + e * FB + f + 1)
                    else:
                        pe.wait_ge(u_free, c * (NE * FB) + e * FB + f - FB + 1)
                    pe.matmul(pa[:, f, :], up[:, e, f, :], h[:, e % 2, :] if layer == 0 else HT[:, c],
                              start=True, stop=True).then_inc(a_ready, 1)

            def fall(c, e):
                hidden_made = a_free if layer == 0 else u_free
                pe.wait_ge(hidden_made, c * (NE * FREED) + (e + 2) * FREED)
                reusable(pe, y_free, c, e)
                for t in range(CT):
                    for f in range(FB):
                        last = pe.matmul(py[e % 2][:, t, :], hidden[:, e % 2, f, t * P:(t + 1) * P],
                                         down[:, e, f, :], start=f == 0, stop=f == FB - 1)
                last.then_inc(y_ready, 1)

            with pe.Fori(0, CH) as c:
                if layer == 0:
                    pe.wait_ge(g_staged, c + 1)
                    pe.transpose(pg[:, 0, :], gch[:], M["identF"][:]).then_inc(g_flipped, 1)
                    pe.wait_ge(g_kept, c + 1)
                    for t in range(CT):
                        last = pe.matmul(pg[:, t, :], gT[:], b2p[:, t, :], start=True, stop=True)
                    last.then_inc(bias_ready, 1)
                rise(c, 0)
                for e in range(1, NE):
                    rise(c, e)
                    fall(c, e - 1)
                fall(c, NE - 1)
                if layer == 0:
                    pe.wait_ge(x_ready, c + 1)
                    pe.wait_ge(xt_kept, c + 1)
                    for t in range(CT):
                        last = pe.transpose(px[:, t, :], xn[:, t, :], M["identF"][:])
                    last.then_inc(x_flipped, 1)

        @block.scalar
        def _(act):
            act.sem_inc(a_free, FREED)
            act.sem_inc(xt_kept, 1)
            act.wait_ge(w_in, 16 * NLOAD)
            with act.Fori(0, CH) as c:
                if layer == 0:
                    act.wait_ge(g_flipped, c + 1)
                    act.activation(gT[:], pg[0:CT * E, 0, :], ACT.Copy).then_inc(g_kept, 1)
                for e in range(NE):
                    if layer == 0:
                        reusable(act, y_ready, c, e)
                    for f in range(FREED):
                        act.wait_ge(a_ready, c * (NE * BANKS) + e * BANKS + f + 2)
                        if layer == 0:
                            act.activation(hidden[:, e % 2, f, :], pa[:, f, :], ACT.Gelu,
                                           bias=b1[:, e, f:f + 1]).then_inc(a_free, 1)
                        else:
                            act.wait_ge(u_free, c * (NE * FB) + e * FB + f + 1)
                            act.activation(silu[:, f, :], pa[:, f, :], ACT.Silu).then_inc(a_free, 1)
                if layer == 0:
                    act.wait_ge(x_flipped, c + 1)
                    act.activation(XT[:, c], px[:].rearrange("p t d -> p (t d)"), ACT.Copy).then_inc(xt_kept, 1)

        @block.vector
        def _(dve):
            dve.sem_inc(y_free, 2)
            if layer == 1:
                dve.sem_inc(u_free, FB)
            dve.wait_ge(w_in, 16 * NLOAD)
            dve.wait_ge(clean, 2)
            PER = NE + (4 if layer == 0 else 3)

            def feed(c, e):
                dve.wait_ge(a_ready, c * (NE * BANKS) + (max(e - 1, 0) * BANKS + 1))
                dve.tensor_scalar(h[:, e % 2, :], HT[:, c], lng[:, e:e + 1], lnb[:, e:e + 1],
                                  ALU.mult, ALU.add).then_inc(h_ready, 1)

            def gate_up(c, e):
                reusable(dve, y_ready, c, e)
                for f in range(FB):
                    dve.wait_ge(a_ready, c * (NE * BANKS) + e * BANKS + FB + f + 2)
                    dve.wait_ge(a_free, c * (NE * FB) + e * FB + FB + f + 1)
                    dve.tensor_tensor(hidden[:, e % 2, f, :], silu[:, f, :], pa[:, FB + f, :],
                                      ALU.mult).then_inc(u_free, 1)

            def add(c, e, ch):
                dve.wait_ge(y_ready, c * NE + e + 3)
                for t in range(CT):
                    g = gch[:, t * E + e:t * E + e + 1]
                    if layer == 1 and e == 0:
                        last = dve.tensor_scalar(acc[:, t, :], py[0][:, t, :], g, None, ALU.mult)
                    elif e < E:
                        last = dve.scalar_tensor_tensor(acc[:, t, :], py[e % 2][:, t, :], g, acc[:, t, :],
                                                        ALU.mult, ALU.add)
                if e == E:
                    last = dve.tensor_tensor(acc[:], acc[:], py[e % 2][:], ALU.add)
                ch.do(last)
                dve.sem_inc(y_free, 1)

            with dve.Fori(0, CH) as c:
                ch = Chain(dve, chain_d, c * PER)
                ch.do(dve.tensor_copy(gsc[:], gate_sum[:, c]))
                dve.tensor_copy(gch[:, 0:CT * E].rearrange("p (t e) -> p t e", e=E), gates[:, c]).then_inc(g_staged, 1)
                dve.wait_ge(g_staged, c + 1)
                if layer == 0:
                    feed(c, 0)
                    dve.wait_ge(bias_ready, c + 1)
                    for t in range(CT):
                        last = dve.scalar_tensor_tensor(acc[:, t, :], X[:, c, t, :], gsc[:, t:t + 1], pg[:, t, :],
                                                        ALU.mult, ALU.add)
                    ch.do(last)
                for e in range(NE):
                    if layer == 0 and e + 1 < NE:
                        feed(c, e + 1)
                    if layer == 1:
                        gate_up(c, e)
                    if e:
                        add(c, e - 1, ch)
                add(c, NE - 1, ch)
                ch.do(dve.tensor_tensor(y[:], acc[:], X[:, c], ALU.add))
                if layer == 0:
                    dve.wait_ge(xt_kept, c + 1)
                    dve.wait_ge(x_stored, c + 1)
                else:
                    dve.wait_ge(x_stored, c * 16 + 16)
                normalise(dve, ch, xn, y, stats, mv, rstd, CT, stats_ready, rstd_ready, c, M["passed"]).then_inc(x_ready, 1)
                assert ch.k == PER


def scan_layer(nc, M, name):
    with ExitStack() as ctx:
        sem = lambda n: new_semaphore(nc, M, f"{name}_{n}")
        sb = lambda n, shape, dt=F32: ctx.enter_context(nc.sbuf_tensor(f"{name}_{n}", shape, dt))
        pw = [ctx.enter_context(nc.psum_tensor(f"{name}_pw{i}", [P, T], F32)) for i in range(4)]
        k, beta, kv, state, o = sb("k", [P, T]), sb("beta", [P, T]), sb("kv", [P, T]), sb("state", [P, T]), sb("o", [P, T])
        xb, y, z, xn, hn = (sb(n, [P, NT, P]) for n in ("xb", "y", "z", "xn", "hn"))
        stats, mv = sb("stats", [P, NT, 6]), sb("mv", [P, NT, 2])
        ms, tmp, rstd = sb("ms", [P, NT]), sb("tmp", [P, NT]), sb("rstd", [P, NT])
        projected, evacuated, o_ready, out_ready, y_made = (sem("projected"), sem("evacuated"), sem("o_ready"),
                                                            sem("out_ready"), sem("y_made"))
        xb_ready, h_ready, h_flipped, ht_kept, x_ready, x_stored = (sem("xb_ready"), sem("h_ready"), sem("h_flipped"),
                                                                    sem("ht_kept"), sem("x_ready"), sem("x_stored"))
        stats_ready, rstd_ready, chain_d, chain_p = sem("stats_ready"), sem("rstd_ready"), sem("cd"), sem("cp")
        block = ctx.enter_context(nc.Block())
        pout, ph = pw[0], pw[1]
        SETS = 3

        @block.tensor
        def _(pe):
            with pe.Fori(0, B) as b:
                pe.wait_ge(ht_kept, b + 1)
                for n in (1, 2, 3, 0):
                    for half in range(2):
                        c = slice(half * HALF, (half + 1) * HALF)
                        last = pe.matmul(pw[n][:, c], M["w1d"][:, n, :], M["XT"][:, b, c], start=True, stop=True)
                    last.then_inc(projected, 1)
                pe.wait_ge(o_ready, b + 1)
                for t in range(NT):
                    last = pe.matmul(pout[:, t * P:(t + 1) * P], o[:, t * P:(t + 1) * P], M["w1d"][:, 4, :],
                                     start=True, stop=True)
                last.then_inc(out_ready, 1)
                pe.wait_ge(h_ready, b + 1)
                for t in range(NT):
                    last = pe.transpose(ph[:, t * P:(t + 1) * P], hn[:, t, :], M["identF"][:])
                last.then_inc(h_flipped, 1)

        @block.scalar
        def _(act):
            act.sem_inc(ht_kept, 1)
            with act.Fori(0, B) as b:
                act.wait_ge(projected, b * 4 + 1)
                act.activation(k[:], pw[1][:], ACT.Copy).then_inc(evacuated, 1)
                act.wait_ge(projected, b * 4 + 3)
                act.activation(beta[:], pw[3][:], ACT.Sigmoid, bias=M["bbeta"][:, 0:1]).then_inc(evacuated, 1)
                act.wait_ge(h_flipped, b + 1)
                act.activation(M["HT"][:, b, :], ph[:], ACT.Copy, scale=M["norm"][:, 0:1]).then_inc(ht_kept, 1)

        @block.gpsimd
        def _(pool):
            pool.sem_inc(x_stored, 1)
            with pool.Fori(0, B) as b:
                bo = M["bo"][:].unsqueeze(1).broadcast_to([P, NT, P])
                pool.wait_ge(y_made, b + 1)
                apart(pool, M["passed"])
                pool.tensor_tensor(xb[:], M["X"][:, b], bo, ALU.add).then_inc(xb_ready, 1)
                for n in range(SETS):
                    rms = n == SETS - 1
                    if rms:
                        pool.wait_ge(x_ready, b + 1)
                        apart(pool, M["passed"])
                        pool.tensor_copy(M["X"][:, b], xn[:]).then_inc(x_stored, 1)
                    make_rstd(pool, Chain(pool, chain_p, b * SETS + n), rstd[:], ms[:] if rms else mv[:, :, 1],
                              tmp[:], M["minus_half"][:, 0:NT], 1.0 / P if rms else 1.0,
                              RMS_EPS if rms else LN_EPS, stats_ready, rstd_ready, b * SETS + n, M["passed"])

        @block.vector
        def _(dve):
            dve.sem_inc(y_made, 1)
            PER = 9
            with dve.Fori(0, B) as b:
                ch = Chain(dve, chain_d, b * PER)
                dve.wait_ge(evacuated, b * 2 + 1)
                dve.wait_ge(projected, b * 4 + 2)
                ch.do(dve.tensor_tensor(kv[:], k[:], pw[2][:], ALU.mult))
                dve.wait_ge(evacuated, b * 2 + 2)
                ch.do(dve.tensor_tensor_scan(state[:], beta[:], kv[:], 0.0, ALU.mult, ALU.add))
                dve.wait_ge(projected, b * 4 + 4)
                dve.tensor_tensor(o[:], state[:], pw[0][:], ALU.mult).then_inc(o_ready, 1)
                dve.wait_ge(out_ready, b + 1)
                dve.wait_ge(xb_ready, b + 1)
                dve.tensor_tensor(y[:], pout[:].rearrange("p (t d) -> p t d", d=P), xb[:], ALU.add).then_inc(y_made, 1)
                dve.wait_ge(y_made, b + 2)
                ch.do(normalise(dve, ch, z, y, stats, mv, rstd, NT, stats_ready, rstd_ready, b * SETS, M["passed"]))
                wide = lambda m: m[:].unsqueeze(1).broadcast_to([P, NT, P])
                ch.do(dve.tensor_tensor(z[:], z[:], wide(M["lng"]), ALU.mult))
                ch.do(dve.tensor_tensor(z[:], z[:], wide(M["lnb"]), ALU.add))
                ch.do(dve.tensor_tensor(z[:], z[:], M["X"][:, b], ALU.add))
                dve.wait_ge(x_stored, b + 1)
                dve.wait_ge(ht_kept, b + 1)
                normalise(dve, ch, xn, z, stats, mv, rstd, NT, stats_ready, rstd_ready, b * SETS + 1, M["passed"]).then_inc(x_ready, 1)
                dve.wait_ge(x_ready, b + 1)
                rms_normalise(dve, ch, hn, xn, z[:], ms[:], rstd, NT, stats_ready, rstd_ready,
                              b * SETS + 2).then_inc(h_ready, 1)
                assert ch.k == PER, ch.k


def build(nc, A, out):
    TT = B * NT
    with ExitStack() as ctx:
        shapes = dict(
            X=[P, B, NT, P], OT=[P, NU, T], HT=[P, B, T],
            w0a=[P, 3, P], wop0=[P, UPB, P], w1d=[P, 5, P], w1a=[P, 3, P], wop1=[P, UPB, P],
            identF=[P, P], pick_sum=[P, P], bo=[P, P], lng=[P, P], lnb=[P, P], norm=[P, 2], bbeta=[P, 1],
            rw=[P, 2, E], rb=[P, E], before=[P, E, E], minus_half=[P, NT], cols=[P, 2 * E + E * BANKS], gates=[P, TT, E], gate_sum=[P, TT])
        M = {k: ctx.enter_context(nc.sbuf_tensor(k, v, F32)) for k, v in shapes.items()}
        for k, n in (("identB", P), ("row0", T), ("first", 3 * P), ("band", 3 * P)):
            M[k] = ctx.enter_context(nc.sbuf_tensor(k, [P, n], BF16))
        M["XT"] = M["OT"][:, 0:B, :]
        M["v9"] = nc.dram_tensor("v9", [NU, P, NT, G, HD + 1], F32, kind="Internal").ap()
        M["parts"] = nc.dram_tensor("parts", [2, B, UPB, PARTS, 32, T], BF16, kind="Internal").ap()
        M["passed"] = nc.alloc_semaphore("passed")
        M["semaphores"] = []
        setup(nc, A, M)
        read_x(nc, A, M)
        for layer, src, w, wop, segments in ((0, "XT", "w0a", "wop0", BANDED), (1, "HT", "w1a", "wop1", FULL)):
            if layer == 1:
                scan_layer(nc, M, "scan")
            project_qkv(nc, M, f"qkv{layer}", M[src], M[w])
            attend(nc, M, f"att{layer}", segments)
            project_out(nc, M, f"out{layer}", M[wop], layer == 1)
            route(nc, M, f"route{layer}", M["XT"] if layer == 0 else M["HT"], layer)
            experts(nc, A, M, f"moe{layer}", layer, out)
            if layer == 0:
                clear_semaphores(nc, M)


_INS = ['L0_attn_x', 'L0_attn_Wq', 'L0_attn_Wk', 'L0_attn_Wv', 'L0_attn_Wo', 'L0_ffn_router_W', 'L0_ffn_router_b',
        'L0_ffn_ln_g', 'L0_ffn_ln_b', 'L0_ffn_W1', 'L0_ffn_b1', 'L0_ffn_W2', 'L0_ffn_b2', 'L1_attn_Wq',
        'L1_attn_Wk', 'L1_attn_Wv', 'L1_attn_Wbeta', 'L1_attn_b_beta', 'L1_attn_Wo', 'L1_attn_b_o',
        'L1_attn_ln_g', 'L1_attn_ln_b', 'L1_ffn_norm1_w', 'L1_ffn_norm2_w', 'L1_ffn_wq', 'L1_ffn_wk',
        'L1_ffn_wv', 'L1_ffn_wo', 'L1_ffn_router_w', 'L1_ffn_sh_gate', 'L1_ffn_sh_up', 'L1_ffn_sh_down',
        'L1_ffn_e_gate', 'L1_ffn_e_up', 'L1_ffn_e_down']


def kernel(**inputs):
    import numpy as _np
    import concourse.bacc as _bacc
    from concourse import mybir as _mybir
    from concourse.bass_utils import run_bass_kernel_spmd as _run

    nc = _bacc.Bacc("TRN2", target_bir_lowering=False, num_devices=1)
    arrays, args = {}, {}
    for name in _INS:
        a = _np.ascontiguousarray(inputs[name])
        arrays[f"in_{name}"] = a
        args[name] = nc.dram_tensor(f"in_{name}", a.shape, _mybir.dt.from_np(a.dtype), kind="ExternalInput").ap()
    out = nc.dram_tensor("out_0", (B, T, P), _mybir.dt.float32, kind="ExternalOutput").ap()
    build(nc, args, out)
    r = _run(nc, [arrays], core_ids=[0])
    return r.results[0]["out_0"]
```

```python
from contextlib import ExitStack

import concourse.bass as bass
from concourse import mybir

F32 = mybir.dt.float32
BF16 = mybir.dt.bfloat16
ALU = mybir.AluOpType
ACT = mybir.ActivationFunctionType
AX = mybir.AxisListType

P = 128
B, T = 4, 1024
NT = T // P
H, HD = 16, 8
G = 4
UPB = H // G
NU = B * UPB
HALF = 512
CH = B * T // HALF
CT = HALF // P
E = 8
BANKS = 4
PARTS = 3
KROWS = PARTS * PARTS * HD
KMAX = 96
SCALE = float(HD) ** -0.5
MASKED = -1.0e30
LN_EPS = 1e-05
RMS_EPS = 1e-06

FULL = [[(0, 0, HALF, ()), (HALF, HALF, HALF, ())] for _ in range(NT)]


def banded_segments():
    out = [[(0, 0, HALF, ((P, HALF - P, "row0", P),)), (HALF, HALF, HALF, ((0, HALF, "row0", HALF),))],
           [(0, 0, 3 * P, ((0, P, "first", 0), (2 * P, P, "first", 2 * P)))]]
    for r in range(2, NT):
        n = (min(r + 2, NT) - (r - 1)) * P
        masks = ((0, P, "band", 0), (2 * P, P, "band", 2 * P))
        out.append([(0, (r - 1) * P, n, masks[:n // P - 1]), (n, 0, 1, ())])
    return out


BANDED = banded_segments()


class Chain:

    def __init__(self, engine, semaphore, base=0):
        self.engine, self.semaphore, self.base, self.k = engine, semaphore, base, 0

    def mark(self, instruction):
        self.k += 1
        instruction.then_inc(self.semaphore, 1)

    def settle(self):
        self.engine.wait_ge(self.semaphore, self.base + self.k)

    def do(self, instruction):
        self.mark(instruction)
        self.settle()


def apart(engine, passed):
    engine.sem_inc(passed, 1)


def new_semaphore(nc, M, name):
    handle = nc.alloc_semaphore(name)
    M["semaphores"].append(handle)
    return handle


def clear_semaphores(nc, M):
    nc.clear_and_free_semaphores(M["semaphores"])
    nc.all_engine_barrier()
    M["semaphores"] = []


def bc_free(ap, n):
    return ap.unsqueeze(len(ap.shape)).broadcast_to(list(ap.shape) + [n])


def normalise(dve, chain, dst, src, stats, mv, rstd, tiles, stats_ready, rstd_ready, occasion, passed):
    for t in range(tiles):
        last = dve.bn_stats(stats[:, t, :], src[:, t, :])
    chain.do(last)
    apart(dve, passed)
    for t in range(tiles):
        last = dve.bn_aggr(mv[:, t, :], stats[:, t, :])
    last.then_inc(stats_ready, 1)
    dve.wait_ge(rstd_ready, occasion + 1)
    for t in range(tiles):
        last = dve.tensor_scalar(dst[:, t, :], src[:, t, :], mv[:, t, 0:1], rstd[:, t:t + 1],
                                 ALU.subtract, ALU.mult)
    return last


def rms_normalise(dve, chain, dst, src, square, ms, rstd, tiles, stats_ready, rstd_ready, occasion):
    chain.do(dve.tensor_tensor(square, src[:], src[:], ALU.mult))
    dve.tensor_reduce(ms, square, AX.X, ALU.add).then_inc(stats_ready, 1)
    dve.wait_ge(rstd_ready, occasion + 1)
    for t in range(tiles):
        last = dve.tensor_scalar(dst[:, t, :], src[:, t, :], rstd[:, t:t + 1], None, ALU.mult)
    return last


def make_rstd(pool, chain, rstd, src, tmp, minus_half, scale, eps, stats_ready, rstd_ready, occasion, passed):
    pool.wait_ge(stats_ready, occasion + 1)
    apart(pool, passed)
    chain.do(pool.tensor_scalar(tmp, src, scale, eps, ALU.mult, ALU.add))
    pool.tensor_tensor(rstd, tmp, minus_half, ALU.pow).then_inc(rstd_ready, 1)


def setup(nc, A, M):
    with ExitStack() as ctx:
        sem = lambda name: new_semaphore(nc, M, "su_" + name)
        sb = lambda name, shape, dt=F32: ctx.enter_context(nc.sbuf_tensor("su_" + name, shape, dt))
        pt = ctx.enter_context(nc.psum_tensor("su_pt", [P, 8, HALF], F32))
        flip = sb("flip", [P, 5, P])
        wo_nat = sb("wo_nat", [P, P])
        wo_sp = sb("wo_sp", [P, UPB, G, 32])
        qvT = sb("qvT", [P, 2, P])
        group = sb("group", [P, P])
        wbeta = sb("wbeta", [P, H])
        rows = sb("rows", [P, P])
        weights_in, consts, masks, placed = sem("weights_in"), sem("consts"), sem("masks"), sem("placed")
        spread, flipped, kept, folded = sem("spread"), sem("flipped"), sem("kept"), sem("folded")
        pool_chain = sem("pool_chain")
        block = ctx.enter_context(nc.Block())
        NB1 = E * (A["L0_ffn_b1"].shape[1] // P)
        loads = [(flip[:, n, :], A[k][:, :]) for n, k in enumerate(
            ["L0_attn_Wq", "L0_attn_Wk", "L0_attn_Wv", "L1_attn_Wq", "L1_attn_Wv"])]
        loads += [(wo_nat[:], A["L0_attn_Wo"]), (wbeta[:], A["L1_attn_Wbeta"])]
        loads += [(M["w1d"][:, 1, :], A["L1_attn_Wk"]), (M["w1d"][:, 4, :], A["L1_attn_Wo"])]
        loads += [(M["w1a"][:, n, :], A[k]) for n, k in enumerate(["L1_ffn_wq", "L1_ffn_wk", "L1_ffn_wv"])]
        row = lambda k: A[k].unsqueeze(0).broadcast_to([P, P])
        loads += [(M["bo"][:], row("L1_attn_b_o")), (M["lng"][:], row("L1_attn_ln_g")),
                  (M["lnb"][:], row("L1_attn_ln_b"))]
        loads += [(M["norm"][:, 0:1], A["L1_ffn_norm1_w"].unsqueeze(1)),
                  (M["norm"][:, 1:2], A["L1_ffn_norm2_w"].unsqueeze(1))]
        loads += [(M["rw"][:, 0, :], A["L0_ffn_router_W"]), (M["rw"][:, 1, :], A["L1_ffn_router_w"]),
                  (M["rb"][:], A["L0_ffn_router_b"].unsqueeze(0).broadcast_to([P, E]))]
        bb = A["L1_attn_b_beta"].unsqueeze(1).broadcast_to([H, HD])
        NLOAD = len(loads) + 1

        @block.sync
        def _(sp):
            for dst, src in loads:
                sp.dma_start(dst, src).then_inc(weights_in, 16)
            sp.dma_start(M["bbeta"][:], bb).then_inc(weights_in, 16)
            sp.wait_ge(consts, 3)
            sp.dma_start(rows[0:E, :], A["L0_ffn_ln_g"]).then_inc(placed, 16)
            sp.dma_start(rows[E:2 * E, :], A["L0_ffn_ln_b"]).then_inc(placed, 16)
            sp.dma_start(rows[2 * E:2 * E + NB1, :],
                         A["L0_ffn_b1"].rearrange("e (f p) -> (e f) p", p=P)).then_inc(placed, 16)
            wo = A["L1_ffn_wo"].rearrange("(g j d) n -> j d g n", j=G, d=HD)
            for j in range(G):
                sp.dma_start(M["wop1"][32 * j:32 * j + HD, :, :], wo[j]).then_inc(placed, 16)
            sp.wait_ge(placed, 16 * (G + 3))

        @block.gpsimd
        def _(pool):
            ch = Chain(pool, pool_chain)
            pool.memset(M["wop1"][:], 0.0).then_inc(consts, 1)
            pool.memset(wo_sp[:], 0.0).then_inc(consts, 1)
            pool.memset(rows[:], 0.0).then_inc(consts, 1)
            pool.memset(M["minus_half"][:], -0.5).then_inc(consts, 1)
            for t in (M["identF"], M["identB"], M["row0"], M["first"], M["band"], M["before"]):
                ch.mark(pool.memset(t[:], 0.0))
            ch.mark(pool.memset(group[:], 1.0))
            ch.settle()
            for t in (M["identF"], M["identB"]):
                ch.mark(pool.affine_select(out=t[:], in_=t[:], compare_op=ALU.not_equal, fill=1.0, base=0,
                                           pattern=[[-1, P]], channel_multiplier=1))
            bf = M["before"][:]
            ch.mark(pool.affine_select(out=bf, in_=bf, compare_op=ALU.is_ge, fill=1.0, base=0,
                                       pattern=[[-1, E], [1, E]], channel_multiplier=0))
            g3 = group[:].rearrange("p (h d) -> p h d", d=HD)
            ch.do(pool.affine_select(out=g3, in_=g3, compare_op=ALU.is_ge, fill=0.0, base=0,
                                     pattern=[[-HD, H], [0, HD]], channel_multiplier=1))
            ch.do(pool.affine_select(out=g3, in_=g3, compare_op=ALU.is_ge, fill=0.0, base=HD - 1,
                                     pattern=[[HD, H], [0, HD]], channel_multiplier=-1))
            low = lambda ap: pool.affine_select(out=ap, in_=ap, compare_op=ALU.is_ge, fill=MASKED, base=0,
                                                pattern=[[1, P]], channel_multiplier=-1)
            high = lambda ap: pool.affine_select(out=ap, in_=ap, compare_op=ALU.is_ge, fill=MASKED, base=0,
                                                 pattern=[[-1, P]], channel_multiplier=1)
            ch.mark(low(M["band"][:, 0:P]))
            ch.mark(high(M["band"][:, 2 * P:3 * P]))
            ch.mark(low(M["first"][:, 0:P]))
            ch.mark(high(M["first"][:, 2 * P:3 * P]))
            ch.mark(high(M["row0"][:, P:2 * P]))
            ch.mark(pool.memset(M["row0"][:, 2 * P:], MASKED))
            ch.settle()
            pool.memset(M["first"][:, 0:1], 0.0).then_inc(masks, 1)
            pool.memset(M["row0"][0:1, :], 0.0).then_inc(masks, 1)

        @block.vector
        def _(dve):
            dve.wait_ge(weights_in, 16 * NLOAD)
            dve.wait_ge(consts, 3)
            dve.tensor_copy(wo_sp[:, :, :, 0:HD],
                            wo_nat[:].rearrange("p (g j d) -> p g j d", g=UPB, j=G)).then_inc(spread, 1)
            dve.tensor_copy(M["w1d"][:, 3, :].rearrange("p (h d) -> p h d", d=HD),
                            bc_free(wbeta[:], HD)).then_inc(spread, 1)
            dve.wait_ge(flipped, 1)
            dve.tensor_copy(M["w0a"][:], pt[:, 0, 0:3 * P].rearrange("p (n c) -> p n c", c=P)).then_inc(kept, 1)
            dve.tensor_copy(qvT[:], pt[:, 1, 0:2 * P].rearrange("p (n c) -> p n c", c=P)).then_inc(kept, 1)
            dve.tensor_copy(M["wop0"][:], pt[:, 2, :].rearrange("p (n c) -> p n c", c=P)).then_inc(kept, 1)
            dve.wait_ge(folded, 1)
            dve.tensor_copy(M["w1d"][:, 0, :], pt[:, 3, 0:P]).then_inc(kept, 1)
            dve.tensor_copy(M["w1d"][:, 2, :], pt[:, 3, P:2 * P]).then_inc(kept, 1)
            dve.tensor_copy(M["cols"][:], pt[:, 3, 2 * P:2 * P + 2 * E + NB1]).then_inc(kept, 1)

        @block.tensor
        def _(pe):
            pe.wait_ge(weights_in, 16 * NLOAD)
            pe.wait_ge(pool_chain, 12)
            pe.wait_ge(spread, 2)
            for n in range(3):
                pe.transpose(pt[:, 0, n * P:(n + 1) * P], flip[:, n, :], M["identF"][:])
            for n in range(2):
                pe.transpose(pt[:, 1, n * P:(n + 1) * P], flip[:, 3 + n, :], M["identF"][:])
            for g in range(UPB):
                last = pe.transpose(pt[:, 2, g * P:(g + 1) * P], wo_sp[:, g].rearrange("p j c -> p (j c)"),
                                    M["identF"][:])
            last.then_inc(flipped, 1)
            pe.wait_ge(kept, 3)
            pe.wait_ge(placed, 16 * (G + 3))
            pe.transpose(pt[:, 3, 2 * P:3 * P], rows[:], M["identF"][:])
            for n in range(2):
                last = pe.matmul(pt[:, 3, n * P:(n + 1) * P], qvT[:, n, :], group[:], start=True, stop=True)
            last.then_inc(folded, 1)


def read_x(nc, A, M):
    with ExitStack() as ctx:
        sem = lambda name: new_semaphore(nc, M, "rx_" + name)
        xb = ctx.enter_context(nc.sbuf_tensor("rx_xb", [P, NT, P], F32))
        pt = ctx.enter_context(nc.psum_tensor("rx_pt", [P, NT, P], F32))
        x_in, taken, flipped, freed = sem("x_in"), sem("taken"), sem("flipped"), sem("freed")
        block = ctx.enter_context(nc.Block())
        x = A["L0_attn_x"].rearrange("b (t p) d -> b p t d", p=P)

        @block.sync
        def _(sp):
            sp.dma_start(xb[:], x[0]).then_inc(x_in, 16)
            with sp.Fori(1, B) as b:
                sp.wait_ge(taken, b)
                sp.wait_ge(flipped, b)
                apart(sp, M["passed"])
                sp.dma_start(xb[:], x[b]).then_inc(x_in, 16)

        @block.vector
        def _(dve):
            with dve.Fori(0, B) as b:
                dve.wait_ge(x_in, 16 * b + 16)
                dve.tensor_copy(M["X"][:, b], xb[:]).then_inc(taken, 1)

        @block.tensor
        def _(pe):
            with pe.Fori(0, B) as b:
                pe.wait_ge(x_in, 16 * b + 16)
                pe.wait_ge(freed, b + 1)
                for t in range(NT):
                    last = pe.transpose(pt[:, t, :], xb[:, t, :], M["identF"][:])
                last.then_inc(flipped, 1)

        @block.scalar
        def _(act):
            act.sem_inc(freed, 1)
            with act.Fori(0, B) as b:
                act.wait_ge(flipped, b + 1)
                act.activation(M["XT"][:, b, :], pt[:].rearrange("p t c -> p (t c)"), ACT.Copy).then_inc(freed, 1)


def project_qkv(nc, M, name, src, w):
    with ExitStack() as ctx:
        sem = lambda n: new_semaphore(nc, M, f"{name}_{n}")
        sb = lambda n, shape, dt=F32: ctx.enter_context(nc.sbuf_tensor(f"{name}_{n}", shape, dt))
        ps = lambda n: ctx.enter_context(nc.psum_tensor(f"{name}_{n}", [P, T], F32))
        prod = [ps("pq"), ps("pk")]
        pv, pvt = ps("pv"), ps("pvt")
        parts = [sb("qparts", [P, PARTS, T], BF16), sb("kparts", [P, PARTS, T], BF16)]
        rest = [sb("qrest", [P, T]), sb("krest", [P, T])]
        vT = sb("vT", [P, T])
        v9 = sb("v9", [P, UPB, NT, G, HD + 1])
        projected, first, second, third = sem("projected"), sem("first"), sem("second"), sem("third")
        rest1, rest_done = sem("rest1"), sem("rest_done")
        v_ready, v_kept, v_flipped, v_stored, parts_out = (sem("v_ready"), sem("v_kept"), sem("v_flipped"),
                                                           sem("v_stored"), sem("parts_out"))
        v_out = sem("v_out")
        block = ctx.enter_context(nc.Block())

        @block.gpsimd
        def _(pool):
            pool.memset(v9[:], 1.0).then_inc(v_out, 16)

        @block.tensor
        def _(pe):
            with pe.Fori(0, B) as b:
                for n in range(2):
                    pe.wait_ge(rest1, 2 * b + n + 1)
                    for half in range(2):
                        c = slice(half * HALF, (half + 1) * HALF)
                        last = pe.matmul(prod[n][:, c], w[:, n, :], src[:, b, c], start=True, stop=True)
                    last.then_inc(projected, 1)
                pe.wait_ge(v_kept, b + 1)
                for half in range(2):
                    c = slice(half * HALF, (half + 1) * HALF)
                    last = pe.matmul(pv[:, c], w[:, 2, :], src[:, b, c], start=True, stop=True)
                last.then_inc(v_ready, 1)
                pe.wait_ge(v_kept, b + 2)
                pe.wait_ge(v_stored, b + 1)
                for t in range(NT):
                    c = slice(t * P, (t + 1) * P)
                    last = pe.transpose(pvt[:, c], vT[:, c], M["identF"][:])
                last.then_inc(v_flipped, 1)

        @block.scalar
        def _(act):
            act.sem_inc(v_kept, 1)
            with act.Fori(0, B) as b:
                for n in range(2):
                    act.wait_ge(projected, 2 * b + n + 1)
                    act.wait_ge(parts_out, 32 * UPB * b + 1)
                    act.activation(parts[n][:, 0, :], prod[n][:], ACT.Copy).then_inc(first, 1)
                act.wait_ge(v_ready, b + 1)
                act.wait_ge(v_flipped, b + 1)
                act.activation(vT[:], pv[:], ACT.Copy).then_inc(v_kept, 1)
                for n in range(2):
                    act.wait_ge(rest1, 2 * b + n + 3)
                    act.activation(parts[n][:, 1, :], rest[n][:], ACT.Copy).then_inc(second, 1)

        @block.vector
        def _(dve):
            dve.sem_inc(rest1, 2)
            dve.sem_inc(v_stored, 1)
            dve.sem_inc(third, 1)
            with dve.Fori(0, B) as b:
                for n in range(2):
                    dve.wait_ge(first, 2 * b + n + 1)
                    if n == 0:
                        dve.wait_ge(third, 2 * b + 1)
                    dve.tensor_tensor(rest[n][:], prod[n][:], parts[n][:, 0, :], ALU.subtract).then_inc(rest1, 1)
                for n in range(2):
                    dve.wait_ge(second, 2 * b + n + 1)
                    dve.tensor_tensor(parts[n][:, 2, :], rest[n][:], parts[n][:, 1, :],
                                      ALU.subtract).then_inc(third, 1)
                dve.wait_ge(v_flipped, b + 2)
                dve.wait_ge(v_out, b * 16 + 16)
                v = pvt[:].rearrange("p (t g j d) -> p g t j d", t=NT, g=UPB, j=G)
                for g in range(UPB):
                    last = dve.tensor_copy(v9[:, g, :, :, 0:HD], v[:, g])
                last.then_inc(v_stored, 1)

        @block.sync
        def _(sp):
            sp.sem_inc(parts_out, 1)
            sp.sem_inc(v_flipped, 1)
            with sp.Fori(0, B) as b:
                for n in range(2):
                    sp.wait_ge(third, 2 * b + n + 2)
                    apart(sp, M["passed"])
                    for g in range(UPB):
                        rows = slice(32 * g, 32 * g + 32)
                        sp.dma_start(M["parts"][n, b, g].rearrange("i r t -> r i t"),
                                     parts[n][rows, :, :]).then_inc(parts_out, 16)
                sp.wait_ge(v_stored, b + 2)
                apart(sp, M["passed"])
                sp.dma_start(M["v9"].rearrange("(b g) p t j d -> b p g (t j d)", g=UPB)[b],
                             v9[:].rearrange("p g t j d -> p g (t j d)")).then_inc(v_out, 16)
            sp.wait_ge(parts_out, 32 * UPB * B + 1)
            sp.wait_ge(v_out, 16 * B + 16)


def attend(nc, M, name, segments):
    with ExitStack() as ctx:
        sem = lambda n: new_semaphore(nc, M, f"{name}_{n}")
        sb = lambda n, shape, dt=F32: ctx.enter_context(nc.sbuf_tensor(f"{name}_{n}", shape, dt))
        NBUF = 3
        Q = [sb(f"q{i}", [KMAX, G, T], BF16) for i in range(NBUF)]
        K = [sb(f"k{i}", [KMAX, G, T], BF16) for i in range(NBUF)]
        vu = [sb(f"vu{i}", [P, NT, G, HD + 1]) for i in range(NBUF)]
        negmax = [sb(f"negmax{i}", [P, P]) for i in range(NBUF)]
        mparts = sb("mparts", [32, PARTS, P], BF16)
        mrest = sb("mrest", [32, P])
        zero3 = sb("zero3", [PARTS, T], BF16)
        prob = sb("prob", [P, 2, G, T])
        warm = sb("warm", [P, 2])
        sums, minus_one, recip = sb("sums", [P, 32]), sb("minus_one", [P, 32]), sb("recip", [P, T])
        one = [ctx.enter_context(nc.psum_tensor(f"{name}_one{i}", [P, T], F32)) for i in range(2)]
        st = ctx.enter_context(nc.psum_tensor(f"{name}_st", [P, 2, HALF], F32))
        o = ctx.enter_context(nc.psum_tensor(f"{name}_o", [P, T], F32))
        qk_in = [sem(f"qk_in{i}") for i in range(NBUF)]
        clean, clean_pool = sem("clean"), sem("clean_pool")
        one_ready, one_free = sem("one_ready"), sem("one_free")
        max_split, max_in, split_chain = sem("max_split"), sem("max_in"), sem("split_chain")
        st_ready, prob_ready, prob_free = sem("st_ready"), sem("prob_ready"), sem("prob_free")
        v_in = [sem(f"v_in{i}") for i in range(NBUF)]
        o_kept, o_done, sums_in, inverted = sem("o_kept"), sem("o_done"), sem("sums_in"), sem("inverted")
        o_half = sem("o_half")
        rsum_out, recip_in = sem("rsum_out"), sem("recip_in")
        block = ctx.enter_context(nc.Block())

        qparts = M["parts"][0].rearrange("b g i (h d) t -> (b g) i d h t", d=HD)
        kparts = M["parts"][1].rearrange("b g i (h d) t -> (b g) i d h t", d=HD)
        QK_LOADS = 16 * (2 * PARTS * PARTS + 1)
        ITEMS = G * NT
        ONE = ITEMS + 2
        wide = [len([s for s in row if s[2] > 1]) for row in segments]
        halved = all(w == 2 for w in wide)
        LOOPS = NU // NBUF - 1
        STEPS = G * sum(wide)

        def width(r):
            return sum(s[2] for s in segments[r])

        def pieces(r):
            if wide[r] == 2:
                return [(s[0], s[2], [s]) for s in segments[r]]
            return [(0, width(r), segments[r])]

        def scores(pe, dst, left, right, j, r, segs, at):
            for c0, t0, n, masks in segs:
                c = c0 - at
                last = pe.matmul(dst[:, c:c + n], left[:, j, r * P:(r + 1) * P], right[:, j, t0:t0 + n],
                                 start=True, stop=not masks, skip_group_check=True)
                for m, (first, cols, mask, m0) in enumerate(masks):
                    last = pe.matmul(dst[:, c + first:c + first + cols], M["identB"][:], M[mask][:, m0:m0 + cols],
                                     start=False, stop=m == len(masks) - 1, skip_group_check=True)
            return last

        def stage1(pe, buf, k, n, parity, half=None):
            j, r = divmod(k, NT)
            if half != 1:
                pe.wait_ge(one_free, n + 1)
            segs = segments[r] if half is None else segments[r][half:half + 1]
            last = scores(pe, one[parity], Q[buf], K[buf], j, r, segs, 0)
            if half != 0:
                last.then_inc(one_ready, 1)

        def flip_max(pe, buf, n, parity):
            pe.wait_ge(one_free, n + 2)
            pe.transpose(one[parity][:, 0:P], negmax[buf][:], M["identF"][:]).then_inc(one_ready, 2)

        def values(pe, buf, r, part):
            runs = []
            for c0, t0, n, _ in segments[r]:
                cut = min(max(HALF - t0, 0), n)
                if cut:
                    runs.append((c0, t0, cut))
                if n - cut:
                    runs.append((c0 + cut, t0 + cut, n - cut))
            for c0, t0, n in (runs[:1], runs[1:])[part]:
                for j in range(G):
                    last = pe.matmul(o[32 * j:32 * j + HD + 1, t0:t0 + n], vu[buf][:, r, j, :],
                                     prob[:, r % 2, j, c0:c0 + n], start=r == 0, stop=r == NT - 1,
                                     skip_group_check=True)
            if part == (1 if len(runs) > 1 else 0):
                last.then_inc(prob_free, 1)
            elif r == NT - 1:
                last.then_inc(o_half, 1)

        AHEAD = (3 if halved else 5)
        FLIP = ITEMS - AHEAD - 1
        EXTRA = lambda item: item >= 8
        loaded = lambda i, m: i + m // NBUF + 1

        def pe_unit(pe, i, m):
            u = NBUF * i + m
            left = NU - 1 - u if isinstance(u, int) else 2
            buf = m % NBUF
            base = ONE * u + ONE
            issued = 2 * AHEAD

            def issue(upto):
                nonlocal issued
                while issued < upto:
                    nxt = 1 if issued < 2 * ITEMS else 2
                    k = issued // 2 if nxt == 1 else issued // 2 - ITEMS
                    if nxt <= left:
                        stage1(pe, (buf + nxt) % NBUF, k, base + (nxt - 1) * ONE + k, k % 2,
                               issued % 2 if halved else None)
                    issued += 1 if halved else 2

            pe.wait_ge(max_in, 16 * PARTS * u + 16 * PARTS)
            step = 0
            for item in range(ITEMS):
                r, j = divmod(item, G)
                due = min(AHEAD + item + 1 + EXTRA(item), ITEMS) if item <= FLIP else AHEAD + 1 + item
                limit = 2 * ITEMS if item <= FLIP else 2 * ITEMS + 2 * AHEAD
                for n_piece, (c0, n, segs) in enumerate(pieces(r)):
                    pe.wait_ge(prob_ready, STEPS * u + step + 1)
                    last = scores(pe, st[:, step % 2, :], K[buf], Q[buf], j, r, segs, c0)
                    last.then_inc(st_ready, 1)
                    step += 1
                    if halved:
                        issue(min(2 * due + ((-1, 1), (0, 0))[j % 2][n_piece], limit))
                    elif n_piece == 0:
                        issue(min(2 * due, limit))
                if item == FLIP:
                    if left:
                        flip_max(pe, (buf + 1) % NBUF, base + ITEMS, 0)
                    if left > 1:
                        pe.wait_ge(qk_in[(buf + 2) % NBUF], QK_LOADS * loaded(i, m + 2))
                if j % 2 == 1 and r == 0 and m:
                    if j == 1:
                        pe.wait_ge(prob_ready, STEPS * u + 2)
                    values(pe, (buf - 1) % NBUF, NT - 1, j // 2)
                if j % 2 == 1 and r >= 1:
                    if r == 1 and j == 1:
                        pe.wait_ge(o_kept, 2 * u + 2)
                        pe.wait_ge(v_in[buf], 16 * loaded(i, m))
                    if j == 1:
                        pe.wait_ge(prob_ready, STEPS * u + G * sum(wide[:r]) + 2)
                    values(pe, buf, r - 1, j // 2)

        @block.tensor
        def _(pe):
            pe.wait_ge(qk_in[0], QK_LOADS)
            pe.wait_ge(clean, 1 + NBUF)
            for k in range(ITEMS):
                stage1(pe, 0, k, k, k % 2)
            flip_max(pe, 0, ITEMS, 0)
            pe.wait_ge(qk_in[1], QK_LOADS)
            for k in range(AHEAD):
                stage1(pe, 1, k, ONE + k, k % 2)
            pe_unit(pe, 0, 0)
            with pe.Fori(0, LOOPS) as i:
                for m in range(1, 1 + NBUF):
                    pe_unit(pe, i, m)
            for m in range(1, 1 + NBUF):
                pe_unit(pe, LOOPS, m)
            pe.wait_ge(prob_ready, STEPS * NU + 2)
            for part in range(2):
                values(pe, (NU - 1) % NBUF, NT - 1, part)

        @block.scalar
        def _(act):
            act.activation(warm[:], M["norm"][:], ACT.Exp)
            act.sem_inc(prob_ready, 2)
            act.sem_inc(o_kept, 2)

            def exponentials(u, item):
                r, j = divmod(item, G)
                step = G * sum(wide[:r]) + j * wide[r]
                if j == 0:
                    act.wait_ge(prob_free, u * NT + r + 1)
                for c0, n, _ in pieces(r):
                    act.wait_ge(st_ready, u * STEPS + step + 1)
                    act.activation(prob[:, r % 2, j, c0:c0 + n], st[:, step % 2, 0:n], ACT.Exp,
                                   scale=SCALE).then_inc(prob_ready, 1)
                    step += 1

            def keep(u, n):
                if n == 0:
                    act.wait_ge(o_half, u + 1)
                else:
                    act.wait_ge(prob_free, u * NT + NT + 2)
                c = slice(0, HALF) if halved == (n == 0) else slice(HALF, T)
                act.activation(M["OT"][:, u, c], o[:, c], ACT.Copy).then_inc(o_kept, 1)

            START = G + 1
            for item in range(START):
                exponentials(0, item)
            with act.Fori(0, NU - 1) as u:
                for item in range(START, ITEMS):
                    exponentials(u, item)
                for item in range(START):
                    exponentials(u + 1, item)
                    if item == START - 3:
                        keep(u, 0)
                keep(u, 1)
            for item in range(START, ITEMS):
                exponentials(NU - 1, item)
            for n in range(2):
                keep(NU - 1, n)

        @block.vector
        def _(dve):
            dve.memset(o[:], 0.0).then_inc(clean, 1)
            for t in negmax:
                dve.memset(t[:], 0.0).then_inc(clean, 1)
            dve.sem_inc(one_free, 2)
            dve.wait_ge(clean, 1 + NBUF)

            def maxima(buf, n0):
                for k in range(ITEMS):
                    j, r = divmod(k, NT)
                    dve.wait_ge(one_ready, n0 + k + 1)
                    dve.tensor_reduce(negmax[buf][:, k:k + 1], one[k % 2][:, 0:width(r)], AX.X,
                                      ALU.max, negate=True).then_inc(one_free, 1)

            def split_max(v, n):
                chain = Chain(dve, split_chain, v * 3)
                dve.wait_ge(one_ready, n + 2)
                m = one[0][0:32, 0:P]
                chain.do(dve.tensor_copy(mparts[:, 0, :], m))
                chain.do(dve.tensor_tensor(mrest[:], m, mparts[:, 0, :], ALU.subtract))
                dve.sem_inc(one_free, 2)
                chain.do(dve.tensor_copy(mparts[:, 1, :], mrest[:]))
                dve.tensor_tensor(mparts[:, 2, :], mrest[:], mparts[:, 1, :], ALU.subtract).then_inc(max_split, 1)

            maxima(0, 0)
            split_max(0, ITEMS)
            with dve.Fori(0, NU // NBUF) as i:
                for s in range(NBUF):
                    u = i * NBUF + s
                    maxima((s + 1) % NBUF, u * ONE + ONE)
                    dve.wait_ge(max_in, u * 16 * PARTS + 16 * PARTS)
                    split_max(u + 1, u * ONE + ONE + ITEMS)

        @block.gpsimd
        def _(pool):
            for t in Q:
                pool.memset(t[64:96], 0.0).then_inc(clean_pool, 1)
            for t in K:
                pool.memset(t[64:96], 1.0).then_inc(clean_pool, 1)
            pool.memset(zero3[:], 0.0).then_inc(clean_pool, 1)
            pool.wait_ge(clean_pool, 2 * NBUF + 1)
            pool.memset(minus_one[:], -1.0).then_inc(inverted, 1)
            pool.sem_inc(prob_free, 2)
            pool.wait_ge(inverted, 1)
            pool.memset(recip[:], 1.0).then_inc(inverted, 1)
            with pool.Fori(0, NU) as u:
                pool.wait_ge(o_kept, 2 * u + 4)
                apart(pool, M["passed"])
                for j in range(G):
                    row = M["OT"][32 * j + HD:32 * j + HD + 1, u, :].rearrange("o (p c) -> o p c", c=32)
                    pool.dma_start(sums[32 * j:32 * j + 32, :], row).then_inc(sums_in, 16)
                pool.wait_ge(sums_in, u * 16 * G + 16 * G)
                pool.tensor_tensor(sums[:], sums[:], minus_one[:], ALU.pow).then_inc(inverted, 1)
                pool.wait_ge(inverted, u + 3)
                apart(pool, M["passed"])
                rsum = M["rsum"][u].rearrange("j (p c) -> (j p) c", c=32)
                pool.dma_start(rsum, sums[:]).then_inc(rsum_out, 16)
                pool.wait_ge(rsum_out, u * 16 + 16)
                apart(pool, M["passed"])
                for j in range(G):
                    pool.dma_start(recip[32 * j:32 * j + HD, :],
                                   M["rsum"][u, j].unsqueeze(0).broadcast_to([HD, T])).then_inc(recip_in, 16)
                pool.wait_ge(recip_in, u * 16 * G + 16 * G)
                apart(pool, M["passed"])
                pool.tensor_tensor(M["OT"][:, u, :], M["OT"][:, u, :], recip[:], ALU.mult).then_inc(o_done, 1)
                pool.wait_ge(o_done, u + 1)

        @block.sync
        def _(sp):
            sp.wait_ge(clean_pool, 2 * NBUF + 1)

            def load(v, s):
                for i in range(PARTS):
                    for j in range(PARTS):
                        rows = slice((PARTS * i + j) * HD, (PARTS * i + j + 1) * HD)
                        sp.dma_start(Q[s][rows], qparts[v, i]).then_inc(qk_in[s], 16)
                        sp.dma_start(K[s][rows], kparts[v, j]).then_inc(qk_in[s], 16)
                sp.dma_start(Q[s][KROWS:KROWS + PARTS],
                             zero3[:].unsqueeze(1).broadcast_to([PARTS, G, T])).then_inc(qk_in[s], 16)
                sp.dma_start(vu[s][:], M["v9"][v]).then_inc(v_in[s], 16)

            def send_max(v, s):
                sp.wait_ge(max_split, v + 1)
                for i in range(PARTS):
                    row = Q[s][KROWS + i:KROWS + i + 1].rearrange("o h (r a) -> o (h r) a", a=P)
                    sp.dma_start(row, mparts[:, i, :]).then_inc(max_in, 16)

            for v in range(NBUF):
                load(v, v)
            send_max(0, 0)
            with sp.Fori(0, NU // NBUF - 1) as i:
                for s in range(NBUF):
                    send_max(i * NBUF + s + 1, (s + 1) % NBUF)
                    sp.wait_ge(prob_free, i * (NBUF * NT) + (s + 1) * NT + 2)
                    apart(sp, M["passed"])
                    load(i * NBUF + NBUF + s, s)
            u = NU - 1 - NBUF
            send_max(u + 1, (u + 1) % NBUF)
            sp.wait_ge(prob_free, (u + 1) * NT + 2)
            load(NU - 1, (NU - 1) % NBUF)
            for v in range(u + 2, NU):
                send_max(v, v % NBUF)


def project_out(nc, M, name, wop, last_layer):
    with ExitStack() as ctx:
        sem = lambda n: new_semaphore(nc, M, f"{name}_{n}")
        sb = lambda n, shape, dt=F32: ctx.enter_context(nc.sbuf_tensor(f"{name}_{n}", shape, dt))
        ps = lambda n: ctx.enter_context(nc.psum_tensor(f"{name}_{n}", [P, T], F32))
        pp, pt, px, ph = ps("pp"), ps("pt"), ps("px"), ps("ph")
        aT = sb("aT", [P, T])
        y, xn, hn = (sb(n, [P, NT, P]) for n in ("y", "xn", "hn"))
        stats, mv = sb("stats", [P, NT, 6]), sb("mv", [P, NT, 2])
        ms, tmp, rstd = sb("ms", [P, NT]), sb("tmp", [P, NT]), sb("rstd", [P, NT])
        projected, a_kept, flipped, y_made = sem("projected"), sem("a_kept"), sem("flipped"), sem("y_made")
        stats_ready, rstd_ready, chain_d, chain_p = sem("stats_ready"), sem("rstd_ready"), sem("cd"), sem("cp")
        x_ready, h_ready, x_flipped, h_flipped = sem("x_ready"), sem("h_ready"), sem("x_flipped"), sem("h_flipped")
        xt_kept, ht_kept, x_stored = sem("xt_kept"), sem("ht_kept"), sem("x_stored")
        block = ctx.enter_context(nc.Block())
        halves = [slice(0, HALF), slice(HALF, T)]

        @block.tensor
        def _(pe):
            with pe.Fori(0, B) as b:
                pe.wait_ge(a_kept, b + 1)
                for c in halves:
                    for g in range(UPB):
                        last = pe.matmul(pp[:, c], wop[:, g, :], M["OT"][:, b * UPB + g, c],
                                         start=g == 0, stop=g == UPB - 1)
                last.then_inc(projected, 1)
                pe.wait_ge(a_kept, b + 2)
                pe.wait_ge(y_made, b + 1)
                for t in range(NT):
                    last = pe.transpose(pt[:, t * P:(t + 1) * P], aT[:, t * P:(t + 1) * P], M["identF"][:])
                last.then_inc(flipped, 1)
                if not last_layer:
                    pe.wait_ge(x_ready, b + 1)
                    pe.wait_ge(xt_kept, b + 1)
                    for t in range(NT):
                        last = pe.transpose(px[:, t * P:(t + 1) * P], xn[:, t, :], M["identF"][:])
                    last.then_inc(x_flipped, 1)
                pe.wait_ge(h_ready, b + 1)
                pe.wait_ge(ht_kept, b + 1)
                for t in range(NT):
                    last = pe.transpose(ph[:, t * P:(t + 1) * P], hn[:, t, :], M["identF"][:])
                last.then_inc(h_flipped, 1)

        @block.scalar
        def _(act):
            act.sem_inc(a_kept, 1)
            act.sem_inc(xt_kept, 1)
            act.sem_inc(ht_kept, 1)
            act.sem_inc(flipped, 1)
            with act.Fori(0, B) as b:
                act.wait_ge(projected, b + 1)
                act.wait_ge(flipped, b + 1)
                act.activation(aT[:], pp[:], ACT.Copy).then_inc(a_kept, 1)
                if not last_layer:
                    act.wait_ge(x_flipped, b + 1)
                    act.activation(M["XT"][:, b, :], px[:], ACT.Copy).then_inc(xt_kept, 1)
                act.wait_ge(h_flipped, b + 1)
                if last_layer:
                    act.activation(M["HT"][:, b, :], ph[:], ACT.Copy, scale=M["norm"][:, 1:2]).then_inc(ht_kept, 1)
                else:
                    act.activation(M["HT"][:, b, :], ph[:], ACT.Copy).then_inc(ht_kept, 1)

        @block.vector
        def _(dve):
            dve.sem_inc(y_made, 1)
            PER = 3 if last_layer else 4
            with dve.Fori(0, B) as b:
                ch = Chain(dve, chain_d, b * PER)
                dve.wait_ge(flipped, b + 2)
                ptt = pt[:].rearrange("p (t c) -> p t c", c=P)
                dve.tensor_tensor(y[:], ptt, M["X"][:, b], ALU.add).then_inc(y_made, 1)
                dve.wait_ge(y_made, b + 2)
                if last_layer:
                    dve.wait_ge(ht_kept, b + 1)
                    ch.do(rms_normalise(dve, ch, hn, y, xn[:], ms[:], rstd, NT, stats_ready, rstd_ready, b))
                    dve.sem_inc(h_ready, 1)
                    ch.do(dve.tensor_tensor(M["X"][:, b], M["X"][:, b], y[:], ALU.add))
                else:
                    dve.wait_ge(xt_kept, b + 1)
                    dve.wait_ge(x_stored, b + 1)
                    ch.do(normalise(dve, ch, xn, y, stats, mv, rstd, NT, stats_ready, rstd_ready, b * 2, M["passed"]))
                    dve.sem_inc(x_ready, 1)
                    dve.wait_ge(ht_kept, b + 1)
                    ch.do(normalise(dve, ch, hn, xn, stats, mv, rstd, NT, stats_ready, rstd_ready, b * 2 + 1, M["passed"]))
                    dve.sem_inc(h_ready, 1)
                assert ch.k == PER

        @block.gpsimd
        def _(pool):
            pool.sem_inc(x_stored, 1)
            with pool.Fori(0, B) as b:
                if last_layer:
                    make_rstd(pool, Chain(pool, chain_p, b), rstd[:], ms[:], tmp[:], M["minus_half"][:, 0:NT],
                              1.0 / P, RMS_EPS, stats_ready, rstd_ready, b, M["passed"])
                else:
                    for n in range(2):
                        make_rstd(pool, Chain(pool, chain_p, b * 2 + n), rstd[:], mv[:, :, 1], tmp[:],
                                  M["minus_half"][:, 0:NT], 1.0, LN_EPS, stats_ready, rstd_ready, b * 2 + n, M["passed"])
                        if n == 0:
                            pool.wait_ge(x_ready, b + 1)
                            apart(pool, M["passed"])
                            pool.tensor_copy(M["X"][:, b], xn[:]).then_inc(x_stored, 1)


def route(nc, M, name, src, layer):
    TT = B * NT
    with ExitStack() as ctx:
        sem = lambda n: new_semaphore(nc, M, f"{name}_{n}")
        sb = lambda n, shape, dt=F32: ctx.enter_context(nc.sbuf_tensor(f"{name}_{n}", shape, dt))
        xs = sb("xs", [P, T])
        logits, expd, prob = sb("logits", [P, TT, E]), sb("expd", [P, TT, E]), sb("prob", [P, TT, E])
        cmp1, cmp2 = sb("cmp1", [P, TT, E, E]), sb("cmp2", [P, TT, E, E])
        top, total, inv = sb("top", [P, TT]), sb("total", [P, TT]), sb("inv", [P, TT])
        rank = sb("rank", [P, TT, E])
        pl = ctx.enter_context(nc.psum_tensor(f"{name}_pl", [P, HALF], F32))
        staged, judged, kept, chain_d, shifted, exped = (sem("staged"), sem("judged"), sem("kept"),
                                                         sem("cd"), sem("shifted"), sem("exped"))
        block = ctx.enter_context(nc.Block())

        @block.scalar
        def _(act):
            act.sem_inc(judged, 1)
            with act.Fori(0, B) as b:
                act.wait_ge(judged, b + 1)
                act.activation(xs[:], src[:, b, :], ACT.Copy).then_inc(staged, 1)
            for n in range(1 + layer):
                act.wait_ge(shifted, n + 1)
                act.activation(expd[:], expd[:], ACT.Exp).then_inc(exped, 1)

        @block.tensor
        def _(pe):
            with pe.Fori(0, B) as b:
                pe.wait_ge(staged, b + 1)
                pe.wait_ge(kept, b + 1)
                for t in range(NT):
                    last = pe.matmul(pl[:, t * E:(t + 1) * E], xs[:, t * P:(t + 1) * P], M["rw"][:, layer, :],
                                     start=True, stop=True)
                last.then_inc(judged, 1)

        @block.vector
        def _(dve):
            dve.sem_inc(kept, 1)
            lb = logits[:].rearrange("p (b t) e -> p b t e", b=B)
            with dve.Fori(0, B) as b:
                dve.wait_ge(judged, b + 2)
                dve.tensor_copy(lb[:, b], pl[:, 0:NT * E].rearrange("p (t e) -> p t e", e=E)).then_inc(kept, 1)
            dve.wait_ge(kept, B + 1)
            ch = Chain(dve, chain_d)
            if layer == 0:
                ch.do(dve.tensor_tensor(logits[:], logits[:], M["rb"][:].unsqueeze(1).broadcast_to([P, TT, E]),
                                        ALU.add))

            def shift(src):
                ch.do(dve.tensor_reduce(top[:], src[:], AX.X, ALU.max))
                dve.tensor_tensor(expd[:], src[:], bc_free(top[:], E), ALU.subtract).then_inc(shifted, 1)

            def divide(dst):
                ch.do(dve.tensor_reduce(total[:], expd[:], AX.X, ALU.add))
                ch.do(dve.reciprocal(inv[:], total[:]))
                ch.do(dve.tensor_tensor(dst, expd[:], bc_free(inv[:], E), ALU.mult))

            shift(logits)
            judge = logits
            if layer == 1:
                dve.wait_ge(exped, 1)
                divide(prob[:])
                shift(prob)
                judge = prob
            other = judge[:].unsqueeze(2).broadcast_to([P, TT, E, E])
            own = bc_free(judge[:], E)
            ch.mark(dve.tensor_tensor(cmp1[:], other, own, ALU.is_gt))
            ch.do(dve.tensor_tensor(cmp2[:], other, own, ALU.is_equal))
            ch.do(dve.tensor_tensor(cmp2[:], cmp2[:], M["before"][:].unsqueeze(1).broadcast_to([P, TT, E, E]),
                                    ALU.mult))
            ch.do(dve.tensor_tensor(cmp1[:], cmp1[:], cmp2[:], ALU.add))
            ch.do(dve.tensor_reduce(rank[:], cmp1[:], AX.X, ALU.add))
            ch.do(dve.tensor_scalar(rank[:], rank[:], 2.0, None, ALU.is_lt))
            dve.wait_ge(exped, 1 + layer)
            ch.do(dve.tensor_tensor(expd[:], expd[:], rank[:], ALU.mult))
            divide(M["gates"][:])
            ch.do(dve.tensor_reduce(M["gate_sum"][:], M["gates"][:], AX.X, ALU.add))


def experts(nc, A, M, name, layer, out):
    F = A["L0_ffn_W1"].shape[2] if layer == 0 else A["L1_ffn_e_gate"].shape[2]
    NE = E if layer == 0 else E + 1
    FB = F // P
    with ExitStack() as ctx:
        sem = lambda n: new_semaphore(nc, M, f"{name}_{n}")
        sb = lambda n, shape, dt=F32: ctx.enter_context(nc.sbuf_tensor(f"{name}_{n}", shape, dt))
        up = sb("up", [P, NE, BANKS, P])
        down = sb("down", [P, NE, FB, P])
        h = sb("h", [P, 2, HALF])
        hidden = sb("hidden", [P, 2, FB, HALF])
        silu = sb("silu", [P, FB, HALF])
        gch = sb("gch", [P, P])
        gsc = sb("gsc", [P, CT])
        gT = sb("gT", [CT * E, P])
        acc, y, xn = sb("acc", [P, CT, P]), sb("y", [P, CT, P]), sb("xn", [P, CT, P])
        stats, mv = sb("stats", [P, CT, 6]), sb("mv", [P, CT, 2])
        tmp, rstd = sb("tmp", [P, CT]), sb("rstd", [P, CT])
        lng, lnb = M["cols"][:, 0:E], M["cols"][:, E:2 * E]
        b1 = M["cols"][:, 2 * E:].rearrange("p (e f) -> p e f", f=BANKS)
        b2p = sb("b2p", [CT * E, CT, P])
        pa = ctx.enter_context(nc.psum_tensor(f"{name}_pa", [P, BANKS, HALF], F32))
        py = [ctx.enter_context(nc.psum_tensor(f"{name}_py{i}", [P, CT, P], F32)) for i in range(2)]
        pg = ctx.enter_context(nc.psum_tensor(f"{name}_pg", [P, CT, P], F32))
        px = ctx.enter_context(nc.psum_tensor(f"{name}_px", [P, CT, P], F32))
        w_in, clean, g_staged, g_flipped, g_kept, bias_ready = (sem("w_in"), sem("clean"), sem("g_staged"),
                                                                sem("g_flipped"), sem("g_kept"), sem("bias_ready"))
        h_ready, a_ready, a_free, u_free, y_ready, y_free = (sem("h_ready"), sem("a_ready"), sem("a_free"),
                                                             sem("u_free"), sem("y_ready"), sem("y_free"))
        stats_ready, rstd_ready, chain_d, chain_p = sem("stats_ready"), sem("rstd_ready"), sem("cd"), sem("cp")
        x_ready, x_flipped, xt_kept, x_stored = sem("x_ready"), sem("x_flipped"), sem("xt_kept"), sem("x_stored")
        block = ctx.enter_context(nc.Block())

        X = M["X"][:].rearrange("p b (k t) d -> p (b k) t d", t=CT)
        XT = M["XT"].rearrange("p b (k c) -> p (b k) c", c=HALF)
        HT = M["HT"][:].rearrange("p b (k c) -> p (b k) c", c=HALF)
        gates = M["gates"][:].rearrange("p (k t) e -> p k t e", t=CT)
        gate_sum = M["gate_sum"][:].rearrange("p (k t) -> p k t", t=CT)
        out_v = out.rearrange("b (k t p) d -> (b k) p t d", t=CT, p=P)
        loads = []
        if layer == 0:
            loads += [(up[:].rearrange("p e f c -> p e (f c)"), A["L0_ffn_W1"].rearrange("e p f -> p e f")),
                      (down[:], A["L0_ffn_W2"].rearrange("e (f p) n -> p e f n", p=P))]
        else:
            two = lambda n: up[:, 0:E, FB * n:FB * n + FB, :].rearrange("p e f c -> p e (f c)")
            one = lambda n: up[:, E, FB * n:FB * n + FB, :].rearrange("p f c -> p (f c)")
            loads += [(two(0), A["L1_ffn_e_gate"].rearrange("e p f -> p e f")),
                      (two(1), A["L1_ffn_e_up"].rearrange("e p f -> p e f")),
                      (one(0), A["L1_ffn_sh_gate"]), (one(1), A["L1_ffn_sh_up"]),
                      (down[:, 0:E], A["L1_ffn_e_down"].rearrange("e (f p) n -> p e f n", p=P)),
                      (down[:, E], A["L1_ffn_sh_down"].rearrange("(f p) n -> p f n", p=P))]
        NLOAD = len(loads) + (CT if layer == 0 else 0)

        @block.sync
        def _(sp):
            for dst, src in loads:
                sp.dma_start(dst, src).then_inc(w_in, 16)
            if layer == 0:
                sp.wait_ge(clean, 2)
                for t in range(CT):
                    sp.dma_start(b2p[E * t:E * t + E, t, :], A["L0_ffn_b2"]).then_inc(w_in, 16)
            else:
                with sp.Fori(0, CH) as c:
                    sp.wait_ge(x_ready, c + 1)
                    apart(sp, M["passed"])
                    sp.dma_start(out_v[c], xn[:]).then_inc(x_stored, 16)
                sp.wait_ge(x_stored, 16 * CH + 16)

        @block.gpsimd
        def _(pool):
            pool.memset(gch[:], 0.0).then_inc(clean, 1)
            pool.memset(b2p[:], 0.0).then_inc(clean, 1)
            pool.sem_inc(x_stored, 16)
            with pool.Fori(0, CH) as c:
                make_rstd(pool, Chain(pool, chain_p, c), rstd[:], mv[:, :, 1], tmp[:], M["minus_half"][:, 0:CT],
                          1.0, LN_EPS, stats_ready, rstd_ready, c, M["passed"])
                if layer == 0:
                    pool.wait_ge(x_ready, c + 1)
                    apart(pool, M["passed"])
                    pool.tensor_copy(X[:, c], xn[:]).then_inc(x_stored, 16)

        FREED = FB if layer == 1 else BANKS

        def reusable(eng, semaphore, c, e):
            eng.wait_ge(semaphore, c * NE + (2 if e < 2 else e + 1))

        @block.tensor
        def _(pe):
            pe.sem_inc(a_ready, 1)
            pe.sem_inc(y_ready, 2)
            pe.wait_ge(w_in, 16 * NLOAD)
            pe.wait_ge(clean, 2)

            def rise(c, e):
                if layer == 0:
                    pe.wait_ge(h_ready, c * NE + e + 1)
                for f in range(BANKS):
                    if layer == 0:
                        pe.wait_ge(a_free, c * (NE * BANKS) + e * BANKS + f + 1)
                    elif f < FB:
                        pe.wait_ge(a_free, c * (NE * FB) + e * FB + f + 1)
                    else:
                        pe.wait_ge(u_free, c * (NE * FB) + e * FB + f - FB + 1)
                    pe.matmul(pa[:, f, :], up[:, e, f, :], h[:, e % 2, :] if layer == 0 else HT[:, c],
                              start=True, stop=True).then_inc(a_ready, 1)

            def fall(c, e):
                hidden_made = a_free if layer == 0 else u_free
                pe.wait_ge(hidden_made, c * (NE * FREED) + (e + 2) * FREED)
                reusable(pe, y_free, c, e)
                for t in range(CT):
                    for f in range(FB):
                        last = pe.matmul(py[e % 2][:, t, :], hidden[:, e % 2, f, t * P:(t + 1) * P],
                                         down[:, e, f, :], start=f == 0, stop=f == FB - 1)
                last.then_inc(y_ready, 1)

            with pe.Fori(0, CH) as c:
                if layer == 0:
                    pe.wait_ge(g_staged, c + 1)
                    pe.transpose(pg[:, 0, :], gch[:], M["identF"][:]).then_inc(g_flipped, 1)
                    pe.wait_ge(g_kept, c + 1)
                    for t in range(CT):
                        last = pe.matmul(pg[:, t, :], gT[:], b2p[:, t, :], start=True, stop=True)
                    last.then_inc(bias_ready, 1)
                rise(c, 0)
                for e in range(1, NE):
                    rise(c, e)
                    fall(c, e - 1)
                fall(c, NE - 1)
                if layer == 0:
                    pe.wait_ge(x_ready, c + 1)
                    pe.wait_ge(xt_kept, c + 1)
                    for t in range(CT):
                        last = pe.transpose(px[:, t, :], xn[:, t, :], M["identF"][:])
                    last.then_inc(x_flipped, 1)

        @block.scalar
        def _(act):
            act.sem_inc(a_free, FREED)
            act.sem_inc(xt_kept, 1)
            act.wait_ge(w_in, 16 * NLOAD)
            with act.Fori(0, CH) as c:
                if layer == 0:
                    act.wait_ge(g_flipped, c + 1)
                    act.activation(gT[:], pg[0:CT * E, 0, :], ACT.Copy).then_inc(g_kept, 1)
                for e in range(NE):
                    if layer == 0:
                        reusable(act, y_ready, c, e)
                    for f in range(FREED):
                        act.wait_ge(a_ready, c * (NE * BANKS) + e * BANKS + f + 2)
                        if layer == 0:
                            act.activation(hidden[:, e % 2, f, :], pa[:, f, :], ACT.Gelu,
                                           bias=b1[:, e, f:f + 1]).then_inc(a_free, 1)
                        else:
                            act.wait_ge(u_free, c * (NE * FB) + e * FB + f + 1)
                            act.activation(silu[:, f, :], pa[:, f, :], ACT.Silu).then_inc(a_free, 1)
                if layer == 0:
                    act.wait_ge(x_flipped, c + 1)
                    act.activation(XT[:, c], px[:].rearrange("p t d -> p (t d)"), ACT.Copy).then_inc(xt_kept, 1)

        @block.vector
        def _(dve):
            dve.sem_inc(y_free, 2)
            if layer == 1:
                dve.sem_inc(u_free, FB)
            dve.wait_ge(w_in, 16 * NLOAD)
            dve.wait_ge(clean, 2)
            PER = NE + (4 if layer == 0 else 3)

            def feed(c, e):
                dve.wait_ge(a_ready, c * (NE * BANKS) + (max(e - 1, 0) * BANKS + 1))
                dve.tensor_scalar(h[:, e % 2, :], HT[:, c], lng[:, e:e + 1], lnb[:, e:e + 1],
                                  ALU.mult, ALU.add).then_inc(h_ready, 1)

            def gate_up(c, e):
                reusable(dve, y_ready, c, e)
                for f in range(FB):
                    dve.wait_ge(a_ready, c * (NE * BANKS) + e * BANKS + FB + f + 2)
                    dve.wait_ge(a_free, c * (NE * FB) + e * FB + FB + f + 1)
                    dve.tensor_tensor(hidden[:, e % 2, f, :], silu[:, f, :], pa[:, FB + f, :],
                                      ALU.mult).then_inc(u_free, 1)

            def add(c, e, ch):
                dve.wait_ge(y_ready, c * NE + e + 3)
                for t in range(CT):
                    g = gch[:, t * E + e:t * E + e + 1]
                    if layer == 1 and e == 0:
                        last = dve.tensor_scalar(acc[:, t, :], py[0][:, t, :], g, None, ALU.mult)
                    elif e < E:
                        last = dve.scalar_tensor_tensor(acc[:, t, :], py[e % 2][:, t, :], g, acc[:, t, :],
                                                        ALU.mult, ALU.add)
                if e == E:
                    last = dve.tensor_tensor(acc[:], acc[:], py[e % 2][:], ALU.add)
                ch.do(last)
                dve.sem_inc(y_free, 1)

            with dve.Fori(0, CH) as c:
                ch = Chain(dve, chain_d, c * PER)
                ch.do(dve.tensor_copy(gsc[:], gate_sum[:, c]))
                dve.tensor_copy(gch[:, 0:CT * E].rearrange("p (t e) -> p t e", e=E), gates[:, c]).then_inc(g_staged, 1)
                dve.wait_ge(g_staged, c + 1)
                if layer == 0:
                    feed(c, 0)
                    dve.wait_ge(bias_ready, c + 1)
                    for t in range(CT):
                        last = dve.scalar_tensor_tensor(acc[:, t, :], X[:, c, t, :], gsc[:, t:t + 1], pg[:, t, :],
                                                        ALU.mult, ALU.add)
                    ch.do(last)
                for e in range(NE):
                    if layer == 0 and e + 1 < NE:
                        feed(c, e + 1)
                    if layer == 1:
                        gate_up(c, e)
                    if e:
                        add(c, e - 1, ch)
                add(c, NE - 1, ch)
                ch.do(dve.tensor_tensor(y[:], acc[:], X[:, c], ALU.add))
                if layer == 0:
                    dve.wait_ge(xt_kept, c + 1)
                    dve.wait_ge(x_stored, c + 1)
                else:
                    dve.wait_ge(x_stored, c * 16 + 16)
                normalise(dve, ch, xn, y, stats, mv, rstd, CT, stats_ready, rstd_ready, c, M["passed"]).then_inc(x_ready, 1)
                assert ch.k == PER


def scan_layer(nc, M, name):
    with ExitStack() as ctx:
        sem = lambda n: new_semaphore(nc, M, f"{name}_{n}")
        sb = lambda n, shape, dt=F32: ctx.enter_context(nc.sbuf_tensor(f"{name}_{n}", shape, dt))
        pw = [ctx.enter_context(nc.psum_tensor(f"{name}_pw{i}", [P, T], F32)) for i in range(4)]
        k, beta, kv, state, o = sb("k", [P, T]), sb("beta", [P, T]), sb("kv", [P, T]), sb("state", [P, T]), sb("o", [P, T])
        xb, y, z, xn, hn = (sb(n, [P, NT, P]) for n in ("xb", "y", "z", "xn", "hn"))
        stats, mv = sb("stats", [P, NT, 6]), sb("mv", [P, NT, 2])
        ms, tmp, rstd = sb("ms", [P, NT]), sb("tmp", [P, NT]), sb("rstd", [P, NT])
        projected, evacuated, o_ready, out_ready, y_made = (sem("projected"), sem("evacuated"), sem("o_ready"),
                                                            sem("out_ready"), sem("y_made"))
        xb_ready, h_ready, h_flipped, ht_kept, x_ready, x_stored = (sem("xb_ready"), sem("h_ready"), sem("h_flipped"),
                                                                    sem("ht_kept"), sem("x_ready"), sem("x_stored"))
        stats_ready, rstd_ready, chain_d, chain_p = sem("stats_ready"), sem("rstd_ready"), sem("cd"), sem("cp")
        block = ctx.enter_context(nc.Block())
        pout, ph = pw[0], pw[1]
        SETS = 3

        @block.tensor
        def _(pe):
            with pe.Fori(0, B) as b:
                pe.wait_ge(ht_kept, b + 1)
                for n in (1, 2, 3, 0):
                    for half in range(2):
                        c = slice(half * HALF, (half + 1) * HALF)
                        last = pe.matmul(pw[n][:, c], M["w1d"][:, n, :], M["XT"][:, b, c], start=True, stop=True)
                    last.then_inc(projected, 1)
                pe.wait_ge(o_ready, b + 1)
                for t in range(NT):
                    last = pe.matmul(pout[:, t * P:(t + 1) * P], o[:, t * P:(t + 1) * P], M["w1d"][:, 4, :],
                                     start=True, stop=True)
                last.then_inc(out_ready, 1)
                pe.wait_ge(h_ready, b + 1)
                for t in range(NT):
                    last = pe.transpose(ph[:, t * P:(t + 1) * P], hn[:, t, :], M["identF"][:])
                last.then_inc(h_flipped, 1)

        @block.scalar
        def _(act):
            act.sem_inc(ht_kept, 1)
            with act.Fori(0, B) as b:
                act.wait_ge(projected, b * 4 + 1)
                act.activation(k[:], pw[1][:], ACT.Copy).then_inc(evacuated, 1)
                act.wait_ge(projected, b * 4 + 3)
                act.activation(beta[:], pw[3][:], ACT.Sigmoid, bias=M["bbeta"][:, 0:1]).then_inc(evacuated, 1)
                act.wait_ge(h_flipped, b + 1)
                act.activation(M["HT"][:, b, :], ph[:], ACT.Copy, scale=M["norm"][:, 0:1]).then_inc(ht_kept, 1)

        @block.gpsimd
        def _(pool):
            pool.sem_inc(x_stored, 1)
            with pool.Fori(0, B) as b:
                bo = M["bo"][:].unsqueeze(1).broadcast_to([P, NT, P])
                pool.wait_ge(y_made, b + 1)
                apart(pool, M["passed"])
                pool.tensor_tensor(xb[:], M["X"][:, b], bo, ALU.add).then_inc(xb_ready, 1)
                for n in range(SETS):
                    rms = n == SETS - 1
                    if rms:
                        pool.wait_ge(x_ready, b + 1)
                        apart(pool, M["passed"])
                        pool.tensor_copy(M["X"][:, b], xn[:]).then_inc(x_stored, 1)
                    make_rstd(pool, Chain(pool, chain_p, b * SETS + n), rstd[:], ms[:] if rms else mv[:, :, 1],
                              tmp[:], M["minus_half"][:, 0:NT], 1.0 / P if rms else 1.0,
                              RMS_EPS if rms else LN_EPS, stats_ready, rstd_ready, b * SETS + n, M["passed"])

        @block.vector
        def _(dve):
            dve.sem_inc(y_made, 1)
            PER = 9
            with dve.Fori(0, B) as b:
                ch = Chain(dve, chain_d, b * PER)
                dve.wait_ge(evacuated, b * 2 + 1)
                dve.wait_ge(projected, b * 4 + 2)
                ch.do(dve.tensor_tensor(kv[:], k[:], pw[2][:], ALU.mult))
                dve.wait_ge(evacuated, b * 2 + 2)
                ch.do(dve.tensor_tensor_scan(state[:], beta[:], kv[:], 0.0, ALU.mult, ALU.add))
                dve.wait_ge(projected, b * 4 + 4)
                dve.tensor_tensor(o[:], state[:], pw[0][:], ALU.mult).then_inc(o_ready, 1)
                dve.wait_ge(out_ready, b + 1)
                dve.wait_ge(xb_ready, b + 1)
                dve.tensor_tensor(y[:], pout[:].rearrange("p (t d) -> p t d", d=P), xb[:], ALU.add).then_inc(y_made, 1)
                dve.wait_ge(y_made, b + 2)
                ch.do(normalise(dve, ch, z, y, stats, mv, rstd, NT, stats_ready, rstd_ready, b * SETS, M["passed"]))
                wide = lambda m: m[:].unsqueeze(1).broadcast_to([P, NT, P])
                ch.do(dve.tensor_tensor(z[:], z[:], wide(M["lng"]), ALU.mult))
                ch.do(dve.tensor_tensor(z[:], z[:], wide(M["lnb"]), ALU.add))
                ch.do(dve.tensor_tensor(z[:], z[:], M["X"][:, b], ALU.add))
                dve.wait_ge(x_stored, b + 1)
                dve.wait_ge(ht_kept, b + 1)
                normalise(dve, ch, xn, z, stats, mv, rstd, NT, stats_ready, rstd_ready, b * SETS + 1, M["passed"]).then_inc(x_ready, 1)
                dve.wait_ge(x_ready, b + 1)
                rms_normalise(dve, ch, hn, xn, z[:], ms[:], rstd, NT, stats_ready, rstd_ready,
                              b * SETS + 2).then_inc(h_ready, 1)
                assert ch.k == PER, ch.k


def build(nc, A, out):
    TT = B * NT
    with ExitStack() as ctx:
        shapes = dict(
            X=[P, B, NT, P], OT=[P, NU, T], HT=[P, B, T],
            w0a=[P, 3, P], wop0=[P, UPB, P], w1d=[P, 5, P], w1a=[P, 3, P], wop1=[P, UPB, P],
            identF=[P, P], bo=[P, P], lng=[P, P], lnb=[P, P], norm=[P, 2], bbeta=[P, 1],
            rw=[P, 2, E], rb=[P, E], before=[P, E, E], minus_half=[P, NT], cols=[P, 2 * E + E * BANKS], gates=[P, TT, E], gate_sum=[P, TT])
        M = {k: ctx.enter_context(nc.sbuf_tensor(k, v, F32)) for k, v in shapes.items()}
        for k, n in (("identB", P), ("row0", T), ("first", 3 * P), ("band", 3 * P)):
            M[k] = ctx.enter_context(nc.sbuf_tensor(k, [P, n], BF16))
        M["XT"] = M["OT"][:, 0:B, :]
        M["v9"] = nc.dram_tensor("v9", [NU, P, NT, G, HD + 1], F32, kind="Internal").ap()
        M["parts"] = nc.dram_tensor("parts", [2, B, UPB, PARTS, 32, T], BF16, kind="Internal").ap()
        M["rsum"] = nc.dram_tensor("rsum", [NU, G, T], F32, kind="Internal").ap()
        M["passed"] = nc.alloc_semaphore("passed")
        M["semaphores"] = []
        setup(nc, A, M)
        read_x(nc, A, M)
        for layer, src, w, wop, segments in ((0, "XT", "w0a", "wop0", BANDED), (1, "HT", "w1a", "wop1", FULL)):
            if layer == 1:
                scan_layer(nc, M, "scan")
            project_qkv(nc, M, f"qkv{layer}", M[src], M[w])
            attend(nc, M, f"att{layer}", segments)
            project_out(nc, M, f"out{layer}", M[wop], layer == 1)
            route(nc, M, f"route{layer}", M["XT"] if layer == 0 else M["HT"], layer)
            experts(nc, A, M, f"moe{layer}", layer, out)
            if layer == 0:
                clear_semaphores(nc, M)


_INS = ['L0_attn_x', 'L0_attn_Wq', 'L0_attn_Wk', 'L0_attn_Wv', 'L0_attn_Wo', 'L0_ffn_router_W', 'L0_ffn_router_b',
        'L0_ffn_ln_g', 'L0_ffn_ln_b', 'L0_ffn_W1', 'L0_ffn_b1', 'L0_ffn_W2', 'L0_ffn_b2', 'L1_attn_Wq',
        'L1_attn_Wk', 'L1_attn_Wv', 'L1_attn_Wbeta', 'L1_attn_b_beta', 'L1_attn_Wo', 'L1_attn_b_o',
        'L1_attn_ln_g', 'L1_attn_ln_b', 'L1_ffn_norm1_w', 'L1_ffn_norm2_w', 'L1_ffn_wq', 'L1_ffn_wk',
        'L1_ffn_wv', 'L1_ffn_wo', 'L1_ffn_router_w', 'L1_ffn_sh_gate', 'L1_ffn_sh_up', 'L1_ffn_sh_down',
        'L1_ffn_e_gate', 'L1_ffn_e_up', 'L1_ffn_e_down']


def kernel(**inputs):
    import numpy as _np
    import concourse.bacc as _bacc
    from concourse import mybir as _mybir
    from concourse.bass_utils import run_bass_kernel_spmd as _run

    nc = _bacc.Bacc("TRN2", target_bir_lowering=False, num_devices=1)
    arrays, args = {}, {}
    for name in _INS:
        a = _np.ascontiguousarray(inputs[name])
        arrays[f"in_{name}"] = a
        args[name] = nc.dram_tensor(f"in_{name}", a.shape, _mybir.dt.from_np(a.dtype), kind="ExternalInput").ap()
    out = nc.dram_tensor("out_0", (B, T, P), _mybir.dt.float32, kind="ExternalOutput").ap()
    build(nc, args, out)
    r = _run(nc, [arrays], core_ids=[0])
    return r.results[0]["out_0"]
```

```python
from contextlib import ExitStack

import concourse.bass as bass
from concourse import mybir

F32 = mybir.dt.float32
BF16 = mybir.dt.bfloat16
ALU = mybir.AluOpType
ACT = mybir.ActivationFunctionType
AX = mybir.AxisListType

P = 128
B, T = 4, 1024
NT = T // P
H, HD = 16, 8
G = 4
UPB = H // G
NU = B * UPB
HALF = 512
CH = B * T // HALF
CT = HALF // P
E = 8
BANKS = 4
PARTS = 3
KROWS = PARTS * PARTS * HD
KMAX = 96
SCALE = float(HD) ** -0.5
MASKED = -1.0e30
LN_EPS = 1e-05
RMS_EPS = 1e-06

FULL = [[(0, 0, HALF, ()), (HALF, HALF, HALF, ())] for _ in range(NT)]


def banded_segments():
    out = [[(0, 0, HALF, ((P, HALF - P, "row0", P),)), (HALF, HALF, HALF, ((0, HALF, "row0", HALF),))],
           [(0, 0, 3 * P, ((0, P, "first", 0), (2 * P, P, "first", 2 * P)))]]
    for r in range(2, NT):
        n = (min(r + 2, NT) - (r - 1)) * P
        masks = ((0, P, "band", 0), (2 * P, P, "band", 2 * P))
        out.append([(0, (r - 1) * P, n, masks[:n // P - 1]), (n, 0, 1, ())])
    return out


BANDED = banded_segments()


class Chain:

    def __init__(self, engine, semaphore, base=0):
        self.engine, self.semaphore, self.base, self.k = engine, semaphore, base, 0

    def mark(self, instruction):
        self.k += 1
        instruction.then_inc(self.semaphore, 1)

    def settle(self):
        self.engine.wait_ge(self.semaphore, self.base + self.k)

    def do(self, instruction):
        self.mark(instruction)
        self.settle()


def apart(engine, passed):
    engine.sem_inc(passed, 1)


def new_semaphore(nc, M, name):
    handle = nc.alloc_semaphore(name)
    M["semaphores"].append(handle)
    return handle


def clear_semaphores(nc, M):
    nc.clear_and_free_semaphores(M["semaphores"])
    nc.all_engine_barrier()
    M["semaphores"] = []


def bc_free(ap, n):
    return ap.unsqueeze(len(ap.shape)).broadcast_to(list(ap.shape) + [n])


def halved_tiles(tiles):
    return [range(0, tiles // 2), range(tiles // 2, tiles)]


def normalise(dve, chain, dst, src, stats, mv, rstd, tiles, stats_ready, rstd_ready, occasion, passed,
              meanwhile=None):
    for part in halved_tiles(tiles):
        for t in part:
            last = dve.bn_stats(stats[:, t, :], src[:, t, :])
        chain.do(last)
        apart(dve, passed)
        for t in part:
            last = dve.bn_aggr(mv[:, t, :], stats[:, t, :])
        last.then_inc(stats_ready, 1)
    if meanwhile:
        meanwhile()
    for n, part in enumerate(halved_tiles(tiles)):
        dve.wait_ge(rstd_ready, occasion * 2 + n + 1)
        for t in part:
            last = dve.tensor_scalar(dst[:, t, :], src[:, t, :], mv[:, t, 0:1], rstd[:, t:t + 1],
                                     ALU.subtract, ALU.mult)
    return last


def rms_normalise(dve, chain, dst, src, square, ms, rstd, tiles, stats_ready, rstd_ready, occasion,
                  meanwhile=None):
    for part in halved_tiles(tiles):
        c = slice(part.start, part.stop)
        chain.do(dve.tensor_tensor(square[:, c], src[:, c], src[:, c], ALU.mult))
        dve.tensor_reduce(ms[:, c], square[:, c], AX.X, ALU.add).then_inc(stats_ready, 1)
    if meanwhile:
        meanwhile()
    for n, part in enumerate(halved_tiles(tiles)):
        dve.wait_ge(rstd_ready, occasion * 2 + n + 1)
        for t in part:
            last = dve.tensor_scalar(dst[:, t, :], src[:, t, :], rstd[:, t:t + 1], None, ALU.mult)
    return last


def make_rstd(pool, chain_semaphore, rstd, src, tmp, minus_half, scale, eps, tiles, stats_ready, rstd_ready,
              occasion, passed):
    chain = Chain(pool, chain_semaphore, occasion * 2)
    for n, part in enumerate(halved_tiles(tiles)):
        c = slice(part.start, part.stop)
        pool.wait_ge(stats_ready, occasion * 2 + n + 1)
        apart(pool, passed)
        chain.do(pool.tensor_scalar(tmp[:, c], src[:, c], scale, eps, ALU.mult, ALU.add))
        pool.tensor_tensor(rstd[:, c], tmp[:, c], minus_half[:, c], ALU.pow).then_inc(rstd_ready, 1)


def setup(nc, A, M):
    with ExitStack() as ctx:
        sem = lambda name: new_semaphore(nc, M, "su_" + name)
        sb = lambda name, shape, dt=F32: ctx.enter_context(nc.sbuf_tensor("su_" + name, shape, dt))
        pt = ctx.enter_context(nc.psum_tensor("su_pt", [P, 8, HALF], F32))
        flip = sb("flip", [P, 5, P])
        wo_nat = sb("wo_nat", [P, P])
        wo_sp = sb("wo_sp", [P, UPB, G, 32])
        wqk = sb("wqk", [P, 2, P])
        qvT = sb("qvT", [P, 2, P])
        group = sb("group", [P, P])
        wbeta = sb("wbeta", [P, H])
        rows = sb("rows", [P, P])
        weights_in, consts, masks, placed = sem("weights_in"), sem("consts"), sem("masks"), sem("placed")
        spread, flipped, kept, folded = sem("spread"), sem("flipped"), sem("kept"), sem("folded")
        pool_chain, x_in, x_flipped, xt_kept = sem("pool_chain"), sem("x_in"), sem("x_flipped"), sem("xt_kept")
        block = ctx.enter_context(nc.Block())
        NB1 = E * (A["L0_ffn_b1"].shape[1] // P)
        loads = [(flip[:, n, :], A[k][:, :]) for n, k in enumerate(
            ["L0_attn_Wq", "L0_attn_Wk", "L0_attn_Wv", "L1_attn_Wq", "L1_attn_Wv"])]
        loads += [(wo_nat[:], A["L0_attn_Wo"]), (wbeta[:], A["L1_attn_Wbeta"])]
        loads += [(M["w1d"][:, 1, :], A["L1_attn_Wk"]), (M["w1d"][:, 4, :], A["L1_attn_Wo"])]
        loads += [(wqk[:, n, :], A[k]) for n, k in enumerate(["L1_ffn_wq", "L1_ffn_wk"])]
        loads += [(M["w1a"][:, 2, :], A["L1_ffn_wv"])]
        row = lambda k: A[k].unsqueeze(0).broadcast_to([P, P])
        loads += [(M["bo"][:], row("L1_attn_b_o")), (M["lng"][:], row("L1_attn_ln_g")),
                  (M["lnb"][:], row("L1_attn_ln_b"))]
        loads += [(M["norm"][:, 0:1], A["L1_ffn_norm1_w"].unsqueeze(1)),
                  (M["norm"][:, 1:2], A["L1_ffn_norm2_w"].unsqueeze(1))]
        loads += [(M["rw"][:, 0, :], A["L0_ffn_router_W"]), (M["rw"][:, 1, :], A["L1_ffn_router_w"]),
                  (M["rb"][:], A["L0_ffn_router_b"].unsqueeze(0).broadcast_to([P, E]))]
        bb = A["L1_attn_b_beta"].unsqueeze(1).broadcast_to([H, HD])
        NLOAD = len(loads) + 1

        @block.sync
        def _(sp):
            for b in range(B):
                sp.dma_start(M["X"][:, b], A["L0_attn_x"][b].rearrange("(t p) d -> p t d", p=P)).then_inc(x_in, 16)
            for dst, src in loads:
                sp.dma_start(dst, src).then_inc(weights_in, 16)
            sp.dma_start(M["bbeta"][:], bb).then_inc(weights_in, 16)
            sp.wait_ge(consts, 3)
            sp.dma_start(rows[0:E, :], A["L0_ffn_ln_g"]).then_inc(placed, 16)
            sp.dma_start(rows[E:2 * E, :], A["L0_ffn_ln_b"]).then_inc(placed, 16)
            sp.dma_start(rows[2 * E:2 * E + NB1, :],
                         A["L0_ffn_b1"].rearrange("e (f p) -> (e f) p", p=P)).then_inc(placed, 16)
            wo = A["L1_ffn_wo"].rearrange("(g j d) n -> j d g n", j=G, d=HD)
            for j in range(G):
                sp.dma_start(M["wop1"][32 * j:32 * j + HD, :, :], wo[j]).then_inc(placed, 16)
            sp.wait_ge(placed, 16 * (G + 3))

        @block.gpsimd
        def _(pool):
            ch = Chain(pool, pool_chain)
            pool.memset(M["wop1"][:], 0.0).then_inc(consts, 1)
            pool.memset(wo_sp[:], 0.0).then_inc(consts, 1)
            pool.memset(rows[:], 0.0).then_inc(consts, 1)
            pool.memset(M["minus_half"][:], -0.5).then_inc(consts, 1)
            for t in (M["identF"], M["identB"], M["row0"], M["first"], M["band"], M["before"]):
                ch.mark(pool.memset(t[:], 0.0))
            ch.mark(pool.memset(group[:], 1.0))
            ch.settle()
            for t in (M["identF"], M["identB"]):
                ch.mark(pool.affine_select(out=t[:], in_=t[:], compare_op=ALU.not_equal, fill=1.0, base=0,
                                           pattern=[[-1, P]], channel_multiplier=1))
            bf = M["before"][:]
            ch.mark(pool.affine_select(out=bf, in_=bf, compare_op=ALU.is_ge, fill=1.0, base=0,
                                       pattern=[[-1, E], [1, E]], channel_multiplier=0))
            g3 = group[:].rearrange("p (h d) -> p h d", d=HD)
            ch.do(pool.affine_select(out=g3, in_=g3, compare_op=ALU.is_ge, fill=0.0, base=0,
                                     pattern=[[-HD, H], [0, HD]], channel_multiplier=1))
            ch.do(pool.affine_select(out=g3, in_=g3, compare_op=ALU.is_ge, fill=0.0, base=HD - 1,
                                     pattern=[[HD, H], [0, HD]], channel_multiplier=-1))
            low = lambda ap: pool.affine_select(out=ap, in_=ap, compare_op=ALU.is_ge, fill=MASKED, base=0,
                                                pattern=[[1, P]], channel_multiplier=-1)
            high = lambda ap: pool.affine_select(out=ap, in_=ap, compare_op=ALU.is_ge, fill=MASKED, base=0,
                                                 pattern=[[-1, P]], channel_multiplier=1)
            ch.mark(low(M["band"][:, 0:P]))
            ch.mark(high(M["band"][:, 2 * P:3 * P]))
            ch.mark(low(M["first"][:, 0:P]))
            ch.mark(high(M["first"][:, 2 * P:3 * P]))
            ch.mark(high(M["row0"][:, P:2 * P]))
            ch.mark(pool.memset(M["row0"][:, 2 * P:], MASKED))
            ch.settle()
            pool.memset(M["first"][:, 0:1], 0.0).then_inc(masks, 1)
            pool.memset(M["row0"][0:1, :], 0.0).then_inc(masks, 1)

        @block.scalar
        def _(act):
            XT = M["XT"].rearrange("p b (k c) -> p (b k) c", c=HALF)
            for c in range(CH):
                act.wait_ge(x_flipped, c + 1)
                act.activation(XT[:, c], pt[:, BANKS + c % BANKS, :], ACT.Copy).then_inc(xt_kept, 1)

        @block.vector
        def _(dve):
            dve.wait_ge(weights_in, 16 * NLOAD)
            dve.wait_ge(consts, 3)
            dve.tensor_copy(wo_sp[:, :, :, 0:HD],
                            wo_nat[:].rearrange("p (g j d) -> p g j d", g=UPB, j=G)).then_inc(spread, 1)
            dve.tensor_copy(M["w1d"][:, 3, :].rearrange("p (h d) -> p h d", d=HD),
                            bc_free(wbeta[:], HD)).then_inc(spread, 1)
            for n in range(2):
                dve.tensor_copy(M["w1a"][:, n, :].rearrange("p (g d j) -> p g j d", g=UPB, j=G),
                                wqk[:, n, :].rearrange("p (g j d) -> p g j d", g=UPB, j=G)).then_inc(spread, 1)
            dve.wait_ge(flipped, 1)
            for n in range(2):
                dve.tensor_copy(M["w0a"][:, n, :].rearrange("p (g d j) -> p g j d", g=UPB, j=G),
                                pt[:, 0, n * P:(n + 1) * P].rearrange("p (g j d) -> p g j d", g=UPB, j=G)).then_inc(kept, 1)
            dve.tensor_copy(M["w0a"][:, 2, :], pt[:, 0, 2 * P:3 * P]).then_inc(kept, 1)
            dve.tensor_copy(qvT[:], pt[:, 1, 0:2 * P].rearrange("p (n c) -> p n c", c=P)).then_inc(kept, 1)
            dve.tensor_copy(M["wop0"][:], pt[:, 2, :].rearrange("p (n c) -> p n c", c=P)).then_inc(kept, 1)
            dve.wait_ge(folded, 1)
            dve.tensor_copy(M["w1d"][:, 0, :], pt[:, 3, 0:P]).then_inc(kept, 1)
            dve.tensor_copy(M["w1d"][:, 2, :], pt[:, 3, P:2 * P]).then_inc(kept, 1)
            dve.tensor_copy(M["cols"][:], pt[:, 3, 2 * P:2 * P + 2 * E + NB1]).then_inc(kept, 1)

        @block.tensor
        def _(pe):
            pe.wait_ge(pool_chain, 12)
            pe.wait_ge(x_in, 16 * B)
            for c in range(CH):
                if c >= BANKS:
                    pe.wait_ge(xt_kept, c - BANKS + 1)
                for t in range(CT):
                    tile = c * CT + t
                    last = pe.transpose(pt[:, BANKS + c % BANKS, t * P:(t + 1) * P],
                                        M["X"][:, tile // NT, tile % NT, :], M["identF"][:])
                last.then_inc(x_flipped, 1)
            pe.wait_ge(weights_in, 16 * NLOAD)
            pe.wait_ge(spread, 4)
            for n in range(3):
                pe.transpose(pt[:, 0, n * P:(n + 1) * P], flip[:, n, :], M["identF"][:])
            for n in range(2):
                pe.transpose(pt[:, 1, n * P:(n + 1) * P], flip[:, 3 + n, :], M["identF"][:])
            for g in range(UPB):
                last = pe.transpose(pt[:, 2, g * P:(g + 1) * P], wo_sp[:, g].rearrange("p j c -> p (j c)"),
                                    M["identF"][:])
            last.then_inc(flipped, 1)
            pe.wait_ge(kept, 5)
            pe.wait_ge(placed, 16 * (G + 3))
            pe.transpose(pt[:, 3, 2 * P:3 * P], rows[:], M["identF"][:])
            for n in range(2):
                last = pe.matmul(pt[:, 3, n * P:(n + 1) * P], qvT[:, n, :], group[:], start=True, stop=True)
            last.then_inc(folded, 1)


class AttentionInputs:

    NBUF = 3
    QK_LOADS = 16 * (PARTS + 2)

    def __init__(self, nc, M, ctx, name):
        sb = lambda n, shape, dt=F32: ctx.enter_context(nc.sbuf_tensor(f"{name}_{n}", shape, dt))
        sem = lambda n: new_semaphore(nc, M, f"{name}_{n}")
        n = self.NBUF
        self.Q = [sb(f"q{i}", [KMAX, G, T], BF16) for i in range(n)]
        self.K = [sb(f"k{i}", [KMAX, G, T], BF16) for i in range(n)]
        self.vu = [sb(f"vu{i}", [P, NT, G, HD + 1]) for i in range(n)]
        self.zero3 = sb("zero3", [PARTS, T], BF16)
        self.qk_in = [sem(f"qk_in{i}") for i in range(n)]
        self.v_in = [sem(f"v_in{i}") for i in range(n)]
        self.cleaned = sem("cleaned")
        self.v9 = M["v9"]
        self.qparts = M["parts"][0].rearrange("b g i (d h) t -> (b g) i d (h t)", d=HD)
        self.kparts = M["parts"][1].rearrange("b g i (d h) t -> (b g) (i d) (h t)", d=HD)

    def clean(self, pool):
        pool.memset(self.zero3[:], 0.0).then_inc(self.cleaned, 1)
        pool.wait_ge(self.cleaned, 1)
        for q, k in zip(self.Q, self.K):
            pool.memset(q[64:96], 0.0).then_inc(self.cleaned, 1)
            pool.memset(k[64:96], 1.0).then_inc(self.cleaned, 1)

    def load(self, sp, v, s):
        flat = lambda t, a, b: t[a:b].rearrange("r h t -> r (h t)")
        for i in range(PARTS):
            sp.dma_start(flat(self.Q[s], PARTS * i * HD, PARTS * (i + 1) * HD),
                         self.qparts[v, i].unsqueeze(0).broadcast_to([PARTS, HD, G * T])).then_inc(self.qk_in[s], 16)
        sp.dma_start(flat(self.K[s], 0, KROWS),
                     self.kparts[v].unsqueeze(0).broadcast_to([PARTS, PARTS * HD, G * T])).then_inc(self.qk_in[s], 16)
        sp.dma_start(self.Q[s][KROWS:KROWS + PARTS],
                     self.zero3[:].unsqueeze(1).broadcast_to([PARTS, G, T])).then_inc(self.qk_in[s], 16)
        sp.dma_start(self.vu[s][:], self.v9[v]).then_inc(self.v_in[s], 16)


def project_qkv(nc, M, name, src, w, IN):
    with ExitStack() as ctx:
        sem = lambda n: new_semaphore(nc, M, f"{name}_{n}")
        sb = lambda n, shape, dt=F32: ctx.enter_context(nc.sbuf_tensor(f"{name}_{n}", shape, dt))
        ps = lambda n: ctx.enter_context(nc.psum_tensor(f"{name}_{n}", [P, T], F32))
        prod = [ps("pq"), ps("pk")]
        pv, pvt = ps("pv"), ps("pvt")
        parts = [sb("qparts", [P, PARTS, T], BF16), sb("kparts", [P, PARTS, T], BF16)]
        rest = [sb("qrest", [P, T]), sb("krest", [P, T])]
        vT = sb("vT", [P, T])
        v9 = sb("v9", [P, UPB, NT, G, HD + 1])
        projected, first, second, third = sem("projected"), sem("first"), sem("second"), sem("third")
        rest1 = sem("rest1")
        v_ready, v_kept, v_flipped, v_stored, parts_out = (sem("v_ready"), sem("v_kept"), sem("v_flipped"),
                                                           sem("v_stored"), sem("parts_out"))
        v_out = sem("v_out")
        block = ctx.enter_context(nc.Block())

        @block.gpsimd
        def _(pool):
            pool.memset(v9[:], 1.0).then_inc(v_out, 16)
            pool.wait_ge(v_out, 16)
            IN.clean(pool)

        @block.tensor
        def _(pe):
            with pe.Fori(0, B) as b:
                pe.wait_ge(v_kept, b + 1)
                for half in range(2):
                    c = slice(half * HALF, (half + 1) * HALF)
                    last = pe.matmul(pv[:, c], w[:, 2, :], src[:, b, c], start=True, stop=True)
                last.then_inc(v_ready, 1)
                for n in range(2):
                    pe.wait_ge(rest1, 2 * b + n + 1)
                    for half in range(2):
                        c = slice(half * HALF, (half + 1) * HALF)
                        last = pe.matmul(prod[n][:, c], w[:, n, :], src[:, b, c], start=True, stop=True)
                    last.then_inc(projected, 1)
                pe.wait_ge(v_kept, b + 2)
                pe.wait_ge(v_stored, b + 1)
                for t in range(NT):
                    c = slice(t * P, (t + 1) * P)
                    last = pe.transpose(pvt[:, c], vT[:, c], M["identF"][:])
                last.then_inc(v_flipped, 1)

        @block.scalar
        def _(act):
            act.sem_inc(v_kept, 1)
            with act.Fori(0, B) as b:
                act.wait_ge(v_ready, b + 1)
                act.wait_ge(v_flipped, b + 1)
                act.activation(vT[:], pv[:], ACT.Copy).then_inc(v_kept, 1)
                for n in range(2):
                    act.wait_ge(projected, 2 * b + n + 1)
                    act.wait_ge(parts_out, 32 * PARTS * b + 1)
                    act.activation(parts[n][:, 0, :], prod[n][:], ACT.Copy).then_inc(first, 1)
                for n in range(2):
                    act.wait_ge(rest1, 2 * b + n + 3)
                    act.activation(parts[n][:, 1, :], rest[n][:], ACT.Copy).then_inc(second, 1)

        @block.vector
        def _(dve):
            dve.sem_inc(rest1, 2)
            dve.sem_inc(v_stored, 1)
            dve.sem_inc(third, 1)
            with dve.Fori(0, B) as b:
                for n in range(2):
                    dve.wait_ge(first, 2 * b + n + 1)
                    if n == 0:
                        dve.wait_ge(third, 2 * b + 1)
                    dve.tensor_tensor(rest[n][:], prod[n][:], parts[n][:, 0, :], ALU.subtract).then_inc(rest1, 1)
                for n in range(2):
                    dve.wait_ge(second, 2 * b + n + 1)
                    dve.tensor_tensor(parts[n][:, 2, :], rest[n][:], parts[n][:, 1, :],
                                      ALU.subtract).then_inc(third, 1)
                dve.wait_ge(v_flipped, b + 2)
                dve.wait_ge(v_out, b * 16 + 16)
                v = pvt[:].rearrange("p (t g j d) -> p g t j d", t=NT, g=UPB, j=G)
                for g in range(UPB):
                    last = dve.tensor_copy(v9[:, g, :, :, 0:HD], v[:, g])
                last.then_inc(v_stored, 1)

        @block.sync
        def _(sp):
            sp.sem_inc(parts_out, 1)
            sp.sem_inc(v_flipped, 1)

            def store(b):
                for n in range(2):
                    sp.wait_ge(third, 2 * b + n + 2)
                    apart(sp, M["passed"])
                    for i in range(PARTS):
                        sp.dma_start(M["parts"].rearrange("n b g i r t -> n b i g r t")[n, b, i],
                                     parts[n][:, i, :]).then_inc(parts_out, 16)
                sp.wait_ge(v_stored, b + 2)
                apart(sp, M["passed"])
                sp.dma_start(M["v9"].rearrange("(b g) p t j d -> b p g (t j d)", g=UPB)[b],
                             v9[:].rearrange("p g t j d -> p g (t j d)")).then_inc(v_out, 16)

            store(0)
            sp.wait_ge(parts_out, 32 * PARTS + 1)
            sp.wait_ge(v_out, 32)
            with sp.Fori(1, B - 1) as b:
                store(b)
            sp.wait_ge(IN.cleaned, 3)
            IN.load(sp, 0, 0)
            store(B - 1)
            sp.wait_ge(IN.cleaned, 2 * IN.NBUF + 1)
            sp.wait_ge(parts_out, 32 * PARTS * B + 1)
            sp.wait_ge(v_out, 16 * B + 16)


def attend(nc, M, name, segments, IN):
    with ExitStack() as ctx:
        sem = lambda n: new_semaphore(nc, M, f"{name}_{n}")
        sb = lambda n, shape, dt=F32: ctx.enter_context(nc.sbuf_tensor(f"{name}_{n}", shape, dt))
        NBUF, QK_LOADS = IN.NBUF, IN.QK_LOADS
        Q, K, vu, qk_in, v_in = IN.Q, IN.K, IN.vu, IN.qk_in, IN.v_in
        negmax = [sb(f"negmax{i}", [P, P]) for i in range(NBUF)]
        mparts = sb("mparts", [32, PARTS, P], BF16)
        mrest = sb("mrest", [32, P])
        prob = sb("prob", [P, 2, G, T])
        warm = sb("warm", [P, 2])
        sums, recip = sb("sums", [P, 32]), sb("recip", [P, T])
        one = [ctx.enter_context(nc.psum_tensor(f"{name}_one{i}", [P, T], F32)) for i in range(2)]
        st = ctx.enter_context(nc.psum_tensor(f"{name}_st", [P, 2, HALF], F32))
        o = ctx.enter_context(nc.psum_tensor(f"{name}_o", [P, T], F32))
        clean = sem("clean")
        one_ready, one_free = sem("one_ready"), sem("one_free")
        max_split, max_in, split_chain = sem("max_split"), sem("max_in"), sem("split_chain")
        st_ready, prob_ready, prob_free = sem("st_ready"), sem("prob_ready"), sem("prob_free")
        o_kept, o_done, sums_in, inverted = sem("o_kept"), sem("o_done"), sem("sums_in"), sem("inverted")
        o_half = sem("o_half")
        rsum_out, recip_in, recip_clean = sem("rsum_out"), sem("recip_in"), sem("recip_clean")
        block = ctx.enter_context(nc.Block())

        ITEMS = G * NT
        ONE = ITEMS + 2
        wide = [len([s for s in row if s[2] > 1]) for row in segments]
        halved = all(w == 2 for w in wide)
        LOOPS = NU // NBUF - 1
        STEPS = G * sum(wide)

        def width(r):
            return sum(s[2] for s in segments[r])

        def pieces(r):
            if wide[r] == 2:
                return [(s[0], s[2], [s]) for s in segments[r]]
            return [(0, width(r), segments[r])]

        def scores(pe, dst, left, right, j, r, segs, at):
            for c0, t0, n, masks in segs:
                c = c0 - at
                last = pe.matmul(dst[:, c:c + n], left[:, j, r * P:(r + 1) * P], right[:, j, t0:t0 + n],
                                 start=True, stop=not masks, skip_group_check=True)
                for m, (first, cols, mask, m0) in enumerate(masks):
                    last = pe.matmul(dst[:, c + first:c + first + cols], M["identB"][:], M[mask][:, m0:m0 + cols],
                                     start=False, stop=m == len(masks) - 1, skip_group_check=True)
            return last

        def stage1(pe, buf, k, n, parity, half=None):
            j, r = divmod(k, NT)
            if half != 1:
                pe.wait_ge(one_free, n + 1)
            segs = segments[r] if half is None else segments[r][half:half + 1]
            last = scores(pe, one[parity], Q[buf], K[buf], j, r, segs, 0)
            if half != 0:
                last.then_inc(one_ready, 1)

        def flip_max(pe, buf, n, parity):
            pe.wait_ge(one_free, n + 2)
            pe.transpose(one[parity][:, 0:P], negmax[buf][:], M["identF"][:]).then_inc(one_ready, 2)

        def values(pe, buf, r, part):
            runs = []
            for c0, t0, n, _ in segments[r]:
                cut = min(max(HALF - t0, 0), n)
                if cut:
                    runs.append((c0, t0, cut))
                if n - cut:
                    runs.append((c0 + cut, t0 + cut, n - cut))
            for c0, t0, n in (runs[:1], runs[1:])[part]:
                for j in range(G):
                    last = pe.matmul(o[32 * j:32 * j + HD + 1, t0:t0 + n], vu[buf][:, r, j, :],
                                     prob[:, r % 2, j, c0:c0 + n], start=r == 0, stop=r == NT - 1,
                                     skip_group_check=True)
            if part == (1 if len(runs) > 1 else 0):
                last.then_inc(prob_free, 1)
            elif r == NT - 1:
                last.then_inc(o_half, 1)

        AHEAD = (4 if halved else 7)
        FLIP = ITEMS - AHEAD - 1
        EXTRA = lambda item: item >= (8 if halved else 3)
        loaded = lambda i, m: i + m // NBUF + 1

        def pe_unit(pe, i, m):
            u = NBUF * i + m
            left = NU - 1 - u if isinstance(u, int) else 2
            buf = m % NBUF
            base = ONE * u + ONE
            issued = 2 * AHEAD

            def issue(upto):
                nonlocal issued
                while issued < upto:
                    nxt = 1 if issued < 2 * ITEMS else 2
                    k = issued // 2 if nxt == 1 else issued // 2 - ITEMS
                    if nxt <= left:
                        stage1(pe, (buf + nxt) % NBUF, k, base + (nxt - 1) * ONE + k, k % 2,
                               issued % 2 if halved else None)
                    issued += 1 if halved else 2

            pe.wait_ge(max_in, 16 * PARTS * u + 16 * PARTS)
            step = 0
            for item in range(ITEMS):
                r, j = divmod(item, G)
                due = min(AHEAD + item + 1 + EXTRA(item), ITEMS) if item <= FLIP else AHEAD + 1 + item
                limit = 2 * ITEMS if item <= FLIP else 2 * ITEMS + 2 * AHEAD
                for n_piece, (c0, n, segs) in enumerate(pieces(r)):
                    pe.wait_ge(prob_ready, STEPS * u + step + 1)
                    last = scores(pe, st[:, step % 2, :], K[buf], Q[buf], j, r, segs, c0)
                    last.then_inc(st_ready, 1)
                    step += 1
                    if halved:
                        issue(min(2 * due + ((-1, 1), (0, 0))[j % 2][n_piece], limit))
                    elif n_piece == 0:
                        issue(min(2 * due, limit))
                if item == FLIP:
                    if left:
                        flip_max(pe, (buf + 1) % NBUF, base + ITEMS, 0)
                    if left > 1:
                        pe.wait_ge(qk_in[(buf + 2) % NBUF], QK_LOADS * loaded(i, m + 2))
                if j % 2 == 1 and r == 0 and m:
                    if j == 1:
                        pe.wait_ge(prob_ready, STEPS * u + 2)
                    values(pe, (buf - 1) % NBUF, NT - 1, j // 2)
                if j % 2 == 1 and r >= 1:
                    if r == 1 and j == 1:
                        pe.wait_ge(o_kept, 2 * u + 2)
                        pe.wait_ge(v_in[buf], 16 * loaded(i, m))
                    if j == 1:
                        pe.wait_ge(prob_ready, STEPS * u + G * sum(wide[:r]) + 2)
                    values(pe, buf, r - 1, j // 2)

        @block.tensor
        def _(pe):
            pe.wait_ge(qk_in[0], QK_LOADS)
            pe.wait_ge(clean, NBUF)
            for k in range(ITEMS):
                stage1(pe, 0, k, k, k % 2)
            flip_max(pe, 0, ITEMS, 0)
            pe.wait_ge(qk_in[1], QK_LOADS)
            for k in range(AHEAD):
                stage1(pe, 1, k, ONE + k, k % 2)
            pe.wait_ge(clean, NBUF + 1)
            pe_unit(pe, 0, 0)
            with pe.Fori(0, LOOPS) as i:
                for m in range(1, 1 + NBUF):
                    pe_unit(pe, i, m)
            for m in range(1, 1 + NBUF):
                pe_unit(pe, LOOPS, m)
            pe.wait_ge(prob_ready, STEPS * NU + 2)
            for part in range(2):
                values(pe, (NU - 1) % NBUF, NT - 1, part)

        @block.scalar
        def _(act):
            act.activation(warm[:], M["norm"][:], ACT.Exp)
            act.sem_inc(prob_ready, 2)
            act.sem_inc(o_kept, 2)

            def exponentials(u, item):
                r, j = divmod(item, G)
                step = G * sum(wide[:r]) + j * wide[r]
                if j == 0:
                    act.wait_ge(prob_free, u * NT + r + 1)
                for c0, n, _ in pieces(r):
                    act.wait_ge(st_ready, u * STEPS + step + 1)
                    act.activation(prob[:, r % 2, j, c0:c0 + n], st[:, step % 2, 0:n], ACT.Exp,
                                   scale=SCALE).then_inc(prob_ready, 1)
                    step += 1

            def keep(u, n):
                if n == 0:
                    act.wait_ge(o_half, u + 1)
                else:
                    act.wait_ge(prob_free, u * NT + NT + 2)
                c = slice(0, HALF) if halved == (n == 0) else slice(HALF, T)
                act.activation(M["OT"][:, u, c], o[:, c], ACT.Copy).then_inc(o_kept, 1)

            START = G + 1
            for item in range(START):
                exponentials(0, item)
            with act.Fori(0, NU - 1) as u:
                for item in range(START, ITEMS):
                    exponentials(u, item)
                for item in range(START):
                    exponentials(u + 1, item)
                    if item == G // 2:
                        keep(u, 0)
                keep(u, 1)
            for item in range(START, ITEMS):
                exponentials(NU - 1, item)
            for n in range(2):
                keep(NU - 1, n)

        @block.vector
        def _(dve):
            for t in negmax:
                dve.memset(t[:], 0.0).then_inc(clean, 1)
            dve.sem_inc(one_free, 2)
            dve.wait_ge(clean, NBUF)

            def invert(u):
                dve.wait_ge(sums_in, u * 16 * G + 16 * G)
                dve.reciprocal(sums[:], sums[:]).then_inc(inverted, 1)

            def maxima(buf, n0, ended=None):
                for k in range(ITEMS):
                    j, r = divmod(k, NT)
                    dve.wait_ge(one_ready, n0 + k + 1)
                    dve.tensor_reduce(negmax[buf][:, k:k + 1], one[k % 2][:, 0:width(r)], AX.X,
                                      ALU.max, negate=True).then_inc(one_free, 1)
                    if k == ITEMS - 8 and ended is not None:
                        invert(ended)

            def split_max(v, n):
                chain = Chain(dve, split_chain, v * 3)
                dve.wait_ge(one_ready, n + 2)
                m = one[0][0:32, 0:P]
                chain.do(dve.tensor_copy(mparts[:, 0, :], m))
                chain.do(dve.tensor_tensor(mrest[:], m, mparts[:, 0, :], ALU.subtract))
                dve.sem_inc(one_free, 2)
                chain.do(dve.tensor_copy(mparts[:, 1, :], mrest[:]))
                dve.tensor_tensor(mparts[:, 2, :], mrest[:], mparts[:, 1, :], ALU.subtract).then_inc(max_split, 1)

            def unit(u, buf, ended):
                maxima(buf, u * ONE + ONE, ended)
                dve.wait_ge(max_in, u * 16 * PARTS + 16 * PARTS)
                split_max(u + 1, u * ONE + ONE + ITEMS)

            maxima(0, 0)
            split_max(0, ITEMS)
            dve.memset(o[:], 0.0).then_inc(clean, 1)
            unit(0, 1, None)
            with dve.Fori(0, LOOPS) as i:
                for m in range(1, 1 + NBUF):
                    u = i * NBUF + m
                    unit(u, (m + 1) % NBUF, u - 1)
            for u in range(LOOPS * NBUF + 1, NU - 1):
                unit(u, (u + 1) % NBUF, u - 1)
            for u in (NU - 2, NU - 1):
                invert(u)

        @block.gpsimd
        def _(pool):
            pool.sem_inc(prob_free, 2)
            pool.memset(recip[:], 1.0).then_inc(recip_clean, 1)
            with pool.Fori(0, NU) as u:
                pool.wait_ge(recip_in, u * 16 * G + 16 * G)
                apart(pool, M["passed"])
                pool.tensor_tensor(M["OT"][:, u, :], M["OT"][:, u, :], recip[:], ALU.mult).then_inc(o_done, 1)
            pool.wait_ge(o_done, NU + 1)

        @block.sync
        def _(sp):
            def send_max(v, s):
                sp.wait_ge(max_split, v + 1)
                for i in range(PARTS):
                    row = Q[s][KROWS + i:KROWS + i + 1].rearrange("o h (r a) -> o (h r) a", a=P)
                    sp.dma_start(row, mparts[:, i, :]).then_inc(max_in, 16)

            def fetch_sums(u):
                sp.wait_ge(o_kept, 2 * u + 4)
                apart(sp, M["passed"])
                for j in range(G):
                    row = M["OT"][32 * j + HD:32 * j + HD + 1, u, :].rearrange("o (p c) -> o p c", c=32)
                    sp.dma_start(sums[32 * j:32 * j + 32, :], row).then_inc(sums_in, 16)

            def spread_inverses(u):
                sp.wait_ge(inverted, u + 1)
                apart(sp, M["passed"])
                sp.dma_start(M["rsum"][u].rearrange("j (p c) -> (j p) c", c=32), sums[:]).then_inc(rsum_out, 16)
                sp.wait_ge(rsum_out, u * 16 + 16)
                sp.wait_ge(o_done, u + 1)
                apart(sp, M["passed"])
                for j in range(G):
                    sp.dma_start(recip[32 * j:32 * j + HD, :],
                                 M["rsum"][u, j].unsqueeze(0).broadcast_to([HD, T])).then_inc(recip_in, 16)

            for v in range(1, NBUF):
                IN.load(sp, v, v)
            send_max(0, 0)
            send_max(1, 1)
            sp.wait_ge(prob_free, NT + 2)
            fetch_sums(0)
            IN.load(sp, NBUF, 0)
            sp.wait_ge(recip_clean, 1)
            sp.sem_inc(o_done, 1)
            with sp.Fori(0, LOOPS) as i:
                for m in range(1, 1 + NBUF):
                    u = i * NBUF + m
                    send_max(u + 1, (m + 1) % NBUF)
                    spread_inverses(u - 1)
                    sp.wait_ge(prob_free, u * NT + NT + 2)
                    fetch_sums(u)
                    IN.load(sp, u + NBUF, m % NBUF)
            for u in range(LOOPS * NBUF + 1, NU):
                if u + 1 < NU:
                    send_max(u + 1, (u + 1) % NBUF)
                spread_inverses(u - 1)
                fetch_sums(u)
            spread_inverses(NU - 1)


def project_out(nc, M, name, wop, last_layer, W):
    with ExitStack() as ctx:
        sem = lambda n: new_semaphore(nc, M, f"{name}_{n}")
        sb = lambda n, shape, dt=F32: ctx.enter_context(nc.sbuf_tensor(f"{name}_{n}", shape, dt))
        ps = lambda n: ctx.enter_context(nc.psum_tensor(f"{name}_{n}", [P, T], F32))
        pp, pt, px, ph = ps("pp"), ps("pt"), ps("px"), ps("ph")
        aT, xs = sb("aT", [P, T]), sb("xs", [P, T])
        y, xn, hn = (sb(n, [P, NT, P]) for n in ("y", "xn", "hn"))
        stats, mv = sb("stats", [P, NT, 6]), sb("mv", [P, NT, 2])
        ms, tmp, rstd = sb("ms", [P, NT]), sb("tmp", [P, NT]), sb("rstd", [P, NT])
        projected, a_kept, flipped, y_made = sem("projected"), sem("a_kept"), sem("flipped"), sem("y_made")
        stats_ready, rstd_ready, chain_d, chain_p = sem("stats_ready"), sem("rstd_ready"), sem("cd"), sem("cp")
        x_ready, h_ready, x_flipped, h_flipped = sem("x_ready"), sem("h_ready"), sem("x_flipped"), sem("h_flipped")
        xt_kept, ht_kept = sem("xt_kept"), sem("ht_kept")
        router_in, judged, logits_kept = sem("router_in"), sem("judged"), sem("logits_kept")
        logits = M["logits"][:].rearrange("p (b n) e -> p b (n e)", b=B)
        block = ctx.enter_context(nc.Block())
        halves = [slice(0, HALF), slice(HALF, T)]

        @block.sync
        def _(sp):
            for dst, src in W["loads"]:
                sp.dma_start(dst, src).then_inc(W["w_in"], 16)

        @block.tensor
        def _(pe):
            def project(b):
                pe.wait_ge(a_kept, b + 1)
                for c in halves:
                    for g in range(UPB):
                        last = pe.matmul(pp[:, c], wop[:, g, :], M["OT"][:, b * UPB + g, c],
                                         start=g == 0, stop=g == UPB - 1)
                last.then_inc(projected, 1)

            def flip_a(b):
                pe.wait_ge(a_kept, b + 2)
                pe.wait_ge(y_made, b + 1)
                for t in range(NT):
                    last = pe.transpose(pt[:, t * P:(t + 1) * P], aT[:, t * P:(t + 1) * P], M["identF"][:])
                last.then_inc(flipped, 1)

            def flip_x(b):
                pe.wait_ge(x_ready, b + 1)
                pe.wait_ge(xt_kept, b + 1)
                pe.wait_ge(logits_kept, b + 1)
                for t in range(NT):
                    last = pe.transpose(px[:, t * P:(t + 1) * P], xn[:, t, :], M["identF"][:])
                last.then_inc(x_flipped, 1)

            def flip_h(b):
                pe.wait_ge(h_ready, b + 1)
                pe.wait_ge(ht_kept, b + 1)
                for t in range(NT):
                    last = pe.transpose(ph[:, t * P:(t + 1) * P], hn[:, t, :], M["identF"][:])
                last.then_inc(h_flipped, 1)

            def judge(b):
                pe.wait_ge(router_in, b + 1)
                pe.wait_ge(logits_kept, b + 1)
                for t in range(NT):
                    last = pe.matmul(px[:, t * E:(t + 1) * E], xs[:, t * P:(t + 1) * P],
                                     M["rw"][:, 1 if last_layer else 0, :], start=True, stop=True)
                last.then_inc(judged, 1)

            project(0)
            flip_a(0)
            with pe.Fori(1, B) as b:
                project(b)
                if not last_layer:
                    flip_x(b - 1)
                flip_a(b)
                flip_h(b - 1)
                judge(b - 1)
            if not last_layer:
                flip_x(B - 1)
            flip_h(B - 1)
            judge(B - 1)

        @block.scalar
        def _(act):
            act.sem_inc(a_kept, 1)
            act.sem_inc(xt_kept, 1)
            act.sem_inc(ht_kept, 1)
            act.sem_inc(flipped, 1)
            act.sem_inc(logits_kept, 1)
            act.sem_inc(judged, 1)

            def keep_a(b):
                act.wait_ge(projected, b + 1)
                act.wait_ge(flipped, b + 1)
                act.activation(aT[:], pp[:], ACT.Copy).then_inc(a_kept, 1)

            def keep_xh(b):
                if not last_layer:
                    act.wait_ge(x_flipped, b + 1)
                    act.activation(M["XT"][:, b, :], px[:], ACT.Copy).then_inc(xt_kept, 1)
                    act.wait_ge(judged, b + 1)
                    act.activation(xs[:], px[:], ACT.Copy).then_inc(router_in, 1)
                act.wait_ge(h_flipped, b + 1)
                if last_layer:
                    act.wait_ge(judged, b + 1)
                    act.activation(xs[:], ph[:], ACT.Copy, scale=M["norm"][:, 1:2]).then_inc(router_in, 1)
                    act.activation(M["HT"][:, b, :], ph[:], ACT.Copy, scale=M["norm"][:, 1:2]).then_inc(ht_kept, 1)
                else:
                    act.activation(M["HT"][:, b, :], ph[:], ACT.Copy).then_inc(ht_kept, 1)
                act.wait_ge(judged, b + 2)
                act.activation(logits[:, b], px[:, 0:NT * E], ACT.Copy).then_inc(logits_kept, 1)

            keep_a(0)
            with act.Fori(1, B) as b:
                keep_a(b)
                keep_xh(b - 1)
            keep_xh(B - 1)

        @block.vector
        def _(dve):
            dve.sem_inc(y_made, 1)
            PER = 4 if last_layer else 7
            with dve.Fori(0, B) as b:
                ch = Chain(dve, chain_d, b * PER)
                dve.wait_ge(flipped, b + 2)
                ptt = pt[:].rearrange("p (t c) -> p t c", c=P)
                dve.tensor_tensor(y[:], ptt, M["X"][:, b], ALU.add).then_inc(y_made, 1)
                dve.wait_ge(y_made, b + 2)
                if last_layer:
                    dve.wait_ge(ht_kept, b + 1)
                    ch.do(rms_normalise(dve, ch, hn, y, xn[:], ms[:], rstd, NT, stats_ready, rstd_ready, b))
                    dve.sem_inc(h_ready, 1)
                    ch.do(dve.tensor_tensor(M["X"][:, b], M["X"][:, b], y[:], ALU.add))
                else:
                    dve.wait_ge(xt_kept, b + 1)
                    ch.do(normalise(dve, ch, xn, y, stats, mv, rstd, NT, stats_ready, rstd_ready, b * 2, M["passed"]))
                    dve.sem_inc(x_ready, 1)
                    dve.wait_ge(ht_kept, b + 1)
                    ch.do(normalise(dve, ch, hn, xn, stats, mv, rstd, NT, stats_ready, rstd_ready, b * 2 + 1, M["passed"],
                                    lambda: ch.mark(dve.tensor_copy(M["X"][:, b], xn[:]))))
                    dve.sem_inc(h_ready, 1)
                assert ch.k == PER

        @block.gpsimd
        def _(pool):
            with pool.Fori(0, B) as b:
                if last_layer:
                    make_rstd(pool, chain_p, rstd[:], ms[:], tmp[:], M["minus_half"][:, 0:NT],
                              1.0 / P, RMS_EPS, NT, stats_ready, rstd_ready, b, M["passed"])
                else:
                    for n in range(2):
                        make_rstd(pool, chain_p, rstd[:], mv[:, :, 1], tmp[:],
                                  M["minus_half"][:, 0:NT], 1.0, LN_EPS, NT, stats_ready, rstd_ready, b * 2 + n, M["passed"])


def route(dve, M, R, layer):
    TT = B * NT
    ch = Chain(dve, R["chain"])
    logits, expd, prob, hot, second, best = (M["logits"], R["expd"], R["prob"], R["hot"], R["second"], R["best"])
    if layer == 0:
        ch.do(dve.tensor_tensor(logits[:], logits[:], M["rb"][:].unsqueeze(1).broadcast_to([P, TT, E]), ALU.add))

    def shift(src):
        ch.do(dve.tensor_reduce(R["top"][:], src[:], AX.X, ALU.max))
        dve.tensor_tensor(expd[:], src[:], bc_free(R["top"][:], E), ALU.subtract).then_inc(R["shifted"], 1)

    def divide(dst):
        ch.do(dve.tensor_reduce(R["total"][:], expd[:], AX.X, ALU.add))
        ch.do(dve.reciprocal(R["inv"][:], R["total"][:]))
        ch.do(dve.tensor_tensor(dst, expd[:], bc_free(R["inv"][:], E), ALU.mult))

    def pick(dst, src):
        ch.do(dve.tensor_reduce(R["top"][:], src[:], AX.X, ALU.max))
        ch.do(dve.tensor_tensor(dst[:], src[:], bc_free(R["top"][:], E), ALU.is_equal))
        ch.do(dve.tensor_tensor(dst[:], dst[:], R["order"][:].unsqueeze(1).broadcast_to([P, TT, E]), ALU.mult))
        ch.do(dve.tensor_reduce(R["total"][:], dst[:], AX.X, ALU.max))
        ch.do(dve.tensor_tensor(dst[:], dst[:], bc_free(R["total"][:], E), ALU.is_equal))

    shift(logits)
    ch.do(dve.tensor_reduce(R["order"][:], M["before"][:], AX.X, ALU.add))
    ch.do(dve.tensor_scalar(R["order"][:], R["order"][:], -1.0, float(E), ALU.mult, ALU.add))
    judge = logits
    if layer == 1:
        dve.wait_ge(R["exped"], 1)
        divide(prob[:])
        shift(prob)
        judge = prob
    dve.wait_ge(R["shifted"], 1 + layer)
    pick(hot, judge)
    ch.do(dve.scalar_tensor_tensor(best[:], hot[:], 3.0 * MASKED, judge[:], ALU.mult, ALU.add))
    pick(second, best)
    ch.do(dve.tensor_tensor(hot[:], hot[:], second[:], ALU.add))
    dve.wait_ge(R["exped"], 1 + layer)
    ch.do(dve.tensor_tensor(expd[:], expd[:], hot[:], ALU.mult))
    divide(M["gates"][:])
    ch.do(dve.tensor_reduce(M["gate_sum"][:], M["gates"][:], AX.X, ALU.add))


def expert_weights(nc, A, M, ctx, layer):
    F = A["L0_ffn_W1"].shape[2] if layer == 0 else A["L1_ffn_e_gate"].shape[2]
    NE = E if layer == 0 else E + 1
    FB = F // P
    sb = lambda n, shape: ctx.enter_context(nc.sbuf_tensor(f"moe{layer}_{n}", shape, F32))
    up = sb("up", [P, NE, BANKS, P])
    down = sb("down", [P, NE, FB, P])
    if layer == 0:
        loads = [(up[:, e:e + 2].rearrange("p e f c -> p e (f c)"), A["L0_ffn_W1"][e:e + 2].rearrange("e p f -> p e f"))
                 for e in range(0, E, 2)]
        loads += [(down[:, e:e + 2], A["L0_ffn_W2"][e:e + 2].rearrange("e (f p) n -> p e f n", p=P))
                  for e in range(0, E, 2)]
    else:
        two = lambda n: up[:, 0:E, FB * n:FB * n + FB, :].rearrange("p e f c -> p e (f c)")
        one = lambda n: up[:, E, FB * n:FB * n + FB, :].rearrange("p f c -> p (f c)")
        loads = [(two(0), A["L1_ffn_e_gate"].rearrange("e p f -> p e f")),
                 (two(1), A["L1_ffn_e_up"].rearrange("e p f -> p e f")),
                 (one(0), A["L1_ffn_sh_gate"]), (one(1), A["L1_ffn_sh_up"]),
                 (down[:, 0:E], A["L1_ffn_e_down"].rearrange("e (f p) n -> p e f n", p=P)),
                 (down[:, E], A["L1_ffn_sh_down"].rearrange("(f p) n -> p f n", p=P))]
    return dict(up=up, down=down, loads=loads, w_in=new_semaphore(nc, M, f"moe{layer}_w_in"), NE=NE, FB=FB)


def experts(nc, A, M, name, layer, W, out):
    up, down, w_in, NE, FB = W["up"], W["down"], W["w_in"], W["NE"], W["FB"]
    NB = 2 if layer == 0 else 3
    assert NE % NB == 0
    with ExitStack() as ctx:
        sem = lambda n: new_semaphore(nc, M, f"{name}_{n}")
        sb = lambda n, shape, dt=F32: ctx.enter_context(nc.sbuf_tensor(f"{name}_{n}", shape, dt))
        ps = lambda n, shape: ctx.enter_context(nc.psum_tensor(f"{name}_{n}", shape, F32))
        hidden = sb("hidden", [P, NB, FB, HALF])
        gch = sb("gch", [P, P])
        gsc = sb("gsc", [P, CT])
        acc, y, xn = sb("acc", [P, CT, P]), sb("y", [P, CT, P]), sb("xn", [P, CT, P])
        stats, mv = sb("stats", [P, CT, 6]), sb("mv", [P, CT, 2])
        tmp, rstd = sb("tmp", [P, CT]), sb("rstd", [P, CT])
        pa = ps("pa", [P, BANKS, HALF])
        py = [ps(f"py{i}", [P, CT, P]) for i in range(NB)]
        if layer == 0:
            h = sb("h", [P, 2, HALF])
            gT = sb("gT", [CT * E, P])
            b2p = sb("b2p", [CT * E, CT, P])
            lng, lnb = M["cols"][:, 0:E], M["cols"][:, E:2 * E]
            b1 = M["cols"][:, 2 * E:].rearrange("p (e f) -> p e f", f=BANKS)
            pg, px = ps("pg", [P, CT, P]), ps("px", [P, CT, P])
        else:
            silu = sb("silu", [P, FB, HALF])
        warm = sb("warm", [P, 2])
        R = {n: sb(n, [P, B * NT, E]) for n in ("expd", "prob", "hot", "second", "best")}
        R.update({n: sb(n, [P, B * NT]) for n in ("top", "total", "inv")}, order=sb("order", [P, E]),
                 shifted=sem("shifted"), exped=sem("exped"), chain=sem("route_chain"))
        b2_in, clean, g_staged, g_flipped, g_kept, bias_ready = (sem("b2_in"), sem("clean"), sem("g_staged"),
                                                                 sem("g_flipped"), sem("g_kept"), sem("bias_ready"))
        h_ready, a_ready, a_free, u_free, y_ready, y_free = (sem("h_ready"), sem("a_ready"), sem("a_free"),
                                                             sem("u_free"), sem("y_ready"), sem("y_free"))
        stats_ready, rstd_ready, chain_d, chain_p = sem("stats_ready"), sem("rstd_ready"), sem("cd"), sem("cp")
        x_ready, x_flipped, xt_kept, x_stored = sem("x_ready"), sem("x_flipped"), sem("xt_kept"), sem("x_stored")
        block = ctx.enter_context(nc.Block())

        X = M["X"][:].rearrange("p b (k t) d -> p (b k) t d", t=CT)
        XT = M["XT"].rearrange("p b (k c) -> p (b k) c", c=HALF)
        HT = M["HT"][:].rearrange("p b (k c) -> p (b k) c", c=HALF)
        gates = M["gates"][:].rearrange("p (k t) e -> p k t e", t=CT)
        gate_sum = M["gate_sum"][:].rearrange("p (k t) -> p k t", t=CT)
        out_v = out.rearrange("b (k t p) d -> (b k) p t d", t=CT, p=P)
        W_IN = 16 * len(W["loads"])

        @block.sync
        def _(sp):
            if layer == 0:
                sp.wait_ge(clean, 2)
                for t in range(CT):
                    sp.dma_start(b2p[E * t:E * t + E, t, :], A["L0_ffn_b2"]).then_inc(b2_in, 16)
                sp.wait_ge(b2_in, 16 * CT)
            else:
                with sp.Fori(0, CH) as c:
                    sp.wait_ge(x_ready, c + 1)
                    apart(sp, M["passed"])
                    sp.dma_start(out_v[c], xn[:]).then_inc(x_stored, 16)
                sp.wait_ge(x_stored, 16 * CH + 16)

        @block.gpsimd
        def _(pool):
            pool.memset(gch[:], 0.0).then_inc(clean, 1)
            if layer == 0:
                pool.memset(b2p[:], 0.0).then_inc(clean, 1)
            pool.sem_inc(x_stored, 16)
            with pool.Fori(0, CH) as c:
                make_rstd(pool, chain_p, rstd[:], mv[:, :, 1], tmp[:], M["minus_half"][:, 0:CT],
                          1.0, LN_EPS, CT, stats_ready, rstd_ready, c, M["passed"])
                if layer == 0:
                    pool.wait_ge(x_ready, c + 1)
                    apart(pool, M["passed"])
                    pool.tensor_copy(X[:, c], xn[:]).then_inc(x_stored, 16)

        FREED = FB if layer == 1 else BANKS

        @block.tensor
        def _(pe):
            pe.sem_inc(a_ready, BANKS + 1)
            pe.sem_inc(y_ready, NB)
            pe.wait_ge(w_in, W_IN)
            if layer == 0:
                pe.wait_ge(b2_in, 16 * CT)

            def rise(c, e):
                if layer == 0:
                    pe.wait_ge(h_ready, c * NE + e + 1)
                for f in range(BANKS):
                    if layer == 0:
                        pe.wait_ge(a_free, c * (NE * BANKS) + e * BANKS + f + 1)
                    elif f < FB:
                        pe.wait_ge(a_free, c * (NE * FB) + e * FB + f + 1)
                    else:
                        pe.wait_ge(u_free, c * (NE * FB) + e * FB + f - FB + 1)
                    pe.matmul(pa[:, f, :], up[:, e, f, :], h[:, e % 2, :] if layer == 0 else HT[:, c],
                              start=True, stop=True).then_inc(a_ready, 1)

            def fall(c, e):
                hidden_made = a_free if layer == 0 else u_free
                pe.wait_ge(hidden_made, c * (NE * FREED) + (e + 2) * FREED)
                pe.wait_ge(y_free, c * NE + e + 1)
                for t in range(CT):
                    for f in range(FB):
                        last = pe.matmul(py[e % NB][:, t, :], hidden[:, e % NB, f, t * P:(t + 1) * P],
                                         down[:, e, f, :], start=f == 0, stop=f == FB - 1)
                last.then_inc(y_ready, 1)

            def flip_x(c):
                pe.wait_ge(x_ready, c + 1)
                pe.wait_ge(xt_kept, c + 1)
                for t in range(CT):
                    last = pe.transpose(px[:, t, :], xn[:, t, :], M["identF"][:])
                last.then_inc(x_flipped, 1)

            def chunk(c, first, final):
                for e in range(NE):
                    if e + 1 < NE:
                        rise(c, e + 1)
                    elif not final:
                        rise(c + 1, 0)
                    if layer == 0 and e == 0:
                        pe.wait_ge(g_staged, c * 2 + 2)
                        pe.transpose(pg[:, 0, :], gch[:], M["identF"][:]).then_inc(g_flipped, 1)
                    fall(c, e)
                    if layer == 0 and e == 0:
                        pe.wait_ge(g_kept, c + 1)
                        for t in range(CT):
                            last = pe.matmul(pg[:, t, :], gT[:], b2p[:, t, :], start=True, stop=True)
                        last.then_inc(bias_ready, 1)
                    if layer == 0 and e == 1 and not first:
                        flip_x(c - 1)

            rise(0, 0)
            chunk(0, True, False)
            with pe.Fori(1, CH - 1) as c:
                chunk(c, False, False)
            chunk(CH - 1, False, True)
            if layer == 0:
                flip_x(CH - 1)

        @block.scalar
        def _(act):
            for n in range(1 + layer):
                act.wait_ge(R["shifted"], n + 1)
                act.activation(R["expd"][:], R["expd"][:], ACT.Exp).then_inc(R["exped"], 1)
            act.activation(warm[:], M["norm"][:], ACT.Gelu if layer == 0 else ACT.Silu)
            act.sem_inc(a_free, FREED)
            act.sem_inc(xt_kept, 1)

            def keep_x(c):
                act.wait_ge(x_flipped, c + 1)
                act.activation(XT[:, c], px[:].rearrange("p t d -> p (t d)"), ACT.Copy).then_inc(xt_kept, 1)

            def chunk(c, first):
                for e in range(NE):
                    if layer == 0 and e == 2:
                        act.wait_ge(g_flipped, c + 1)
                        act.activation(gT[:], pg[0:CT * E, 0, :], ACT.Copy).then_inc(g_kept, 1)
                    if layer == 0 and e == 3 and not first:
                        keep_x(c - 1)
                    if layer == 0:
                        act.wait_ge(y_ready, c * NE + e + 1)
                    for f in range(FREED):
                        act.wait_ge(a_ready, c * (NE * BANKS) + e * BANKS + f + 2 + BANKS)
                        if layer == 0:
                            act.activation(hidden[:, e % NB, f, :], pa[:, f, :], ACT.Gelu,
                                           bias=b1[:, e, f:f + 1]).then_inc(a_free, 1)
                        else:
                            act.wait_ge(u_free, c * (NE * FB) + e * FB + f + 1)
                            act.activation(silu[:, f, :], pa[:, f, :], ACT.Silu).then_inc(a_free, 1)

            chunk(0, True)
            with act.Fori(1, CH) as c:
                chunk(c, False)
            if layer == 0:
                keep_x(CH - 1)

        @block.vector
        def _(dve):
            dve.sem_inc(y_free, NB)
            if layer == 1:
                dve.sem_inc(u_free, FB)
            dve.wait_ge(clean, 2 - layer)
            PER = NE + (4 if layer == 0 else 3)

            def feed(c, e):
                dve.wait_ge(a_ready, c * (NE * BANKS) + e * BANKS + 1)
                dve.tensor_scalar(h[:, e % 2, :], HT[:, c], lng[:, e:e + 1], lnb[:, e:e + 1],
                                  ALU.mult, ALU.add).then_inc(h_ready, 1)

            def gate_up(c, e):
                dve.wait_ge(y_ready, c * NE + e + 1)
                for f in range(FB):
                    dve.wait_ge(a_ready, c * (NE * BANKS) + e * BANKS + FB + f + 2 + BANKS)
                    dve.wait_ge(a_free, c * (NE * FB) + e * FB + FB + f + 1)
                    dve.tensor_tensor(hidden[:, e % NB, f, :], silu[:, f, :], pa[:, FB + f, :],
                                      ALU.mult).then_inc(u_free, 1)

            def add(c, e, ch):
                dve.wait_ge(y_ready, c * NE + e + 1 + NB)
                for t in range(CT):
                    g = gch[:, t * E + e:t * E + e + 1]
                    if layer == 1 and e == 0:
                        last = dve.tensor_scalar(acc[:, t, :], py[0][:, t, :], g, None, ALU.mult)
                    elif e < E:
                        last = dve.scalar_tensor_tensor(acc[:, t, :], py[e % NB][:, t, :], g, acc[:, t, :],
                                                        ALU.mult, ALU.add)
                if e == E:
                    last = dve.tensor_tensor(acc[:], acc[:], py[e % NB][:], ALU.add)
                ch.do(last)
                dve.sem_inc(y_free, 1)

            def stage_gates(c):
                dve.tensor_copy(gsc[:], gate_sum[:, c]).then_inc(g_staged, 1)
                dve.tensor_copy(gch[:, 0:CT * E].rearrange("p (t e) -> p t e", e=E),
                                gates[:, c]).then_inc(g_staged, 1)

            def chunk(c, final):
                ch = Chain(dve, chain_d, c * PER)
                dve.wait_ge(g_staged, c * 2 + 2)
                for e in range(NE):
                    if layer == 0 and e + 2 < NE:
                        feed(c, e + 2)
                    elif layer == 0 and not final:
                        feed(c + 1, e + 2 - NE)
                    if layer == 0 and e == 1:
                        dve.wait_ge(bias_ready, c + 1)
                        for t in range(CT):
                            last = dve.scalar_tensor_tensor(acc[:, t, :], X[:, c, t, :], gsc[:, t:t + 1],
                                                            pg[:, t, :], ALU.mult, ALU.add)
                        ch.do(last)
                    if layer == 1 and e:
                        gate_up(c, e)
                    if e:
                        add(c, e - 1, ch)
                if layer == 1 and not final:
                    gate_up(c + 1, 0)
                add(c, NE - 1, ch)
                if not final:
                    stage_gates(c + 1)
                ch.do(dve.tensor_tensor(y[:], acc[:], X[:, c], ALU.add))
                if layer == 0:
                    dve.wait_ge(xt_kept, c + 1)
                dve.wait_ge(x_stored, c * 16 + 16)
                normalise(dve, ch, xn, y, stats, mv, rstd, CT, stats_ready, rstd_ready, c, M["passed"]).then_inc(x_ready, 1)
                assert ch.k == PER

            if layer == 0:
                feed(0, 0)
                feed(0, 1)
            route(dve, M, R, layer)
            stage_gates(0)
            if layer == 1:
                gate_up(0, 0)
            with dve.Fori(0, CH - 1) as c:
                chunk(c, False)
            chunk(CH - 1, True)


def scan_layer(nc, M, name):
    with ExitStack() as ctx:
        sem = lambda n: new_semaphore(nc, M, f"{name}_{n}")
        sb = lambda n, shape, dt=F32: ctx.enter_context(nc.sbuf_tensor(f"{name}_{n}", shape, dt))
        pw = [ctx.enter_context(nc.psum_tensor(f"{name}_pw{i}", [P, T], F32)) for i in range(4)]
        k, beta, kv, state, o = sb("k", [P, T]), sb("beta", [P, T]), sb("kv", [P, T]), sb("state", [P, T]), sb("o", [P, T])
        xb, y, z, xn, hn = (sb(n, [P, NT, P]) for n in ("xb", "y", "z", "xn", "hn"))
        stats, mv = sb("stats", [P, NT, 6]), sb("mv", [P, NT, 2])
        ms, tmp, rstd, warm = sb("ms", [P, NT]), sb("tmp", [P, NT]), sb("rstd", [P, NT]), sb("warm", [P, 2])
        projected, evacuated, o_ready, out_ready, y_made = (sem("projected"), sem("evacuated"), sem("o_ready"),
                                                            sem("out_ready"), sem("y_made"))
        xb_ready, h_ready, h_flipped, ht_kept, x_ready = (sem("xb_ready"), sem("h_ready"), sem("h_flipped"),
                                                                    sem("ht_kept"), sem("x_ready"))
        stats_ready, rstd_ready, chain_d, chain_p = sem("stats_ready"), sem("rstd_ready"), sem("cd"), sem("cp")
        block = ctx.enter_context(nc.Block())
        pout, ph = pw[0], pw[1]
        SETS = 3

        @block.tensor
        def _(pe):
            def project(b):
                pe.wait_ge(ht_kept, b + 1)
                pe.wait_ge(o_ready, b + 1)
                for n in (1, 2, 3, 0):
                    if n == 0:
                        pe.wait_ge(y_made, b + 1)
                    for half in range(2):
                        c = slice(half * HALF, (half + 1) * HALF)
                        last = pe.matmul(pw[n][:, c], M["w1d"][:, n, :], M["XT"][:, b, c], start=True, stop=True)
                    last.then_inc(projected, 1)

            def project_out(b):
                pe.wait_ge(o_ready, b + 2)
                for t in range(NT):
                    last = pe.matmul(pout[:, t * P:(t + 1) * P], o[:, t * P:(t + 1) * P], M["w1d"][:, 4, :],
                                     start=True, stop=True)
                last.then_inc(out_ready, 1)

            def flip_h(b, keys):
                pe.wait_ge(h_ready, b + 1)
                pe.wait_ge(evacuated, keys)
                for t in range(NT):
                    last = pe.transpose(ph[:, t * P:(t + 1) * P], hn[:, t, :], M["identF"][:])
                last.then_inc(h_flipped, 1)

            project(0)
            project_out(0)
            with pe.Fori(0, B - 1) as b:
                project(b + 1)
                project_out(b + 1)
                flip_h(b, b * 2 + 3)
            flip_h(B - 1, 2 * B)

        @block.scalar
        def _(act):
            act.activation(warm[:], M["norm"][:], ACT.Sigmoid)
            act.sem_inc(ht_kept, 2)

            def keep(b):
                act.wait_ge(projected, b * 4 + 1)
                act.wait_ge(o_ready, b + 1)
                act.activation(k[:], pw[1][:], ACT.Copy).then_inc(evacuated, 1)
                act.wait_ge(projected, b * 4 + 3)
                act.activation(beta[:], pw[3][:], ACT.Sigmoid, bias=M["bbeta"][:, 0:1]).then_inc(evacuated, 1)

            def keep_h(b):
                act.wait_ge(h_flipped, b + 1)
                act.activation(M["HT"][:, b, :], ph[:], ACT.Copy, scale=M["norm"][:, 0:1]).then_inc(ht_kept, 1)

            keep(0)
            with act.Fori(0, B - 1) as b:
                keep(b + 1)
                keep_h(b)
            keep_h(B - 1)

        @block.gpsimd
        def _(pool):
            def residual(b):
                bo = M["bo"][:].unsqueeze(1).broadcast_to([P, NT, P])
                pool.wait_ge(y_made, b + 1)
                apart(pool, M["passed"])
                pool.tensor_tensor(xb[:], M["X"][:, b], bo, ALU.add).then_inc(xb_ready, 1)

            def factors(b):
                for n in range(SETS):
                    rms = n == SETS - 1
                    make_rstd(pool, chain_p, rstd[:], ms[:] if rms else mv[:, :, 1],
                              tmp[:], M["minus_half"][:, 0:NT], 1.0 / P if rms else 1.0,
                              RMS_EPS if rms else LN_EPS, NT, stats_ready, rstd_ready, b * SETS + n, M["passed"])

            residual(0)
            with pool.Fori(0, B - 1) as b:
                residual(b + 1)
                factors(b)
            factors(B - 1)

        @block.vector
        def _(dve):
            dve.sem_inc(y_made, 1)
            dve.sem_inc(o_ready, 1)
            OWN, SCAN = 11, 2

            def recurrence(b, ch):
                def inputs():
                    dve.wait_ge(evacuated, b * 2 + 1)
                    dve.wait_ge(projected, b * 4 + 2)
                    ch.do(dve.tensor_tensor(kv[:], k[:], pw[2][:], ALU.mult))

                def recur():
                    dve.wait_ge(evacuated, b * 2 + 2)
                    ch.do(dve.tensor_tensor_scan(state[:], beta[:], kv[:], 0.0, ALU.mult, ALU.add))

                def outputs():
                    dve.wait_ge(projected, b * 4 + 4)
                    dve.tensor_tensor(o[:], state[:], pw[0][:], ALU.mult).then_inc(o_ready, 1)
                return lambda: (inputs(), recur(), outputs())

            def norms(b, ch, next_recurrence):
                dve.wait_ge(out_ready, b + 1)
                dve.wait_ge(xb_ready, b + 1)
                dve.tensor_tensor(y[:], pout[:].rearrange("p (t d) -> p t d", d=P), xb[:], ALU.add).then_inc(y_made, 1)
                dve.wait_ge(y_made, b + 2)
                ch.do(normalise(dve, ch, z, y, stats, mv, rstd, NT, stats_ready, rstd_ready, b * SETS, M["passed"]))
                wide = lambda m: m[:].unsqueeze(1).broadcast_to([P, NT, P])
                ch.do(dve.tensor_tensor(z[:], z[:], wide(M["lng"]), ALU.mult))
                ch.do(dve.tensor_tensor(z[:], z[:], wide(M["lnb"]), ALU.add))
                ch.do(dve.tensor_tensor(z[:], z[:], M["X"][:, b], ALU.add))
                dve.wait_ge(ht_kept, b + 2)
                normalise(dve, ch, xn, z, stats, mv, rstd, NT, stats_ready, rstd_ready, b * SETS + 1, M["passed"],
                          next_recurrence).then_inc(x_ready, 1)
                dve.wait_ge(x_ready, b + 1)

                def keep_x():
                    ch.do(dve.tensor_copy(M["X"][:, b], xn[:]))
                rms_normalise(dve, ch, hn, xn, z[:], ms[:], rstd, NT, stats_ready, rstd_ready,
                              b * SETS + 2, keep_x).then_inc(h_ready, 1)

            ch = Chain(dve, chain_d)
            recurrence(0, ch)()
            with dve.Fori(0, B - 1) as b:
                ch = Chain(dve, chain_d, SCAN + b * (OWN + SCAN))
                norms(b, ch, recurrence(b + 1, ch))
                assert ch.k == OWN + SCAN, ch.k
            norms(B - 1, Chain(dve, chain_d, SCAN + (B - 1) * (OWN + SCAN)), None)


def build(nc, A, out):
    TT = B * NT
    with ExitStack() as ctx:
        shapes = dict(
            X=[P, B, NT, P], OT=[P, NU, T], HT=[P, B, T],
            w0a=[P, 3, P], wop0=[P, UPB, P], w1d=[P, 5, P], w1a=[P, 3, P], wop1=[P, UPB, P],
            identF=[P, P], bo=[P, P], lng=[P, P], lnb=[P, P], norm=[P, 2], bbeta=[P, 1],
            rw=[P, 2, E], rb=[P, E], before=[P, E, E], minus_half=[P, NT],
            cols=[P, 2 * E + E * BANKS], logits=[P, TT, E], gates=[P, TT, E], gate_sum=[P, TT])
        M = {k: ctx.enter_context(nc.sbuf_tensor(k, v, F32)) for k, v in shapes.items()}
        for k, n in (("identB", P), ("row0", T), ("first", 3 * P), ("band", 3 * P)):
            M[k] = ctx.enter_context(nc.sbuf_tensor(k, [P, n], BF16))
        M["XT"] = M["OT"][:, 0:B, :]
        M["v9"] = nc.dram_tensor("v9", [NU, P, NT, G, HD + 1], F32, kind="Internal").ap()
        M["parts"] = nc.dram_tensor("parts", [2, B, UPB, PARTS, 32, T], BF16, kind="Internal").ap()
        M["rsum"] = nc.dram_tensor("rsum", [NU, G, T], F32, kind="Internal").ap()
        M["passed"] = nc.alloc_semaphore("passed")
        M["semaphores"] = []
        setup(nc, A, M)
        for layer, src, w, wop, segments in ((0, "XT", "w0a", "wop0", BANDED), (1, "HT", "w1a", "wop1", FULL)):
            if layer == 1:
                scan_layer(nc, M, "scan")
            with ExitStack() as held:
                IN = AttentionInputs(nc, M, held, f"in{layer}")
                project_qkv(nc, M, f"qkv{layer}", M[src], M[w], IN)
                attend(nc, M, f"att{layer}", segments, IN)
            with ExitStack() as held:
                W = expert_weights(nc, A, M, held, layer)
                project_out(nc, M, f"out{layer}", M[wop], layer == 1, W)
                experts(nc, A, M, f"moe{layer}", layer, W, out)
            if layer == 0:
                clear_semaphores(nc, M)


_INS = ['L0_attn_x', 'L0_attn_Wq', 'L0_attn_Wk', 'L0_attn_Wv', 'L0_attn_Wo', 'L0_ffn_router_W', 'L0_ffn_router_b',
        'L0_ffn_ln_g', 'L0_ffn_ln_b', 'L0_ffn_W1', 'L0_ffn_b1', 'L0_ffn_W2', 'L0_ffn_b2', 'L1_attn_Wq',
        'L1_attn_Wk', 'L1_attn_Wv', 'L1_attn_Wbeta', 'L1_attn_b_beta', 'L1_attn_Wo', 'L1_attn_b_o',
        'L1_attn_ln_g', 'L1_attn_ln_b', 'L1_ffn_norm1_w', 'L1_ffn_norm2_w', 'L1_ffn_wq', 'L1_ffn_wk',
        'L1_ffn_wv', 'L1_ffn_wo', 'L1_ffn_router_w', 'L1_ffn_sh_gate', 'L1_ffn_sh_up', 'L1_ffn_sh_down',
        'L1_ffn_e_gate', 'L1_ffn_e_up', 'L1_ffn_e_down']


def kernel(**inputs):
    import numpy as _np
    import concourse.bacc as _bacc
    from concourse import mybir as _mybir
    from concourse.bass_utils import run_bass_kernel_spmd as _run

    nc = _bacc.Bacc("TRN2", target_bir_lowering=False, num_devices=1)
    arrays, args = {}, {}
    for name in _INS:
        a = _np.ascontiguousarray(inputs[name])
        arrays[f"in_{name}"] = a
        args[name] = nc.dram_tensor(f"in_{name}", a.shape, _mybir.dt.from_np(a.dtype), kind="ExternalInput").ap()
    out = nc.dram_tensor("out_0", (B, T, P), _mybir.dt.float32, kind="ExternalOutput").ap()
    build(nc, args, out)
    r = _run(nc, [arrays], core_ids=[0])
    return r.results[0]["out_0"]
```
